# Optimizing a Trainium2 kernel written in Bass

```python
import numpy as np
import jax
import jax.numpy as jnp

def _softmax(x, axis=-1):
    return jax.nn.softmax(x, axis=axis)

def _gelu(x):
    return jax.nn.gelu(x, approximate=True)

def _silu(x):
    return jax.nn.silu(x)

def _sigmoid(x):
    return jax.nn.sigmoid(x)

def _layernorm(x, axis=-1, eps=1e-05):
    m = jnp.mean(x, axis=axis, keepdims=True)
    v = jnp.var(x, axis=axis, keepdims=True)
    return (x - m) / jnp.sqrt(v + eps)

def _scatter_add(tgt, idx, src, axis=0):
    return tgt.at[idx].add(src)

def _segment_sum(src, seg, n):
    return jax.ops.segment_sum(src, seg, n)
kernel_name = 'mk_xattn_ffn_d4_seqx_r4_597673'

def setup_inputs(seed: int=0):
    np.random.seed(seed)
    _w = jnp.asarray

    def _rec_inputs():
        import jax
        import jax.numpy as jnp
        _rk = jax.random.key(seed)
        x = 7.22e-05 + 1 * jax.random.normal(jax.random.fold_in(_rk, 1), (2, 1024, 256), jnp.float32)
        _lenS = 1024 - jax.random.randint(jax.random.fold_in(_rk, 7), (2,), 0, max(1, 1024 // 4) + 1, jnp.int32)
        _lenS2 = 77 - jax.random.randint(jax.random.fold_in(_rk, 8), (2,), 0, max(1, 77 // 4) + 1, jnp.int32)
        _ctx_1024P = jax.random.normal(jax.random.fold_in(_rk, 11), (2, 16, 256), jnp.float32)
        _ctx_1024c = jax.random.dirichlet(jax.random.fold_in(_rk, 511), 0.3 * jnp.ones((16,), jnp.float32), (2, 77))
        _ctx_1024t = jnp.einsum('bsk,bkd->bsd', _ctx_1024c, _ctx_1024P)
        _ctx_1024t = _ctx_1024t * jax.lax.rsqrt(jnp.mean(jnp.square(_ctx_1024t)) + 1e-12) * 0.953939
        ctx_1024 = 4.13588e-05 + 0.999923 * (_ctx_1024t + 0.3 * jax.random.normal(jax.random.fold_in(_rk, 611), (2, 77, 256), jnp.float32))
        _validS = jnp.arange(1024)[None, :] < _lenS[:, None]
        _validS2 = jnp.arange(77)[None, :] < _lenS2[:, None]
        _causal = jnp.tril(jnp.ones((1024, 1024), dtype=bool))
        mask_Bx1xSxS2_bk1 = jnp.broadcast_to(_validS2[:, None, None, :], (2, 1, 1024, 77))
        mask_Bx1xSxS2_ik1 = jnp.where(jnp.broadcast_to(_validS2[:, None, None, :], (2, 1, 1024, 77)), 1, 0).astype(jnp.int32)
        mask_BxSxS2_ik1 = jnp.where(jnp.broadcast_to(_validS2[:, None, :], (2, 1024, 77)), 1, 0).astype(jnp.int32)
        mask_BxS2_bf1 = jnp.ones((2, 77), dtype=bool)
        return (x, ctx_1024, mask_Bx1xSxS2_bk1, mask_Bx1xSxS2_ik1, mask_BxSxS2_ik1, mask_BxS2_bf1)
    x, ctx_1024, mask_Bx1xSxS2_bk1, mask_Bx1xSxS2_ik1, mask_BxSxS2_ik1, mask_BxS2_bf1 = _rec_inputs()

    def _L0_xattn_setup():
        import jax, jax.numpy as jnp
        import numpy as np
        B, S, D, H = (4, 512, 256, 16)
        HD = D // H
        key = jax.random.key(seed)
        ks = jax.random.split(key, 12)
        scale = 1.0 / np.sqrt(D)
        inp = {'queries': jax.random.normal(ks[0], (B, S, D), jnp.float32), 'keys': jax.random.normal(ks[1], (B, S, D), jnp.float32), 'values': jax.random.normal(ks[2], (B, S, D), jnp.float32), 'mask': jax.random.randint(ks[3], (B, 1, S, S), 0, 2).astype(bool), 'Wq': jax.random.normal(ks[4], (D, D), jnp.float32) * scale, 'bq': jnp.zeros((D,), jnp.float32), 'Wk': jax.random.normal(ks[5], (D, D), jnp.float32) * scale, 'bk': jnp.zeros((D,), jnp.float32), 'Wv': jax.random.normal(ks[6], (D, D), jnp.float32) * scale, 'bv': jnp.zeros((D,), jnp.float32), 'Wo': jax.random.normal(ks[7], (D, D), jnp.float32) * scale, 'bo': jnp.zeros((D,), jnp.float32)}
        return inp
    _L0_xattn_all = _L0_xattn_setup()
    _L0_xattn_in = {k: v for k, v in _L0_xattn_all.items() if k in ('Wq', 'bq', 'Wk', 'bk', 'Wv', 'bv', 'Wo', 'bo')}
    del _L0_xattn_all

    def _L0_ffn_setup():
        import jax, jax.numpy as jnp
        import numpy as np
        B, S, D, O, E, K = (4, 512, 256, 256, 8, 2)
        key = jax.random.key(seed)
        ks = jax.random.split(key, 5)
        scale_in = 1.0 / np.sqrt(D)
        x = jax.random.normal(ks[0], (B, S, D), dtype=jnp.float32)
        gate_w = jax.random.uniform(ks[1], (E, D), jnp.float32, -scale_in, scale_in)
        gate_b = jax.random.uniform(ks[2], (E,), jnp.float32, -scale_in, scale_in)
        expert_w = jax.random.uniform(ks[3], (E, D, O), jnp.float32, -scale_in, scale_in)
        expert_b = jax.random.uniform(ks[4], (E, O), jnp.float32, -scale_in, scale_in)
        return {'x': x, 'gate_w': gate_w, 'gate_b': gate_b, 'expert_w': expert_w, 'expert_b': expert_b}
    _L0_ffn_all = _L0_ffn_setup()
    _L0_ffn_in = {k: v for k, v in _L0_ffn_all.items() if k in ('gate_w', 'gate_b', 'expert_w', 'expert_b')}
    del _L0_ffn_all

    def _L1_xattn_setup():
        import jax, jax.numpy as jnp
        import numpy as np
        import math
        HEAD = 16
        D_MODEL = 256
        HEAD_DIM = D_MODEL // HEAD
        B, S = (2, 512)
        key = jax.random.key(seed)
        ks = jax.random.split(key, 9)
        sc = 1.0 / math.sqrt(D_MODEL)
        return {'q': jax.random.normal(ks[0], (B, S, D_MODEL), dtype=jnp.float32), 'k': jax.random.normal(ks[1], (B, S, D_MODEL), dtype=jnp.float32), 'v': jax.random.normal(ks[2], (B, S, D_MODEL), dtype=jnp.float32), 'mask': jax.random.randint(ks[3], (B, 1, S, S), 0, 2, dtype=jnp.int32), 'wq': jax.random.normal(ks[4], (D_MODEL, D_MODEL), dtype=jnp.float32) * sc, 'wk': jax.random.normal(ks[5], (D_MODEL, D_MODEL), dtype=jnp.float32) * sc, 'wv': jax.random.normal(ks[6], (D_MODEL, D_MODEL), dtype=jnp.float32) * sc, 'wo': jax.random.normal(ks[7], (D_MODEL, D_MODEL), dtype=jnp.float32) * sc, 'bo': jax.random.normal(ks[8], (D_MODEL,), dtype=jnp.float32) * 0.01}
    _L1_xattn_all = _L1_xattn_setup()
    _L1_xattn_in = {k: v for k, v in _L1_xattn_all.items() if k in ('wq', 'wk', 'wv', 'wo', 'bo')}
    del _L1_xattn_all

    def _L1_ffn_setup():
        import jax, jax.numpy as jnp
        import numpy as np
        INT8_MAX = 127.0

        def _absmax_scale(x, axes):
            amax = jnp.max(jnp.abs(x), axis=axes, keepdims=True)
            return jnp.maximum(amax, 1e-12) / INT8_MAX
        key = jax.random.key(seed)
        k1, k2 = jax.random.split(key)
        lhs = jax.random.normal(k1, (4, 2048, 256), dtype=jnp.float32)
        rhs = jax.random.normal(k2, (256, 256), dtype=jnp.float32)
        return {'lhs': lhs, 'rhs': rhs}
    _L1_ffn_all = _L1_ffn_setup()
    _L1_ffn_in = {k: v for k, v in _L1_ffn_all.items() if k in ('rhs',)}
    del _L1_ffn_all

    def _L2_xattn_setup():
        import jax, jax.numpy as jnp
        import numpy as np
        NEG = -9000000000000000.0
        EPS = 1e-05
        key = jax.random.key(seed)
        k1, k2, k3, k4 = jax.random.split(key, 4)
        B, S, D = (4, 512, 256)
        q = jax.random.normal(k1, (B, S, D), dtype=jnp.float32)
        k = jax.random.normal(k2, (B, S, D), dtype=jnp.float32)
        v = jax.random.normal(k3, (B, S, D), dtype=jnp.float32)
        mask = jax.random.randint(k4, (B, S, S), 0, 2, dtype=jnp.int32)
        gamma = jnp.ones((D,), dtype=jnp.float32)
        beta = jnp.zeros((D,), dtype=jnp.float32)
        return {'q': q, 'k': k, 'v': v, 'mask': mask, 'gamma': gamma, 'beta': beta}
    _L2_xattn_all = _L2_xattn_setup()
    _L2_xattn_in = {k: v for k, v in _L2_xattn_all.items() if k in ('gamma', 'beta')}
    del _L2_xattn_all

    def _L2_ffn_setup():
        import jax, jax.numpy as jnp
        import numpy as np
        H = 256
        I = 128
        E = 8
        TOPK = 2
        NGROUP = 4
        TOPKG = 2
        SCALE = 1.0
        B, S = (4, 256)

        def _gate(xf, gate_weight, bias):
            T = xf.shape[0]
            logits = xf @ gate_weight.T
            scores = jax.nn.sigmoid(logits)
            scores_for_choice = scores + bias[None, :]
            gsz = E // NGROUP
            grp = scores_for_choice.reshape(T, NGROUP, gsz)
            group_scores = jax.lax.top_k(grp, 2)[0].sum(-1)
            _, group_idx = jax.lax.top_k(group_scores, TOPKG)
            rows = jnp.arange(T)[:, None]
            group_mask = jnp.zeros((T, NGROUP), xf.dtype).at[rows, group_idx].set(1.0)
            score_mask = jnp.broadcast_to(group_mask[:, :, None], (T, NGROUP, gsz)).reshape(T, E)
            tmp_scores = jnp.where(score_mask > 0, scores_for_choice, 0.0)
            _, topk_idx = jax.lax.top_k(tmp_scores, TOPK)
            topk_weight = jnp.take_along_axis(scores, topk_idx, axis=1)
            if TOPK > 1:
                topk_weight = topk_weight / (topk_weight.sum(-1, keepdims=True) + 1e-20)
            topk_weight = topk_weight * SCALE
            return (topk_idx, topk_weight)
        key = jax.random.key(seed)
        k0, k1, k2, k3, k4 = jax.random.split(key, 5)
        return {'hidden_states': jax.random.normal(k0, (B, S, H), jnp.float32), 'gate_weight': jax.random.normal(k1, (E, H), jnp.float32) * (1.0 / np.sqrt(H)), 'e_score_correction_bias': jnp.zeros((E,), jnp.float32), 'gate_proj': jax.random.normal(k2, (E, I, H), jnp.float32) * 0.02, 'up_proj': jax.random.normal(k3, (E, I, H), jnp.float32) * 0.02, 'down_proj': jax.random.normal(k4, (E, H, I), jnp.float32) * 0.02}
    _L2_ffn_all = _L2_ffn_setup()
    _L2_ffn_in = {k: v for k, v in _L2_ffn_all.items() if k in ('gate_weight', 'e_score_correction_bias', 'gate_proj', 'up_proj', 'down_proj')}
    del _L2_ffn_all

    def _L3_xattn_setup():
        import jax, jax.numpy as jnp
        import numpy as np
        B, M, N = (2, 256, 512)
        D_MODEL = 256
        H, HKV, D = (16, 4, 64)
        GROUPS = H // HKV
        THETA = 10000.0
        MAX_REL = M + N

        def _freqs_cis(dim, seq_len, theta):
            inv = 1.0 / theta ** (jnp.arange(0, dim, 2, dtype=jnp.float32) / dim)
            f = jnp.outer(jnp.arange(seq_len, dtype=jnp.float32), inv)
            f = jnp.repeat(f, 2, axis=-1)
            return (jnp.cos(f), jnp.sin(f))

        def _apply_rope(x, cos, sin):
            cos = cos[None, None]
            sin = sin[None, None]
            d = x.shape[-1]
            x1, x2 = (x[..., :d // 2], x[..., d // 2:])
            c1, c2 = (cos[..., :d // 2], cos[..., d // 2:])
            s1, s2 = (sin[..., :d // 2], sin[..., d // 2:])
            return jnp.concatenate([x1 * c1 - x2 * s1, x1 * s2 + x2 * c2], axis=-1)
        key = jax.random.key(seed)
        ks = jax.random.split(key, 8)
        sc = lambda fan_in: 1.0 / np.sqrt(fan_in)
        return {'q': jax.random.normal(ks[0], (B, M, D_MODEL), jnp.float32), 'kv': jax.random.normal(ks[1], (B, N, D_MODEL), jnp.float32), 'Wq': jax.random.normal(ks[2], (D_MODEL, H * D), jnp.float32) * sc(D_MODEL), 'Wk': jax.random.normal(ks[3], (D_MODEL, HKV * D), jnp.float32) * sc(D_MODEL), 'Wv': jax.random.normal(ks[4], (D_MODEL, HKV * D), jnp.float32) * sc(D_MODEL), 'Wo': jax.random.normal(ks[5], (H * D, D_MODEL), jnp.float32) * sc(H * D), 'rel_pos_bias': jnp.zeros((H, MAX_REL), jnp.float32), 'mask': jnp.ones((B, N), dtype=bool)}
    _L3_xattn_all = _L3_xattn_setup()
    _L3_xattn_in = {k: v for k, v in _L3_xattn_all.items() if k in ('Wq', 'Wk', 'Wv', 'Wo', 'rel_pos_bias')}
    del _L3_xattn_all

    def _L3_ffn_setup():
        import jax, jax.numpy as jnp
        import numpy as np
        E = 8
        C = 320
        D = 256
        H = 1024
        B, S = (4, 512)
        key = jax.random.key(seed)
        ks = jax.random.split(key, 12)
        sc = 0.02
        return {'input': jax.random.normal(ks[0], (B, S, D), jnp.float32), 'router_w': jax.random.normal(ks[1], (D, E), jnp.float32) * sc, 'router_b': jnp.zeros((E,), jnp.float32), 'w1': jax.random.normal(ks[2], (E, D, H), jnp.float32) * sc, 'b1': jnp.zeros((E, H), jnp.float32), 'w2': jax.random.normal(ks[3], (E, H, D), jnp.float32) * sc, 'b2': jnp.zeros((E, D), jnp.float32), 'ow1': jax.random.normal(ks[4], (D, H), jnp.float32) * sc, 'ob1': jnp.zeros((H,), jnp.float32), 'ow2': jax.random.normal(ks[5], (H, D), jnp.float32) * sc, 'ob2': jnp.zeros((D,), jnp.float32)}
    _L3_ffn_all = _L3_ffn_setup()
    _L3_ffn_in = {k: v for k, v in _L3_ffn_all.items() if k in ('router_w', 'router_b', 'w1', 'b1', 'w2', 'b2', 'ow1', 'ob1', 'ow2', 'ob2')}
    del _L3_ffn_all
    return {'x': x, 'ctx_1024': ctx_1024, 'mask_Bx1xSxS2_bk1': mask_Bx1xSxS2_bk1, 'mask_Bx1xSxS2_ik1': mask_Bx1xSxS2_ik1, 'mask_BxSxS2_ik1': mask_BxSxS2_ik1, 'mask_BxS2_bf1': mask_BxS2_bf1, 'L0_xattn_Wq': _L0_xattn_in['Wq'], 'L0_xattn_bq': _L0_xattn_in['bq'], 'L0_xattn_Wk': _L0_xattn_in['Wk'], 'L0_xattn_bk': _L0_xattn_in['bk'], 'L0_xattn_Wv': _L0_xattn_in['Wv'], 'L0_xattn_bv': _L0_xattn_in['bv'], 'L0_xattn_Wo': _L0_xattn_in['Wo'], 'L0_xattn_bo': _L0_xattn_in['bo'], 'L0_ffn_gate_w': _L0_ffn_in['gate_w'], 'L0_ffn_gate_b': _L0_ffn_in['gate_b'], 'L0_ffn_expert_w': _L0_ffn_in['expert_w'], 'L0_ffn_expert_b': _L0_ffn_in['expert_b'], 'L1_xattn_wq': _L1_xattn_in['wq'], 'L1_xattn_wk': _L1_xattn_in['wk'], 'L1_xattn_wv': _L1_xattn_in['wv'], 'L1_xattn_wo': _L1_xattn_in['wo'], 'L1_xattn_bo': _L1_xattn_in['bo'], 'L1_ffn_rhs': _L1_ffn_in['rhs'], 'L2_xattn_gamma': _L2_xattn_in['gamma'], 'L2_xattn_beta': _L2_xattn_in['beta'], 'L2_ffn_gate_weight': _L2_ffn_in['gate_weight'], 'L2_ffn_e_score_correction_bias': _L2_ffn_in['e_score_correction_bias'], 'L2_ffn_gate_proj': _L2_ffn_in['gate_proj'], 'L2_ffn_up_proj': _L2_ffn_in['up_proj'], 'L2_ffn_down_proj': _L2_ffn_in['down_proj'], 'L3_xattn_Wq': _L3_xattn_in['Wq'], 'L3_xattn_Wk': _L3_xattn_in['Wk'], 'L3_xattn_Wv': _L3_xattn_in['Wv'], 'L3_xattn_Wo': _L3_xattn_in['Wo'], 'L3_xattn_rel_pos_bias': _L3_xattn_in['rel_pos_bias'], 'L3_ffn_router_w': _L3_ffn_in['router_w'], 'L3_ffn_router_b': _L3_ffn_in['router_b'], 'L3_ffn_w1': _L3_ffn_in['w1'], 'L3_ffn_b1': _L3_ffn_in['b1'], 'L3_ffn_w2': _L3_ffn_in['w2'], 'L3_ffn_b2': _L3_ffn_in['b2'], 'L3_ffn_ow1': _L3_ffn_in['ow1'], 'L3_ffn_ob1': _L3_ffn_in['ob1'], 'L3_ffn_ow2': _L3_ffn_in['ow2'], 'L3_ffn_ob2': _L3_ffn_in['ob2']}

def reference(x, ctx_1024, mask_Bx1xSxS2_bk1, mask_Bx1xSxS2_ik1, mask_BxSxS2_ik1, mask_BxS2_bf1, L0_xattn_Wq, L0_xattn_bq, L0_xattn_Wk, L0_xattn_bk, L0_xattn_Wv, L0_xattn_bv, L0_xattn_Wo, L0_xattn_bo, L0_ffn_gate_w, L0_ffn_gate_b, L0_ffn_expert_w, L0_ffn_expert_b, L1_xattn_wq, L1_xattn_wk, L1_xattn_wv, L1_xattn_wo, L1_xattn_bo, L1_ffn_rhs, L2_xattn_gamma, L2_xattn_beta, L2_ffn_gate_weight, L2_ffn_e_score_correction_bias, L2_ffn_gate_proj, L2_ffn_up_proj, L2_ffn_down_proj, L3_xattn_Wq, L3_xattn_Wk, L3_xattn_Wv, L3_xattn_Wo, L3_xattn_rel_pos_bias, L3_ffn_router_w, L3_ffn_router_b, L3_ffn_w1, L3_ffn_b1, L3_ffn_w2, L3_ffn_b2, L3_ffn_ow1, L3_ffn_ob1, L3_ffn_ow2, L3_ffn_ob2):
    import jax
    import jax.numpy as jnp

    def _L0_xattn_ref(queries, keys, values, mask, Wq, bq, Wk, bk, Wv, bv, Wo, bo):
        import jax, jax.numpy as jnp
        import numpy as np
        B, S, D, H = (4, 512, 256, 16)
        HD = D // H
        b, sq, d = queries.shape

        def split_heads(x):
            return x.reshape(b, x.shape[1], H, HD).transpose(0, 2, 1, 3)
        q = split_heads(queries @ Wq + bq)
        k = split_heads(keys @ Wk + bk)
        v = split_heads(values @ Wv + bv)
        scores = jnp.einsum('bhqd,bhkd->bhqk', q, k) / jnp.sqrt(jnp.float32(HD))
        scores = jnp.where(mask, jnp.float32(-1000000000000000.0), scores)
        attn = jax.nn.softmax(scores, axis=-1)
        ctx = jnp.einsum('bhqk,bhkd->bhqd', attn, v)
        ctx = ctx.transpose(0, 2, 1, 3).reshape(b, sq, d)
        return ctx @ Wo + bo

    def _L0_ffn_ref(x, gate_w, gate_b, expert_w, expert_b):
        import jax, jax.numpy as jnp
        import numpy as np
        B, S, D, O, E, K = (4, 512, 256, 256, 8, 2)
        logits = jnp.einsum('bsd,ed->bse', x, gate_w) + gate_b
        if K < E:
            topv, topi = jax.lax.top_k(logits, K)
            keep = jax.nn.one_hot(topi, E, dtype=jnp.float32).sum(axis=-2)
            logits = jnp.where(keep > 0, logits, -jnp.inf)
        gate_score = jax.nn.softmax(logits, axis=-1)
        expert_out = jnp.einsum('bsd,edo->bseo', x, expert_w) + expert_b
        out = jnp.einsum('bseo,bse->bso', expert_out, gate_score)
        return out

    def _L1_xattn_ref(q, k, v, mask, wq, wk, wv, wo, bo):
        import jax, jax.numpy as jnp
        import numpy as np
        import math
        HEAD = 16
        D_MODEL = 256
        HEAD_DIM = D_MODEL // HEAD
        B, S = (2, 512)
        N, Lq, _ = q.shape
        Lk = k.shape[1]
        qh = (q @ wq).reshape(N, Lq, HEAD, HEAD_DIM)
        kh = (k @ wk).reshape(N, Lk, HEAD, HEAD_DIM)
        vh = (v @ wv).reshape(N, Lk, HEAD, HEAD_DIM)
        scores = jnp.einsum('nqha,nkha->nhqk', qh, kh)
        scores = jnp.where(mask == 0, jnp.float32(-10000000000.0), scores)
        attn = jax.nn.softmax(scores / math.sqrt(HEAD_DIM), axis=-1)
        out = jnp.einsum('nhqk,nkha->nqha', attn, vh).reshape(N, Lq, D_MODEL)
        return out @ wo + bo

    def _L1_ffn_ref(lhs, rhs):
        import jax, jax.numpy as jnp
        import numpy as np
        INT8_MAX = 127.0

        def _absmax_scale(x, axes):
            amax = jnp.max(jnp.abs(x), axis=axes, keepdims=True)
            return jnp.maximum(amax, 1e-12) / INT8_MAX
        lhs_scale = _absmax_scale(lhs, (2,))
        rhs_scale = _absmax_scale(rhs, (0,))
        q_lhs = jnp.clip(jnp.round(lhs / lhs_scale), -INT8_MAX, INT8_MAX).astype(jnp.int8)
        q_rhs = jnp.clip(jnp.round(rhs / rhs_scale), -INT8_MAX, INT8_MAX).astype(jnp.int8)
        acc = jax.lax.dot_general(q_lhs, q_rhs, (((2,), (0,)), ((), ())), preferred_element_type=jnp.int32)
        return acc.astype(jnp.float32) * lhs_scale * rhs_scale

    def _L2_xattn_ref(q, k, v, mask, gamma, beta):
        import jax, jax.numpy as jnp
        import numpy as np
        NEG = -9000000000000000.0
        EPS = 1e-05
        d_k = q.shape[-1]
        logits = jnp.einsum('bsd,btd->bst', q, k) / jnp.sqrt(jnp.asarray(d_k, q.dtype))
        logits = jnp.where(mask == 0, jnp.asarray(NEG, logits.dtype), logits)
        attn = jax.nn.softmax(logits, axis=-1)
        x = jnp.einsum('bst,btd->bsd', attn, v)
        mu = jnp.mean(x, axis=-1, keepdims=True)
        var = jnp.mean(jnp.square(x - mu), axis=-1, keepdims=True)
        xhat = (x - mu) * jax.lax.rsqrt(var + EPS)
        return xhat * gamma + beta

    def _L2_ffn_ref(hidden_states, gate_weight, e_score_correction_bias, gate_proj, up_proj, down_proj):
        import jax, jax.numpy as jnp
        import numpy as np
        H = 256
        I = 128
        E = 8
        TOPK = 2
        NGROUP = 4
        TOPKG = 2
        SCALE = 1.0
        B, S = (4, 256)

        def _gate(xf, gate_weight, bias):
            T = xf.shape[0]
            logits = xf @ gate_weight.T
            scores = jax.nn.sigmoid(logits)
            scores_for_choice = scores + bias[None, :]
            gsz = E // NGROUP
            grp = scores_for_choice.reshape(T, NGROUP, gsz)
            group_scores = jax.lax.top_k(grp, 2)[0].sum(-1)
            _, group_idx = jax.lax.top_k(group_scores, TOPKG)
            rows = jnp.arange(T)[:, None]
            group_mask = jnp.zeros((T, NGROUP), xf.dtype).at[rows, group_idx].set(1.0)
            score_mask = jnp.broadcast_to(group_mask[:, :, None], (T, NGROUP, gsz)).reshape(T, E)
            tmp_scores = jnp.where(score_mask > 0, scores_for_choice, 0.0)
            _, topk_idx = jax.lax.top_k(tmp_scores, TOPK)
            topk_weight = jnp.take_along_axis(scores, topk_idx, axis=1)
            if TOPK > 1:
                topk_weight = topk_weight / (topk_weight.sum(-1, keepdims=True) + 1e-20)
            topk_weight = topk_weight * SCALE
            return (topk_idx, topk_weight)
        Bv, Sv, Hv = hidden_states.shape
        xf = hidden_states.reshape(-1, Hv).astype(jnp.float32)
        topk_idx, topk_weight = _gate(xf, gate_weight.astype(jnp.float32), e_score_correction_bias.astype(jnp.float32))
        y = jnp.zeros_like(xf)
        for e in range(E):
            combine_w = jnp.where(topk_idx == e, topk_weight, 0.0).sum(-1)
            g = xf @ gate_proj[e].T
            u = xf @ up_proj[e].T
            o = jax.nn.silu(g) * u @ down_proj[e].T
            y = y + combine_w[:, None] * o
        return y.reshape(Bv, Sv, Hv)

    def _L3_xattn_ref(q, kv, Wq, Wk, Wv, Wo, rel_pos_bias, mask):
        import jax, jax.numpy as jnp
        import numpy as np
        B, M, N = (2, 256, 512)
        D_MODEL = 256
        H, HKV, D = (16, 4, 64)
        GROUPS = H // HKV
        THETA = 10000.0
        MAX_REL = M + N

        def _freqs_cis(dim, seq_len, theta):
            inv = 1.0 / theta ** (jnp.arange(0, dim, 2, dtype=jnp.float32) / dim)
            f = jnp.outer(jnp.arange(seq_len, dtype=jnp.float32), inv)
            f = jnp.repeat(f, 2, axis=-1)
            return (jnp.cos(f), jnp.sin(f))

        def _apply_rope(x, cos, sin):
            cos = cos[None, None]
            sin = sin[None, None]
            d = x.shape[-1]
            x1, x2 = (x[..., :d // 2], x[..., d // 2:])
            c1, c2 = (cos[..., :d // 2], cos[..., d // 2:])
            s1, s2 = (sin[..., :d // 2], sin[..., d // 2:])
            return jnp.concatenate([x1 * c1 - x2 * s1, x1 * s2 + x2 * c2], axis=-1)
        Bq, Mq, _ = q.shape
        Nk = kv.shape[1]
        Q = (q @ Wq).reshape(Bq, Mq, H, D).transpose(0, 2, 1, 3)
        K = (kv @ Wk).reshape(Bq, Nk, HKV, D).transpose(0, 2, 1, 3)
        V = (kv @ Wv).reshape(Bq, Nk, HKV, D).transpose(0, 2, 1, 3)
        cos_q, sin_q = _freqs_cis(D, Mq, THETA)
        cos_k, sin_k = _freqs_cis(D, Nk, THETA)
        Q = _apply_rope(Q, cos_q, sin_q)
        K = _apply_rope(K, cos_k, sin_k)
        K = jnp.repeat(K, GROUPS, axis=1)
        V = jnp.repeat(V, GROUPS, axis=1)
        scale = D ** (-0.5)
        scores = jnp.einsum('bhqd,bhkd->bhqk', Q, K) * scale
        rel = jnp.abs(jnp.arange(Mq)[:, None] - jnp.arange(Nk)[None, :])
        rel = jnp.clip(rel, 0, MAX_REL - 1)
        scores = scores + rel_pos_bias[:, rel][None]
        m = mask[:, None, None, :]
        scores = jnp.where(m, scores, -1000000000.0)
        attn = jax.nn.softmax(scores, axis=-1)
        out = jnp.einsum('bhqk,bhkd->bhqd', attn, V)
        out = out.transpose(0, 2, 1, 3).reshape(Bq, Mq, H * D)
        return out @ Wo

    def _L3_ffn_ref(input, router_w, router_b, w1, b1, w2, b2, ow1, ob1, ow2, ob2):
        import jax, jax.numpy as jnp
        import numpy as np
        E = 8
        C = 320
        D = 256
        H = 1024
        B, S = (4, 512)
        Bq, Sq, Dq = input.shape
        N = Bq * Sq
        xf = input.reshape(N, Dq)
        probs = jax.nn.softmax(xf @ router_w + router_b, axis=-1)
        eid = jnp.argmax(probs, axis=-1)
        onehot = jax.nn.one_hot(eid, E, dtype=xf.dtype)
        rank = (jnp.cumsum(onehot, axis=0)[jnp.arange(N), eid] - 1.0).astype(jnp.int32)
        valid = rank < C
        pos = jnp.where(valid, rank, 0)
        vmask = valid.astype(xf.dtype)[:, None]
        buf = jnp.zeros((E, C, Dq), xf.dtype).at[eid, pos].add(xf * vmask)
        h = jax.nn.relu(jnp.einsum('ecd,edh->ech', buf, w1) + b1[:, None, :])
        y = jnp.einsum('ech,ehd->ecd', h, w2) + b2[:, None, :]
        y_tok = y[eid, pos] * vmask
        yov = jax.nn.relu(xf @ ow1 + ob1) @ ow2 + ob2
        out = y_tok + yov * (1.0 - vmask)
        return out.reshape(Bq, Sq, Dq)
    x = x + _L0_xattn_ref(_layernorm(x, axis=-1), ctx_1024, ctx_1024, mask_Bx1xSxS2_bk1, L0_xattn_Wq, L0_xattn_bq, L0_xattn_Wk, L0_xattn_bk, L0_xattn_Wv, L0_xattn_bv, L0_xattn_Wo, L0_xattn_bo)
    x = x + _L0_ffn_ref(_layernorm(x, axis=-1), L0_ffn_gate_w, L0_ffn_gate_b, L0_ffn_expert_w, L0_ffn_expert_b)
    x = x + _L1_xattn_ref(_layernorm(x, axis=-1), ctx_1024, ctx_1024, mask_Bx1xSxS2_ik1, L1_xattn_wq, L1_xattn_wk, L1_xattn_wv, L1_xattn_wo, L1_xattn_bo)
    x = x + _L1_ffn_ref(_layernorm(x, axis=-1), L1_ffn_rhs)
    x = x + _L2_xattn_ref(_layernorm(x, axis=-1), ctx_1024, ctx_1024, mask_BxSxS2_ik1, L2_xattn_gamma, L2_xattn_beta)
    x = x + _L2_ffn_ref(_layernorm(x, axis=-1), L2_ffn_gate_weight, L2_ffn_e_score_correction_bias, L2_ffn_gate_proj, L2_ffn_up_proj, L2_ffn_down_proj)
    x = x + _L3_xattn_ref(_layernorm(x, axis=-1), ctx_1024, L3_xattn_Wq, L3_xattn_Wk, L3_xattn_Wv, L3_xattn_Wo, L3_xattn_rel_pos_bias, mask_BxS2_bf1)
    x = x + _L3_ffn_ref(_layernorm(x, axis=-1), L3_ffn_router_w, L3_ffn_router_b, L3_ffn_w1, L3_ffn_b1, L3_ffn_w2, L3_ffn_b2, L3_ffn_ow1, L3_ffn_ob1, L3_ffn_ow2, L3_ffn_ob2)
    return x

_drawn_inputs = setup_inputs


def setup_inputs(seed=0):
    import zlib

    import numpy as np

    out = dict(_drawn_inputs(seed))
    spreads = {'L0_xattn_bq': (0.0, 0.1),
     'L0_xattn_bk': (0.0, 2.0),
     'L0_xattn_bv': (0.0, 0.1),
     'L0_xattn_bo': (0.0, 0.1),
     'L2_xattn_gamma': (1.0, 0.6),
     'L2_xattn_beta': (0.0, 0.8),
     'L2_ffn_e_score_correction_bias': (0.0, 0.8),
     'L3_xattn_rel_pos_bias': (0.0, 0.8),
     'L3_ffn_router_b': (0.0, 0.8),
     'L3_ffn_b1': (0.0, 0.8),
     'L3_ffn_b2': (0.0, 0.8),
     'L3_ffn_ob1': (0.0, 0.8),
     'L3_ffn_ob2': (0.0, 2.0)}
    factors = {'L0_ffn_expert_b': 3.03,
     'L1_xattn_bo': 6.049,
     'L2_ffn_gate_weight': 8.0,
     'L2_ffn_gate_proj': 8.0,
     'L2_ffn_up_proj': 8.0,
     'L2_ffn_down_proj': 8.0,
     'L3_xattn_Wq': 4.27,
     'L3_xattn_Wk': 4.233,
     'L3_ffn_router_w': 5.532,
     'L3_ffn_w1': 8.0,
     'L3_ffn_w2': 6.857,
     'L3_ffn_ow1': 8.0,
     'L3_ffn_ow2': 8.0}
    for name, (base, spread) in spreads.items():
        noise = np.random.default_rng([zlib.crc32(name.encode()), seed]).standard_normal(out[name].shape)
        drawn = base * np.exp(spread * noise) if base else spread * noise
        out[name] = jnp.asarray(drawn.astype(out[name].dtype))
    for name, factor in factors.items():
        out[name] = (out[name] * factor).astype(out[name].dtype)
    return out
```

```python
from contextlib import ExitStack

import numpy as np
import concourse.bass as bass
from concourse import mybir

P = 128
ALU = mybir.AluOpType
ACT = mybir.ActivationFunctionType
F32 = mybir.dt.float32
BF16 = mybir.dt.bfloat16
I32 = mybir.dt.int32
U32 = mybir.dt.uint32
STAGES = 8
U8 = mybir.dt.uint8
AX = mybir.AxisListType.X
ds = bass.ds

B, S, D = 2, 1024, 256
T = B * S
NT = T // P
KC = D // P
SK = 77
H = 16
HD = D // H
HPB = 6
HEAD_RUNS = [(0, 0, 6), (0, 6, 8), (1, 8, 12), (1, 12, 16)]
NEG = -float(2 ** 100)
EPS = 1e-5
NBLK = -(-H * SK // P)
VHEADS = 3
VHEAD0 = [min(j * P // SK, H - VHEADS) for j in range(NBLK)]
PERIODS = 3
PGROUPS = [(0, 4), (4, 8), (8, NBLK)]
PG = len(PGROUPS)
CH0 = 6
VC = HD + 1


def is_static(i):
    return isinstance(i, int)


def inside(i):
    return not is_static(i) or 0 <= i < NT


def wait(eng, sem, value):
    if not is_static(value) or value > 0:
        eng.wait_ge(sem, value)


def pipeline(eng, step, first, lo, hi, last):
    for t in range(first, lo):
        step(t, t % 2)
    with eng.Fori(0, (hi - lo) // 2) as j:
        step(j * 2 + lo, lo % 2)
        step(j * 2 + (lo + 1), (lo + 1) % 2)
    for t in range(hi, last):
        step(t, t % 2)


class Chain:

    def __init__(self, eng, sem, per_turn=0):
        self.eng, self.sem, self.base, self.n = eng, sem, 0, 0

    def at(self, base):
        self.base, self.n = base, 0

    def __call__(self, ins):
        self.n += 1
        ins.then_inc(self.sem, 1)
        self.eng.wait_ge(self.sem, self.base + self.n)


class Core:
    pass


def sb(c, name, shape, dt=F32):
    return c.stage_ctx.enter_context(c.nc.sbuf_tensor(name, shape, dt))


def sem(c, name):
    c.stage_sems.append(c.nc.alloc_semaphore(name=name))
    return c.stage_sems[-1]


def run_stage(c, stage, last=False):
    with ExitStack() as c.stage_ctx:
        c.stage_sems = []
        stage()
    if not last:
        c.nc.clear_and_free_semaphores(c.stage_sems)
        c.nc.all_engine_barrier()


def xt(c, i):
    return c.x[:, ds(i * D, D)]


def mean_of(c, i):
    return c.mean[:, ds(i, 1)]


def rstd_of(c, i):
    return c.rstd[:, ds(i, 1)]


def bst_of(c, i):
    return c.bst[:, ds(i * 6, 6)]


def dve_rstd(c, dve, chain, ve_ready, std_ready, bst=None):
    nv = c.nc.vector
    st = (c.bst if bst is None else bst)[:, :].rearrange("p (i s) -> p i s", s=6)
    chain(nv.tensor_tensor(c.mean[:, :], st[:, :, 1], st[:, :, 4], ALU.add))
    chain(nv.tensor_tensor(c.ve[:, :], st[:, :, 1], st[:, :, 4], ALU.subtract))
    nv.tensor_scalar(c.mean[:, :], c.mean[:, :], 0.5, None, ALU.mult)
    chain(nv.tensor_tensor(c.rstd[:, :], st[:, :, 2], st[:, :, 5], ALU.add))
    chain(nv.scalar_tensor_tensor(out=c.ve[:, :], in0=c.ve[:, :], scalar=0.25, in1=c.ve[:, :],
                                  op0=ALU.mult, op1=ALU.mult))
    chain(nv.scalar_tensor_tensor(out=c.ve[:, :], in0=c.rstd[:, :], scalar=1.0 / D, in1=c.ve[:, :],
                                  op0=ALU.mult, op1=ALU.add))
    nv.tensor_scalar(c.ve[:, :], c.ve[:, :], EPS, None, ALU.add).then_inc(ve_ready, 1)
    dve.wait_ge(std_ready, 1 if bst is None else 2)
    chain(nv.reciprocal(c.rstd[:, :], c.std[:, :]))


def act_std(c, act, ve_ready, std_ready, nth=1):
    act.wait_ge(ve_ready, nth)
    c.nc.scalar.activation(c.std[:, :], c.ve[:, :], ACT.Sqrt).then_inc(std_ready, 1)


def load_stage(c, d):
    nc = c.nc
    x_in = [sem(c, f"x_in{b}") for b in range(B)]
    const_in = sem(c, "const_in")
    st = sem(c, "stats_chain")
    const_done = sem(c, "const_done")
    tiled_f = sb(c, "tiled_f", [SK, HPB * SK])
    zeros = sb(c, "zeros", [P, 17 * D])
    zero_ok, zero_out = sem(c, "zero_ok"), sem(c, "zero_out")
    xv = c.x[:, :].rearrange("p (q b n) -> p q b n", b=B, n=D)
    with nc.Block() as block:
        @block.sync
        def _(sp):
            for b in range(B):
                sp.dma_start(xv[:, :, b, :], d["x"][b].rearrange("(q p) n -> p q n", p=P)).then_inc(x_in[b], 16)
            sp.dma_start(c.ctxT[:, :, :], d["ctxT"].rearrange("(k p) n -> p k n", p=P)).then_inc(const_in, 16)
            sp.dma_start(c.ctxn[:, :, :], d["ctx_1024"].rearrange("b s n -> s b n")).then_inc(const_in, 16)
            sp.wait_ge(const_in, 128)
            sp.wait_ge(zero_ok, 1)
            for j in range(2):
                sp.dma_start(c.xd[j * 17 * P:(j + 1) * 17 * P, :].rearrange("(p r) n -> p (r n)", p=P),
                             zeros[:, :]).then_inc(zero_out, 16)
            sp.dma_start(c.yd[E3 * CAP:, :].rearrange("(p r) n -> p (r n)", p=P), zeros[:, 0:OVB * D]
                         ).then_inc(zero_out, 16)
            sp.wait_ge(zero_out, 48)

        @block.gpsimd
        def _(pool):
            nc.gpsimd.memset(zeros[:, :], 0.0).then_inc(zero_ok, 1)

        @block.scalar
        def _(act):
            act.dma_start(c.ident[:, :], d["c_ident"]).then_inc(const_in, 16)
            act.dma_start(tiled_f[:, :], d["c_tiled"]).then_inc(const_in, 16)
            act.dma_start(c.hmask[:, :], d["c_hmask"]).then_inc(const_in, 16)
            act.dma_start(c.hmask2[:, :], d["c_hmask2"]).then_inc(const_in, 16)
            act.dma_start(c.down[:, :], d["c_down"].partition_broadcast(P)).then_inc(const_in, 16)
            act.dma_start(c.down4[:, :], d["c_down4"].partition_broadcast(P)).then_inc(const_in, 16)

        @block.vector
        def _(dve):
            for i in range(NT):
                if i < 2:
                    dve.wait_ge(x_in[i], 16)
                nc.vector.bn_stats(bst_of(c, i), xt(c, i)).then_inc(st, 1)
            dve.wait_ge(const_in, 128)
            nc.vector.tensor_copy(c.tiledI[:, :], tiled_f[:, :])
            nc.vector.tensor_copy(c.identb[:, :], c.ident[:, :]).then_inc(const_done, 1)
            nc.vector.memset(c.ones[:, :], 1.0)


def attn16(c, d, n, masked_when_zero, has_bias, scale, w, nxt=None):
    nc = c.nc
    L = f"a{n}_"
    mraw = sb(c, L + "mraw", [SK, B, S], I32 if masked_when_zero else U8)
    maskT = sb(c, L + "maskT", [SK, B * S], BF16)
    KT = sb(c, L + "KT", [P, KC, B * SK])
    KB = sb(c, L + "KB", [P, KC, B, 8, SK])
    VB = sb(c, L + "VB", [P, B, NBLK * VHEADS, VC])
    ctxP = sb(c, L + "ctxP", [P, KC * B, PERIODS, SK])
    vsel = sb(c, L + "vsel", [P, NBLK * VHEADS])
    bvb = sb(c, L + "bvb", [P, NBLK * VHEADS * HD]) if has_bias else None
    names = ("w_in", "mask_in", "k_ps", "k_sb", "kb_ok", "v_ps", "v_sb", "v_tmp", "ctx_ok", "mask_ok", "ve_ok", "std_ok", "chain",
             "ln_ok", "lnT_ps", "lnT_ok", "q_ps", "qT_ok", "s_ps", "shifted", "exp_ok", "pT_ps", "pT_ok",
             "pv_ps", "o_ok", "oT_ps", "oT_ok", "y_ps", "y_used", "biased", "mx_chain", "stats_ok")
    (w_in, mask_in, k_ps, k_sb, kb_ok, v_ps, v_sb, v_tmp, ctx_ok, mask_ok, ve_ok, std_ok, chain_s,
     ln_ok, lnT_ps, lnT_ok, q_ps, qT_ok, s_ps, shifted, exp_ok, pT_ps, pT_ok,
     pv_ps, o_ok, oT_ps, oT_ok, y_ps, y_used, biased, mx_chain, stats_ok) = [sem(c, L + s) for s in names]
    n_in = 6 + (3 if has_bias else 0)
    bank_s = c.psall[:, 0:3 * 512]
    bank_pT = [c.ps[3], c.ps[4]]
    bank_t = c.ps[5]
    bank_q = c.ps[6]
    bank_pv = bank_y = c.ps[7]
    bank_v = [c.ps[0], c.ps[1]]
    sview = bank_s.rearrange("p (b n) -> p b n", b=3)

    with nc.Block() as block:
        @block.sync
        def _(sp):
            for k, name in enumerate(("Wk", "Wv", "Wq", "Wo")):
                sp.dma_start(c.W[k][:, :, :], d[w[name]].rearrange("(k p) n -> p k n", p=P)).then_inc(w_in, 16)
            sp.dma_start(c.bo[:, :], d[w["bo"]].partition_broadcast(P)).then_inc(w_in, 16)
            if has_bias:
                sp.dma_start(c.bq[:, :], d[w["bq"]]).then_inc(w_in, 16)
                sp.dma_start(c.bk[:, :], d[w["bk"]]).then_inc(w_in, 16)
                sp.dma_start(bvb[:, :], d[w["bv"]].partition_broadcast(P)).then_inc(w_in, 16)
            sp.dma_start(vsel[:, :], d["c_vsel"]).then_inc(w_in, 16)
            msrc = d[w["mask"]]
            sp.dma_start(mraw[:, :, :] if masked_when_zero else mraw[:, :, :].bitcast(I32), msrc).then_inc(mask_in, 16)

        @block.gpsimd
        def _(pool):
            nc.gpsimd.tensor_copy(ctxP[:, :, :, :], c.ctxT[:, :, :].rearrange("p k (b n) -> p (k b) n", b=B)
                                  .unsqueeze(2).to_broadcast([P, KC * B, PERIODS, SK])).then_inc(ctx_ok, 1)
            pool.wait_ge(mask_in, 16)
            nc.gpsimd.tensor_scalar(maskT[:, :], mraw[:, :, :].rearrange("k b s -> k (b s)"), 0.0, NEG,
                                    ALU.is_equal if masked_when_zero else ALU.is_gt, ALU.mult).then_inc(mask_ok, 1)
            pool.wait_ge(w_in, 16 * n_in)

            def step(i, b):
                pool.wait_ge(ln_ok, i + 1)
                nc.gpsimd.tensor_tensor(xt(c, i), xt(c, i), c.bo[:, :], ALU.add).then_inc(biased, 1)
            pipeline(pool, step, 0, 0, NT, NT)

        @block.vector
        def _(dve):
            chain = Chain(dve, chain_s)
            dve_rstd(c, dve, chain, ve_ok, std_ok)
            nv = nc.vector

            def layer_norm(i, b):
                wait(dve, lnT_ps, i - 1)
                nv.tensor_scalar(c.ln[b][:, :], xt(c, i), mean_of(c, i), rstd_of(c, i),
                                 ALU.subtract, ALU.mult).then_inc(ln_ok, 1)
            layer_norm(0, 0)
            layer_norm(1, 1)
            dve.wait_ge(k_sb, 2)
            for k in range(KC):
                for b in range(B):
                    last = nv.tensor_tensor(KB[:, k, b, :, :],
                                            KT[:, k, b * SK:(b + 1) * SK].unsqueeze(1).to_broadcast([P, 8, SK]),
                                            c.hmask[:, :].unsqueeze(2).to_broadcast([P, 8, SK]), ALU.mult)
            last.then_inc(kb_ok, 1)
            dve.wait_ge(w_in, 16 * n_in)
            for b in range(B):
                dve.wait_ge(v_ps, b + 1)
                src = bank_v[b][:, 0:NBLK * VHEADS * HD].rearrange("p (g e) -> p g e", e=HD)
                out = VB[:, b, :, 0:HD]
                if has_bias:
                    nv.tensor_tensor(out, src, bvb[:, :].rearrange("p (g e) -> p g e", e=HD), ALU.add
                                     ).then_inc(v_tmp, 1)
                    dve.wait_ge(v_tmp, b + 1)
                    src = out
                nv.tensor_tensor(out, src, vsel[:, :].unsqueeze(2).to_broadcast([P, NBLK * VHEADS, HD]), ALU.mult)
                nv.tensor_copy(VB[:, b, :, HD], vsel[:, :]).then_inc(v_sb, 1)

            def maxima(i, b):
                dve.wait_ge(s_ps, i + 1)
                nv.reduce_max(c.mx[:, 0:12], sview[:, 0:2, 0:HPB * SK].rearrange("p b (h k) -> p b h k", k=SK), AX)
                nv.reduce_max(c.mx[:, 12:16], sview[:, 2, 0:4 * SK].rearrange("p (h k) -> p h k", k=SK),
                              AX).then_inc(mx_chain, 1)

            def shift(i, b):
                wait(dve, pT_ps, PG * (i - 1))
                dve.wait_ge(mx_chain, i + 1)
                for q in range(3):
                    nh = HPB if q < 2 else 4
                    out = c.prob[b][:, q * HPB * SK:(q * HPB + nh) * SK].rearrange("p (h k) -> p h k", k=SK)
                    last = nv.tensor_tensor(out, sview[:, q, 0:nh * SK].rearrange("p (h k) -> p h k", k=SK),
                                            c.mx[:, q * HPB:q * HPB + nh].unsqueeze(2).to_broadcast([P, nh, SK]),
                                            ALU.subtract)
                last.then_inc(shifted, 1)

            def normalise(i, b):
                dve.wait_ge(pv_ps, i + 1)
                pv = bank_pv[:, 0:H * VC].rearrange("p (h e) -> p h e", e=VC)
                chain(nv.reciprocal(c.rden[:, :], pv[:, :, HD]))
                nv.tensor_tensor(c.o[b][:, :].rearrange("p (h e) -> p h e", e=HD), pv[:, :, 0:HD],
                                 c.rden[:, :].unsqueeze(2).to_broadcast([P, H, HD]), ALU.mult).then_inc(o_ok, 1)

            def residual(i, b):
                dve.wait_ge(y_ps, i + 1)
                dve.wait_ge(biased, i + 1)
                nv.tensor_tensor(xt(c, i), xt(c, i), bank_y[:, 0:D], ALU.add).then_inc(y_used, 1)

            def step(t, b):
                chain.at((CH0 + max(0, min(t - 1, NT))) if is_static(t) else t + (CH0 - 1))
                if inside(t + 2):
                    layer_norm(t + 2, b)
                if inside(t):
                    maxima(t, b)
                if inside(t - 2):
                    residual(t - 2, b)
                if inside(t):
                    shift(t, b)
                if inside(t - 2):
                    dve.wait_ge(y_used, t - 1)
                    nv.bn_stats(bst_of(c, t - 2), xt(c, t - 2)).then_inc(stats_ok, 1)
                if inside(t - 1):
                    normalise(t - 1, 1 - b)
            pipeline(dve, step, 0, 2, NT - 2, NT + 2)

        @block.scalar
        def _(act):
            na = nc.scalar
            act_std(c, act, ve_ok, std_ok)
            act.wait_ge(k_ps, 1)
            for k in range(KC):
                if has_bias:
                    ins = na.activation(KT[:, k, :], c.ps[k + 2][:, 0:B * SK], ACT.Identity, bias=c.bk[:, k:k + 1])
                else:
                    ins = na.activation(KT[:, k, :], c.ps[k + 2][:, 0:B * SK], ACT.Copy)
                ins.then_inc(k_sb, 1)

            def lnT_copy(i, b):
                act.wait_ge(lnT_ps, i + 1)
                na.activation(c.lnT[b][:, :], bank_t[:, 0:D], ACT.Copy).then_inc(lnT_ok, 1)

            def q_copy(i, b):
                act.wait_ge(q_ps, i + 1)
                if has_bias:
                    for k in range(KC):
                        ins = na.activation(c.qT[b][:, k * P:(k + 1) * P], bank_q[:, k * P:(k + 1) * P],
                                            ACT.Identity, bias=c.bq[:, k:k + 1])
                else:
                    ins = na.activation(c.qT[b][:, :], bank_q[:, 0:D], ACT.Copy)
                ins.then_inc(qT_ok, 1)

            def exps(i, b):
                act.wait_ge(shifted, i + 1)
                na.activation(c.prob[b][:, :], c.prob[b][:, :], ACT.Exp, scale=scale).then_inc(exp_ok, 1)

            def pT_copy(i, b):
                wait(act, pv_ps, i - 1)
                for g, (j0, j1) in enumerate(PGROUPS):
                    act.wait_ge(pT_ps, i * PG + (g + 1))
                    na.activation(c.pT[b][:, j0 * P:j1 * P], bank_pT[g % 2][:, 0:(j1 - j0) * P],
                                  ACT.Copy).then_inc(pT_ok, 1)

            def oT_copy(i, b):
                act.wait_ge(oT_ps, i + 1)
                na.activation(c.oT[b][:, :], bank_t[:, 0:D], ACT.Copy).then_inc(oT_ok, 1)

            lnT_copy(0, 0)
            lnT_copy(1, 1)
            q_copy(0, 0)

            def step(t, b):
                if inside(t - 2):
                    oT_copy(t - 2, b)
                if inside(t - 1):
                    pT_copy(t - 1, 1 - b)
                if inside(t + 1):
                    q_copy(t + 1, 1 - b)
                if inside(t + 2):
                    lnT_copy(t + 2, b)
                if inside(t):
                    exps(t, b)
            pipeline(act, step, 0, 2, NT - 2, NT + 2)

        @block.tensor
        def _(pe):
            nt = nc.tensor
            pe.wait_ge(w_in, 16 * n_in)
            for m in range(KC):
                for k in range(KC):
                    last = nt.matmul(c.ps[m + 2][:, 0:B * SK], c.W[0][:, k, m * P:(m + 1) * P], c.ctxT[:, k, :],
                                     start=(k == 0), stop=(k == KC - 1))
            last.then_inc(k_ps, 1)
            pe.wait_ge(ctx_ok, 1)
            for b in range(B):
                for j, h0 in enumerate(VHEAD0):
                    key0 = j * P % SK
                    for k in range(KC):
                        rows = ctxP[:, k * B + b, :, :].rearrange("p r k -> p (r k)")
                        last = nt.matmul(bank_v[b][:, j * VHEADS * HD:(j + 1) * VHEADS * HD],
                                         rows[:, key0:key0 + P], c.W[1][:, k, h0 * HD:(h0 + VHEADS) * HD],
                                         start=(k == 0), stop=(k == KC - 1))
                last.then_inc(v_ps, 1)

            def lnT(i, b):
                pe.wait_ge(ln_ok, i + 1)
                wait(pe, lnT_ok, i)
                wait(pe, oT_ok, i - 3)
                for k in range(KC):
                    last = nt.transpose(bank_t[:, k * P:(k + 1) * P], c.ln[b][:, k * P:(k + 1) * P], c.ident[:, :])
                last.then_inc(lnT_ps, 1)

            def queries(i, b):
                pe.wait_ge(lnT_ok, i + 1)
                wait(pe, qT_ok, i)
                for m in range(KC):
                    for k in range(KC):
                        last = nt.matmul(bank_q[:, m * P:(m + 1) * P], c.W[2][:, k, m * P:(m + 1) * P],
                                         c.lnT[b][:, k * P:(k + 1) * P], start=(k == 0), stop=(k == KC - 1))
                last.then_inc(q_ps, 1)

            def scores(i, b, q0):
                pe.wait_ge(qT_ok, i + 1)
                wait(pe, shifted, i)
                for half, h0, h1 in HEAD_RUNS:
                    q, o = h0 // HPB, (h0 % HPB) * SK
                    nt.matmul(sview[:, q, o:o + (h1 - h0) * SK], c.qT[b][:, half * P:(half + 1) * P],
                              KB[:, half, b, h0 - 8 * half:h1 - 8 * half, :].rearrange("p h k -> p (h k)"),
                              start=(h0 % HPB == 0), stop=False, skip_group_check=True)
                for q in range(3):
                    nh = HPB if q < 2 else 4
                    last = nt.matmul(sview[:, q, 0:nh * SK], maskT[:, ds(q0, P)],
                                     c.tiledI[:, 0:nh * SK], start=False, stop=True, skip_group_check=True)
                last.then_inc(s_ps, 1)

            def prob_transpose(i, b, g):
                if g == 0:
                    pe.wait_ge(exp_ok, i + 1)
                wait(pe, pT_ok, i * PG + max(g - 1, 0))
                j0, j1 = PGROUPS[g]
                for j in range(j0, j1):
                    rows = min(P, H * SK - j * P)
                    last = nt.transpose(bank_pT[g % 2][0:rows, (j - j0) * P:(j - j0 + 1) * P],
                                        c.prob[b][:, j * P:j * P + rows], c.ident[:, :])
                last.then_inc(pT_ps, 1)

            def weighted_values(i, b):
                pe.wait_ge(pT_ok, i * PG + PG)
                wait(pe, y_used, i)
                for j, h0 in enumerate(VHEAD0):
                    rows = min(P, H * SK - j * P)
                    last = nt.matmul(bank_pv[:, h0 * VC:(h0 + VHEADS) * VC], c.pT[b][0:rows, j * P:(j + 1) * P],
                                     VB[0:rows, b, j * VHEADS:(j + 1) * VHEADS, :].rearrange("p g e -> p (g e)"),
                                     start=(j == 0), stop=(j == NBLK - 1), skip_group_check=True)
                last.then_inc(pv_ps, 1)

            def o_transpose(i, b):
                pe.wait_ge(o_ok, i + 1)
                wait(pe, lnT_ok, min(i + 4, NT) if is_static(i) else i + 4)
                for k in range(KC):
                    last = nt.transpose(bank_t[:, k * P:(k + 1) * P], c.o[b][:, k * P:(k + 1) * P], c.ident[:, :])
                last.then_inc(oT_ps, 1)

            def project(i, b):
                pe.wait_ge(oT_ok, i + 1)
                for k in range(KC):
                    last = nt.matmul(bank_y[:, 0:D], c.oT[b][:, k * P:(k + 1) * P], c.W[3][:, k, :],
                                     start=(k == 0), stop=(k == KC - 1))
                last.then_inc(y_ps, 1)

            lnT(0, 0)
            lnT(1, 1)
            queries(0, 0)
            pe.wait_ge(kb_ok, 1)
            pe.wait_ge(v_sb, B)
            pe.wait_ge(mask_ok, 1)

            def step(t, b):
                if inside(t):
                    q0 = b * S + (t // 2) * P if is_static(t) else t * (P // 2) + (b * S - b * (P // 2))
                    scores(t, b, q0)
                if inside(t - 2):
                    o_transpose(t - 2, b)
                if inside(t - 1):
                    prob_transpose(t - 1, 1 - b, 0)
                    prob_transpose(t - 1, 1 - b, 1)
                if inside(t - 2):
                    project(t - 2, b)
                if inside(t - 1):
                    prob_transpose(t - 1, 1 - b, 2)
                if inside(t + 1):
                    queries(t + 1, 1 - b)
                if inside(t + 2):
                    lnT(t + 2, b)
                if inside(t - 1):
                    weighted_values(t - 1, 1 - b)
            pipeline(pe, step, 0, 2, NT - 2, NT + 2)


def sems(c, prefix, *names):
    return {n: sem(c, prefix + n) for n in names}


NORM = ("ve_ok", "std_ok", "chain", "ln_ok", "lnT_ps", "lnT_ok")



def dve_ln_all(c, dve, s, chain, keep=None):
    dve_rstd(c, dve, chain, s["ve_ok"], s["std_ok"])
    nv = c.nc.vector

    def step(i, b):
        wait(dve, s["lnT_ps"], i - 1)
        nv.tensor_scalar(c.ln[b][:, :], xt(c, i), mean_of(c, i), rstd_of(c, i),
                         ALU.subtract, ALU.mult).then_inc(s["ln_ok"], 1)
    pipeline(dve, step, 0, 2, NT, NT)


def pe_ln_all(c, pe, s):
    nt = c.nc.tensor

    def step(i, b):
        pe.wait_ge(s["ln_ok"], i + 1)
        wait(pe, s["lnT_ok"], i - 1)
        for k in range(KC):
            last = nt.transpose(c.ps[6 + b][:, k * P:(k + 1) * P], c.ln[b][:, k * P:(k + 1) * P], c.ident[:, :])
        last.then_inc(s["lnT_ps"], 1)
    pipeline(pe, step, 0, 2, NT, NT)


def act_ln_all(c, act, s):
    act_std(c, act, s["ve_ok"], s["std_ok"])
    na = c.nc.scalar

    def step(i, b):
        act.wait_ge(s["lnT_ps"], i + 1)
        na.activation(lnT_tile(c, i), c.ps[6 + b][:, 0:D].rearrange("p (k n) -> p k n", k=KC),
                      ACT.Copy).then_inc(s["lnT_ok"], 1)
    pipeline(act, step, 0, 2, NT, NT)


def lnT_tile(c, i):
    return c.lnT_all[:, :, ds(i * P, P)]


def pe_router(c, s, w):
    for i in range(NT):
        for k in range(KC):
            last = c.nc.tensor.matmul(c.ps[5][:, i * 8:(i + 1) * 8], c.lnT_all[:, k, i * P:(i + 1) * P],
                                      w[:, k, :], start=(k == 0), stop=(k == KC - 1))
    last.then_inc(s["logits_ps"], 1)


def bc(ap, g):
    return ap.unsqueeze(2).to_broadcast([P, NT, g])


def top1(c, chain, l, g, hot, tmp, m):
    nv = c.nc.vector
    chain(nv.reduce_max(m, l, AX))
    chain(nv.tensor_tensor(tmp, l, bc(m, g), ALU.is_equal))
    chain(nv.tensor_tensor(tmp, tmp, c.down[:, 0:NT * g].rearrange("p (i g) -> p i g", g=g)
                           if g == 8 else c.down4[:, 0:NT * g].rearrange("p (i g) -> p i g", g=g), ALU.mult))
    chain(nv.reduce_max(c.first[:, :], tmp, AX))
    chain(nv.tensor_tensor(hot, tmp, bc(c.first[:, :], g), ALU.is_equal))


def top2(c, chain, l, g, keep, l2, tmp, m):
    nv = c.nc.vector
    m2 = c.m2[:, :]
    top1(c, chain, l, g, keep, tmp, m)
    chain(nv.scalar_tensor_tensor(out=l2, in0=keep, scalar=NEG, in1=l, op0=ALU.mult, op1=ALU.add))
    top1(c, chain, l2, g, l2, tmp, m2)
    chain(nv.tensor_tensor(keep, keep, l2, ALU.add))


def g8(t):
    return t[:, :].rearrange("p (i g) -> p i g", g=8)


def moe0(c, d):
    nc = c.nc
    W = sb(c, "m0_W", [P, KC, 8 * D])
    gw = sb(c, "m0_gw", [P, KC, 8])
    gb = sb(c, "m0_gb", [P, 8])
    eb = sb(c, "m0_eb", [8, D])
    gT = sb(c, "m0_gT", [8, NT * P])
    gTs = [sb(c, f"m0_gTs{b}", [8, P]) for b in range(2)]
    s = sems(c, "m0_", *NORM, "w_in", "logits_ps", "max_ok", "exp_ok", "gates_ok", "gT_ps", "gT_ok", "tile_in",
             "gtile_in", "e_ps", "acc", "bias_ps", "y_used", "x_ok")
    gates = g8(c.gates)
    with nc.Block() as block:
        @block.sync
        def _(sp):
            sp.dma_start(gw[:, :, :], d["L0_ffn_gate_wT"].rearrange("(k p) e -> p k e", p=P)).then_inc(s["w_in"], 16)
            sp.dma_start(gb[:, :], d["L0_ffn_gate_b"].partition_broadcast(P)).then_inc(s["w_in"], 16)
            sp.dma_start(eb[:, :], d["L0_ffn_expert_b"]).then_inc(s["w_in"], 16)
            for k in range(KC):
                sp.dma_start(W[:, k, :].rearrange("p (e n) -> p e n", e=8),
                             d["L0_ffn_expert_w"][:, k * P:(k + 1) * P, :].rearrange("e p n -> p e n")
                             ).then_inc(s["w_in"], 16)

        @block.vector
        def _(dve):
            nv = nc.vector
            chain = Chain(dve, s["chain"])
            dve_ln_all(c, dve, s, chain)
            dve.wait_ge(s["logits_ps"], 1)
            l = g8(c.lg)
            chain(nv.tensor_tensor(l, g8(c.ps[5][:, 0:NT * 8]), gb[:, :].unsqueeze(1).to_broadcast([P, NT, 8]), ALU.add))
            top2(c, chain, l, 8, gates, g8(c.lg2), g8(c.lgt), c.m1[:, :])
            nv.tensor_tensor(l, l, bc(c.m1[:, :], 8), ALU.subtract).then_inc(s["max_ok"], 1)
            dve.wait_ge(s["exp_ok"], 1)
            chain(nv.tensor_tensor(gates, gates, l, ALU.mult))
            chain(nv.reduce_sum(c.m1[:, :], gates, AX))
            chain(nv.reciprocal(c.m1[:, :], c.m1[:, :]))
            nv.tensor_tensor(gates, gates, bc(c.m1[:, :], 8), ALU.mult).then_inc(s["gates_ok"], 1)
            for q in range(4):
                dve.wait_ge(s["gT_ps"], q + 1)
                nv.tensor_copy(gT[:, q * 512:(q + 1) * 512], c.ps[q][0:8, :]).then_inc(s["gT_ok"], 1)

            def step(i, b):
                for p in range(4):
                    dve.wait_ge(s["e_ps"], i * 4 + (p + 1))
                    for o in range(2):
                        src = c.ps[p][:, o * D:(o + 1) * D]
                        gate = c.gates[:, ds(i * 8 + (2 * p + o), 1)]
                        if p == 0:
                            ins = nv.tensor_scalar(c.acc[o][:, :], src, gate, None, ALU.mult)
                        else:
                            dve.wait_ge(s["acc"], i * 8 + (2 * p + o - 1))
                            ins = nv.scalar_tensor_tensor(out=c.acc[o][:, :], in0=src, scalar=gate,
                                                          in1=c.acc[o][:, :], op0=ALU.mult, op1=ALU.add)
                        ins.then_inc(s["acc"], 1)
                dve.wait_ge(s["acc"], i * 8 + 8)
                dve.wait_ge(s["bias_ps"], i + 1)
                nv.tensor_tensor(xt(c, i), xt(c, i), c.acc[1][:, :], ALU.add)
                nv.tensor_tensor(c.acc[0][:, :], c.ps[4][:, 0:D], c.acc[0][:, :], ALU.add).then_inc(s["y_used"], 1)
                dve.wait_ge(s["y_used"], i + 1)
                nv.tensor_tensor(xt(c, i), xt(c, i), c.acc[0][:, :], ALU.add).then_inc(s["x_ok"], 1)
                dve.wait_ge(s["x_ok"], i + 1)
                nv.tensor_copy(c.gap[:, b:b + 1], c.ones[:, 0:1])
                nv.bn_stats(bst_of(c, i), xt(c, i))
            pipeline(dve, step, 0, 0, NT, NT)

        @block.scalar
        def _(act):
            na = nc.scalar
            act_ln_all(c, act, s)
            act.wait_ge(s["max_ok"], 1)
            na.activation(c.lg[:, :], c.lg[:, :], ACT.Exp).then_inc(s["exp_ok"], 1)

            def step(i, b):
                wait(act, s["bias_ps"], i - 1)
                na.activation(c.lnT[b][:, :].rearrange("p (k n) -> p k n", k=KC), lnT_tile(c, i),
                              ACT.Copy).then_inc(s["tile_in"], 1)
            pipeline(act, step, 0, 2, NT, NT)

        @block.gpsimd
        def _(pool):
            def step(i, b):
                wait(pool, s["bias_ps"], i - 1)
                nc.gpsimd.tensor_copy(gTs[b][:, :], gT[:, ds(i * P, P)]).then_inc(s["gtile_in"], 1)
            pool.wait_ge(s["gT_ok"], 4)
            pipeline(pool, step, 0, 2, NT, NT)

        @block.tensor
        def _(pe):
            nt = nc.tensor
            pe_ln_all(c, pe, s)
            pe.wait_ge(s["lnT_ok"], NT)
            pe.wait_ge(s["w_in"], 16 * 5)
            pe_router(c, s, gw)
            pe.wait_ge(s["gates_ok"], 1)
            for i in range(NT):
                last = nt.transpose(c.ps[i // 4][0:8, (i % 4) * P:(i % 4 + 1) * P], c.gates[:, i * 8:(i + 1) * 8],
                                    c.ident[:, :])
                if i % 4 == 3:
                    last.then_inc(s["gT_ps"], 1)

            pe.wait_ge(s["gT_ok"], 4)

            def step(i, b):
                pe.wait_ge(s["tile_in"], i + 1)
                for p in range(4):
                    wait(pe, s["acc"], i * 8 - 6 + 2 * p)
                    for k in range(KC):
                        last = nt.matmul(c.ps[p][:, :], c.lnT[b][:, k * P:(k + 1) * P],
                                         W[:, k, p * 512:(p + 1) * 512], start=(k == 0), stop=(k == KC - 1))
                    last.then_inc(s["e_ps"], 1)
                pe.wait_ge(s["gtile_in"], i + 1)
                wait(pe, s["y_used"], i)
                nt.matmul(c.ps[4][:, 0:D], gTs[b][:, :], eb[:, :], start=True, stop=True).then_inc(s["bias_ps"], 1)
            pipeline(pe, step, 0, 2, NT, NT)


ROUND = 1.5 * 2 ** 23
QMAX = 127.0


def int8_linear(c, d):
    nc = c.nc
    R = sb(c, "i8_R", [P, KC, D])
    Rq = sb(c, "i8_Rq", [P, KC, D], BF16)
    RQ = sb(c, "i8_RQ", [P, KC, D], BF16)
    rs, rinv = sb(c, "i8_rs", [P, KC]), sb(c, "i8_rinv", [P, KC])
    rsw = sb(c, "i8_rsw", [P, KC, P])
    rsB = sb(c, "i8_rsB", [P, D])
    ls, linv = sb(c, "i8_ls", [P, NT]), sb(c, "i8_linv", [P, NT])
    r = [sb(c, f"i8_r{b}", [P, D]) for b in range(2)]
    q = [sb(c, f"i8_q{b}", [P, D], BF16) for b in range(2)]
    qT = [sb(c, f"i8_qT{b}", [P, D], BF16) for b in range(2)]
    s = sems(c, "i8_", "ve_ok", "std_ok", "chain", "w_in", "rq_ok", "rT_ps", "RQ_ok", "rsB_ps", "t_ok", "r_ok", "q_ok",
             "qT_ps", "qT_ok", "y_ps", "y_ok", "x_ok", "ln_done")
    with nc.Block() as block:
        @block.sync
        def _(sp):
            sp.dma_start(R[:, :, :], d["L1_ffn_rhsT"].rearrange("(m p) k -> p m k", p=P)).then_inc(s["w_in"], 16)

        @block.vector
        def _(dve):
            nv = nc.vector
            chain = Chain(dve, s["chain"])
            dve.wait_ge(s["w_in"], 16)
            chain(nv.tensor_reduce(out=rs[:, :], in_=R[:, :, :], axis=AX, op=ALU.max, apply_absolute_value=True))
            chain(nv.tensor_scalar(rs[:, :], rs[:, :], 1e-12, 1.0 / QMAX, ALU.max, ALU.mult))
            chain(nv.reciprocal(rinv[:, :], rs[:, :]))
            for m in range(KC):
                chain(nv.tensor_scalar(R[:, m, :], R[:, m, :], rinv[:, m:m + 1], ROUND, ALU.mult, ALU.add))
                chain(nv.tensor_scalar(R[:, m, :], R[:, m, :], ROUND, QMAX, ALU.subtract, ALU.min))
                nv.tensor_scalar(Rq[:, m, :], R[:, m, :], -QMAX, None, ALU.max)
                nv.tensor_scalar(rsw[:, m, :], c.ones[:, :], rs[:, m:m + 1], None, ALU.mult).then_inc(s["rq_ok"], 1)
            dve_rstd(c, dve, chain, s["ve_ok"], s["std_ok"])

            def norm(i, b):
                nv.tensor_scalar(c.lnk[:, ds(i * D, D)], xt(c, i), mean_of(c, i), rstd_of(c, i),
                                 ALU.subtract, ALU.mult).then_inc(s["ln_done"], 1)
            pipeline(dve, norm, 0, 0, NT, NT)
            dve.wait_ge(s["ln_done"], NT)
            chain(nv.tensor_reduce(out=ls[:, :], in_=c.lnk[:, :].rearrange("p (i n) -> p i n", n=D), axis=AX,
                                   op=ALU.max, apply_absolute_value=True))
            chain(nv.tensor_scalar(ls[:, :], ls[:, :], 1e-12, 1.0 / QMAX, ALU.max, ALU.mult))
            chain(nv.reciprocal(linv[:, :], ls[:, :]))
            dve.wait_ge(s["rsB_ps"], 1)
            chain(nv.tensor_copy(rsB[:, :], c.ps[1][:, 0:D]))

            def step(t, b):
                if inside(t):
                    nv.tensor_scalar(r[b][:, :], c.lnk[:, ds(t * D, D)], linv[:, ds(t, 1)], ROUND,
                                     ALU.mult, ALU.add).then_inc(s["t_ok"], 1)
                if inside(t - 2):
                    dve.wait_ge(s["y_ps"], t - 1)
                    nv.scalar_tensor_tensor(out=c.acc[b][:, :], in0=c.ps[4 + b][:, 0:D], scalar=ls[:, ds(t - 2, 1)],
                                            in1=rsB[:, :], op0=ALU.mult, op1=ALU.mult).then_inc(s["y_ok"], 1)
                if inside(t):
                    dve.wait_ge(s["t_ok"], t + 1)
                    nv.tensor_scalar(r[b][:, :], r[b][:, :], ROUND, QMAX, ALU.subtract, ALU.min).then_inc(s["r_ok"], 1)
                if inside(t - 2):
                    dve.wait_ge(s["y_ok"], t - 1)
                    nv.tensor_tensor(xt(c, t - 2), xt(c, t - 2), c.acc[b][:, :], ALU.add).then_inc(s["x_ok"], 1)
                if inside(t):
                    dve.wait_ge(s["r_ok"], t + 1)
                    wait(dve, s["qT_ps"], t - 1)
                    nv.tensor_scalar(q[b][:, :], r[b][:, :], -QMAX, None, ALU.max).then_inc(s["q_ok"], 1)
                if inside(t - 2):
                    dve.wait_ge(s["x_ok"], t - 1)
                    nv.tensor_copy(c.gap[:, b:b + 1], c.ones[:, 0:1])
                    nv.bn_stats(bst_of(c, t - 2), xt(c, t - 2))
            pipeline(dve, step, 0, 2, NT, NT + 2)

        @block.scalar
        def _(act):
            na = nc.scalar
            act.wait_ge(s["rT_ps"], 1)
            na.activation(RQ[:, :, :].rearrange("p k n -> p (k n)"), c.ps[0].bitcast(BF16)[:, 0:KC * D],
                          ACT.Copy).then_inc(s["RQ_ok"], 1)
            act_std(c, act, s["ve_ok"], s["std_ok"])

            def step(i, b):
                act.wait_ge(s["qT_ps"], i + 1)
                wait(act, s["y_ps"], i - 1)
                na.activation(qT[b][:, :], c.ps[6 + b].bitcast(BF16)[:, 0:D], ACT.Copy).then_inc(s["qT_ok"], 1)
            pipeline(act, step, 0, 2, NT, NT)

        @block.tensor
        def _(pe):
            nt = nc.tensor
            pe.wait_ge(s["rq_ok"], KC)
            rT = c.ps[0].bitcast(BF16)
            for k in range(KC):
                for m in range(KC):
                    last = nt.transpose(rT[:, k * D + m * P:k * D + (m + 1) * P], Rq[:, m, k * P:(k + 1) * P],
                                        c.identb[:, :])
            last.then_inc(s["rT_ps"], 1)
            for m in range(KC):
                last = nt.matmul(c.ps[1][:, m * P:(m + 1) * P], rsw[:, m, :], c.ident[:, :], start=True, stop=True)
            last.then_inc(s["rsB_ps"], 1)
            pe.wait_ge(s["RQ_ok"], 1)

            def transpose(i, b):
                pe.wait_ge(s["q_ok"], i + 1)
                wait(pe, s["qT_ok"], i - 1)
                for k in range(KC):
                    last = nt.transpose(c.ps[6 + b].bitcast(BF16)[:, k * P:(k + 1) * P],
                                        q[b][:, k * P:(k + 1) * P], c.identb[:, :])
                last.then_inc(s["qT_ps"], 1)

            def product(i, b):
                pe.wait_ge(s["qT_ok"], i + 1)
                wait(pe, s["y_ok"], i - 1)
                for k in range(KC):
                    last = nt.matmul(c.ps[4 + b][:, 0:D], qT[b][:, k * P:(k + 1) * P], RQ[:, k, :],
                                     start=(k == 0), stop=(k == KC - 1))
                last.then_inc(s["y_ps"], 1)

            def step(t, b):
                if inside(t):
                    transpose(t, b)
                if inside(t - 1):
                    product(t - 1, 1 - b)
            pipeline(pe, step, 0, 2, NT, NT + 1)


def attn1(c, d):
    nc = c.nc
    mraw = sb(c, "b_mraw", [SK, B * S], I32)
    maskT = sb(c, "b_maskT", [SK, B * S], BF16)
    ctxs = sb(c, "b_ctxs", [P, KC, B * SK])
    gam, bet = sb(c, "b_gam", [P, D]), sb(c, "b_bet", [P, D])
    bsty = sb(c, "b_bsty", [P, NT * 6])
    nmx, rsum, rd = ([sb(c, f"b_{n}{b}", [P, 1]) for b in range(2)] for n in ("nmx", "rsum", "rd"))
    s = sems(c, "b_", *NORM, "w_in", "mask_in", "mask_ok", "ctxs_ok", "s_ps", "nmax_ok", "exp_ok", "pT_ps", "pT_ok",
             "pv_ps", "y_ok", "yst", "z_ok", "x_ok", "biased")
    with nc.Block() as block:
        @block.sync
        def _(sp):
            sp.dma_start(mraw[:, :], d["maskT2"]).then_inc(s["mask_in"], 16)
            sp.dma_start(gam[:, :], d["L2_xattn_gamma"].partition_broadcast(P)).then_inc(s["w_in"], 16)
            sp.dma_start(bet[:, :], d["L2_xattn_beta"].partition_broadcast(P)).then_inc(s["w_in"], 16)

        @block.gpsimd
        def _(pool):
            pool.wait_ge(s["mask_in"], 16)
            nc.gpsimd.tensor_scalar(maskT[:, :], mraw[:, :], 0.0, NEG, ALU.is_equal, ALU.mult).then_inc(s["mask_ok"], 1)
            pool.wait_ge(s["w_in"], 32)

            def step(i, b):
                pool.wait_ge(s["ln_ok"], i + 1)
                nc.gpsimd.tensor_tensor(xt(c, i), xt(c, i), bet[:, :], ALU.add).then_inc(s["biased"], 1)
            pipeline(pool, step, 0, 0, NT, NT)

        @block.vector
        def _(dve):
            nv = nc.vector
            chain = Chain(dve, s["chain"])
            nv.tensor_scalar(ctxs[:, :, :], c.ctxT[:, :, :], float(D) ** -0.5, None, ALU.mult).then_inc(s["ctxs_ok"], 1)
            dve_rstd(c, dve, chain, s["ve_ok"], s["std_ok"])

            def layer_norm(i, b):
                wait(dve, s["lnT_ps"], i - 1)
                nv.tensor_scalar(c.ln[b][:, :], xt(c, i), mean_of(c, i), rstd_of(c, i),
                                 ALU.subtract, ALU.mult).then_inc(s["ln_ok"], 1)

            def negative_max(i, b):
                dve.wait_ge(s["s_ps"], i + 1)
                wait(dve, s["exp_ok"], i - 1)
                nv.tensor_reduce(out=nmx[b][:, :], in_=c.ps[b][:, 0:SK], axis=AX, op=ALU.max,
                                 negate=True).then_inc(s["nmax_ok"], 1)

            def weighted(i, b):
                dve.wait_ge(s["pv_ps"], i + 1)
                chain(nv.reciprocal(rd[b][:, :], rsum[b][:, :]))
                nv.tensor_scalar(c.lnk[:, ds(i * D, D)], c.ps[4 + b][:, 0:D], rd[b][:, :], None,
                                 ALU.mult).then_inc(s["y_ok"], 1)
            layer_norm(0, 0)
            layer_norm(1, 1)

            def step(t, b):
                chain.at((CH0 + max(0, min(t - 1, NT))) if is_static(t) else t + (CH0 - 1))
                if inside(t):
                    negative_max(t, b)
                if inside(t - 1):
                    weighted(t - 1, 1 - b)
                    dve.wait_ge(s["y_ok"], t)
                if inside(t + 2):
                    layer_norm(t + 2, b)
                if inside(t - 1):
                    nv.tensor_copy(c.gap[:, b:b + 1], c.ones[:, 0:1])
                    nv.bn_stats(bsty[:, ds(t * 6 - 6, 6)], c.lnk[:, ds(t * D - D, D)]).then_inc(s["yst"], 1)
            pipeline(dve, step, 0, 2, NT - 2, NT + 1)
            chain.at(CH0 + NT)
            dve.wait_ge(s["yst"], NT)
            dve_rstd(c, dve, chain, s["ve_ok"], s["std_ok"], bsty)
            dve.wait_ge(s["biased"], NT)

            def finish(t, b):
                if inside(t):
                    wait(dve, s["x_ok"], t - 1)
                    nv.scalar_tensor_tensor(out=c.acc[b][:, :], in0=c.lnk[:, ds(t * D, D)], scalar=mean_of(c, t),
                                            in1=gam[:, :], op0=ALU.subtract, op1=ALU.mult).then_inc(s["z_ok"], 1)
                if inside(t - 1):
                    dve.wait_ge(s["z_ok"], t)
                    nv.scalar_tensor_tensor(out=xt(c, t - 1), in0=c.acc[1 - b][:, :], scalar=rstd_of(c, t - 1),
                                            in1=xt(c, t - 1), op0=ALU.mult, op1=ALU.add).then_inc(s["x_ok"], 1)
                if inside(t - 2):
                    dve.wait_ge(s["x_ok"], t - 1)
                    nv.tensor_copy(c.gap[:, b:b + 1], c.ones[:, 0:1])
                    nv.bn_stats(bst_of(c, t - 2), xt(c, t - 2))
            pipeline(dve, finish, 0, 2, NT, NT + 2)

        @block.scalar
        def _(act):
            na = nc.scalar
            act_std(c, act, s["ve_ok"], s["std_ok"])

            def lnT_copy(i, b):
                act.wait_ge(s["lnT_ps"], i + 1)
                wait(act, s["s_ps"], i - 1)
                na.activation(c.lnT[b][:, :], c.ps[6 + b][:, 0:D], ACT.Copy).then_inc(s["lnT_ok"], 1)

            def exps(i, b):
                act.wait_ge(s["nmax_ok"], i + 1)
                wait(act, s["pT_ps"], i - 1)
                wait(act, s["y_ok"], i - 1)
                na.activation(c.prob[b][:, 0:SK], c.ps[b][:, 0:SK], ACT.Exp, bias=nmx[b][:, :],
                              accum_out=rsum[b][:, :]).then_inc(s["exp_ok"], 1)

            def pT_copy(i, b):
                act.wait_ge(s["pT_ps"], i + 1)
                wait(act, s["pv_ps"], i - 1)
                na.activation(c.pT[b][0:SK, 0:P], c.ps[2 + b][0:SK, 0:P], ACT.Copy).then_inc(s["pT_ok"], 1)
            lnT_copy(0, 0)

            def step(t, b):
                if inside(t - 1):
                    pT_copy(t - 1, 1 - b)
                if inside(t + 1):
                    lnT_copy(t + 1, 1 - b)
                if inside(t):
                    exps(t, b)
            pipeline(act, step, 0, 2, NT - 2, NT + 1)
            act_std(c, act, s["ve_ok"], s["std_ok"], 2)

        @block.tensor
        def _(pe):
            nt = nc.tensor
            pe.wait_ge(s["ctxs_ok"], 1)
            pe.wait_ge(s["mask_ok"], 1)

            def lnT(i, b):
                pe.wait_ge(s["ln_ok"], i + 1)
                wait(pe, s["lnT_ok"], i - 1)
                for k in range(KC):
                    last = nt.transpose(c.ps[6 + b][:, k * P:(k + 1) * P], c.ln[b][:, k * P:(k + 1) * P], c.ident[:, :])
                last.then_inc(s["lnT_ps"], 1)

            def scores(i, b, q0):
                pe.wait_ge(s["lnT_ok"], i + 1)
                wait(pe, s["exp_ok"], i - 1)
                for k in range(KC):
                    nt.matmul(c.ps[b][:, 0:SK], c.lnT[b][:, k * P:(k + 1) * P], ctxs[:, k, b * SK:(b + 1) * SK],
                              start=(k == 0), stop=False)
                nt.matmul(c.ps[b][:, 0:SK], maskT[:, ds(q0, P)], c.tiledI[:, 0:SK],
                          start=False, stop=True).then_inc(s["s_ps"], 1)

            def prob_transpose(i, b):
                pe.wait_ge(s["exp_ok"], i + 1)
                wait(pe, s["pT_ok"], i - 1)
                nt.transpose(c.ps[2 + b][0:SK, 0:P], c.prob[b][:, 0:SK], c.ident[:, :]).then_inc(s["pT_ps"], 1)

            def weighted_values(i, b):
                pe.wait_ge(s["pT_ok"], i + 1)
                wait(pe, s["y_ok"], i - 1)
                nt.matmul(c.ps[4 + b][:, 0:D], c.pT[b][0:SK, 0:P], c.ctxn[:, b, :], start=True,
                          stop=True).then_inc(s["pv_ps"], 1)
            lnT(0, 0)

            def step(t, b):
                if inside(t):
                    q0 = b * S + (t // 2) * P if is_static(t) else t * (P // 2) + (b * S - b * (P // 2))
                    scores(t, b, q0)
                if inside(t - 1):
                    prob_transpose(t - 1, 1 - b)
                if inside(t + 1):
                    lnT(t + 1, 1 - b)
                if inside(t - 1):
                    weighted_values(t - 1, 1 - b)
            pipeline(pe, step, 0, 2, NT - 2, NT + 1)


def moe2(c, d):
    nc = c.nc
    WG, WU = sb(c, "m2_WG", [P, KC, 8 * P]), sb(c, "m2_WU", [P, KC, 8 * P])
    WD = sb(c, "m2_WD", [P, 8 * D])
    gw, gb = sb(c, "m2_gw", [P, KC, 8]), sb(c, "m2_gb", [P, 8])
    gs, gkeep, gl2, gt = (sb(c, "m2_" + n, [P, NT * 4]) for n in ("gs", "gkeep", "gl2", "gt"))
    sig, sg, hid = ([sb(c, f"m2_{n}{b}", [P, 512]) for b in range(2)] for n in ("sig", "sg", "hid"))
    s = sems(c, "m2_", *NORM, "w_in", "logits_ps", "scores_ok", "lg_used", "gates_ok", "gu_ps", "sig_ok", "sg_ok",
             "hid_ok", "down_ps", "acc")
    CH = NT // 4
    with nc.Block() as block:
        @block.sync
        def _(sp):
            sp.dma_start(gw[:, :, :], d["L2_ffn_gate_weightT"].rearrange("(k p) e -> p k e", p=P)).then_inc(s["w_in"], 16)
            sp.dma_start(gb[:, :], d["L2_ffn_e_score_correction_bias"].partition_broadcast(P)).then_inc(s["w_in"], 16)
            for k in range(KC):
                for W, name in ((WG, "gate_projT"), (WU, "up_projT")):
                    sp.dma_start(W[:, k, :], d["L2_ffn_" + name][k * P:(k + 1) * P, :]).then_inc(s["w_in"], 16)
            sp.dma_start(WD[:, :], d["L2_ffn_down_projT"]).then_inc(s["w_in"], 16)

        @block.vector
        def _(dve):
            nv = nc.vector
            chain = Chain(dve, s["chain"])
            dve_ln_all(c, dve, s, chain)
            dve.wait_ge(s["logits_ps"], 1)
            nv.tensor_copy(c.lg[:, :], c.ps[5][:, 0:NT * 8]).then_inc(s["lg_used"], 1)
            dve.wait_ge(s["scores_ok"], 1)
            score, choice, gates = g8(c.lg), g8(c.choice), g8(c.gates)
            chain(nv.tensor_tensor(choice, score, gb[:, :].unsqueeze(1).to_broadcast([P, NT, 8]), ALU.add))
            pairs = c.choice[:, :].rearrange("p (g two) -> p g two", two=2)
            chain(nv.tensor_tensor(gs[:, :], pairs[:, :, 0], pairs[:, :, 1], ALU.add))
            g4 = lambda t: t[:, :].rearrange("p (i g) -> p i g", g=4)
            top2(c, chain, g4(gs), 4, g4(gkeep), g4(gl2), g4(gt), c.m1[:, :])
            chain(nv.tensor_tensor(pairs, pairs, gkeep[:, :].unsqueeze(2).to_broadcast([P, NT * 4, 2]), ALU.mult))
            top2(c, chain, choice, 8, gates, g8(c.lg2), g8(c.lgt), c.m1[:, :])
            chain(nv.tensor_tensor(gates, gates, score, ALU.mult))
            chain(nv.reduce_sum(c.m1[:, :], gates, AX))
            chain(nv.tensor_scalar(c.m1[:, :], c.m1[:, :], 1e-20, None, ALU.add))
            chain(nv.reciprocal(c.m1[:, :], c.m1[:, :]))
            chain(nv.tensor_tensor(gates, gates, bc(c.m1[:, :], 8), ALU.mult))

            def activate(n, b):
                dve.wait_ge(s["sig_ok"], n + 1)
                nv.tensor_tensor(sg[b][:, :], c.ps[b][:, :], sig[b][:, :], ALU.mult).then_inc(s["sg_ok"], 1)
                wait(dve, s["down_ps"], n - 1)
                dve.wait_ge(s["sg_ok"], n + 1)
                nv.tensor_tensor(hid[b][:, :], c.ps[2 + b][:, :], sg[b][:, :], ALU.mult).then_inc(s["hid_ok"], 1)

            def accumulate(n, tile0, e, b):
                dve.wait_ge(s["down_ps"], n + 1)
                wait(dve, s["acc"], n * 4)
                for j in range(4):
                    xj = c.x[:, ds(tile0 * D + j * D, D)]
                    nv.scalar_tensor_tensor(out=xj, in0=c.ps[4 + 2 * b + j // 2][:, (j % 2) * D:(j % 2 + 1) * D],
                                            scalar=c.gates[:, ds(tile0 * 8 + (j * 8 + e), 1)], in1=xj,
                                            op0=ALU.mult, op1=ALU.add).then_inc(s["acc"], 1)

            def chunk(t):
                for e in range(8):
                    activate(t * 8 + e, e % 2)
                    if e:
                        accumulate(t * 8 + (e - 1), t * 4, e - 1, (e - 1) % 2)
                    elif not is_static(t) or t:
                        accumulate(t * 8 - 1, t * 4 - 4, 7, 1)
            chunk(0)
            with dve.Fori(1, CH) as t:
                chunk(t)
            accumulate(8 * CH - 1, 4 * CH - 4, 7, 1)
            dve.wait_ge(s["acc"], 32 * CH)
            with dve.Fori(0, NT) as i:
                nv.bn_stats(bst_of(c, i), xt(c, i))

        @block.scalar
        def _(act):
            na = nc.scalar
            act_ln_all(c, act, s)
            act.wait_ge(s["lg_used"], 1)
            na.activation(c.lg[:, :], c.lg[:, :], ACT.Sigmoid).then_inc(s["scores_ok"], 1)

            def chunk(t):
                for e in range(8):
                    b = e % 2
                    n = t * 8 + e
                    act.wait_ge(s["gu_ps"], n + 1)
                    wait(act, s["sg_ok"], n - 1)
                    na.activation(sig[b][:, :], c.ps[b][:, :], ACT.Sigmoid).then_inc(s["sig_ok"], 1)
            chunk(0)
            with act.Fori(1, CH) as t:
                chunk(t)

        @block.tensor
        def _(pe):
            nt = nc.tensor
            pe_ln_all(c, pe, s)
            pe.wait_ge(s["lnT_ok"], NT)
            pe.wait_ge(s["w_in"], 16 * 7)
            pe_router(c, s, gw)

            def gate_up(n, t, e, b):
                wait(pe, s["hid_ok"], n - 1)
                for W, bank in ((WG, b), (WU, 2 + b)):
                    for k in range(KC):
                        last = nt.matmul(c.ps[bank][:, :], W[:, k, e * P:(e + 1) * P],
                                         c.lnT_all[:, k, ds(t * 512, 512)], start=(k == 0), stop=(k == KC - 1))
                last.then_inc(s["gu_ps"], 1)

            def down(n, e, b):
                pe.wait_ge(s["hid_ok"], n + 1)
                wait(pe, s["acc"], n * 4 - 4)
                for j in range(4):
                    last = nt.matmul(c.ps[4 + 2 * b + j // 2][:, (j % 2) * D:(j % 2 + 1) * D],
                                     hid[b][:, j * P:(j + 1) * P], WD[:, e * D:(e + 1) * D], start=True, stop=True)
                last.then_inc(s["down_ps"], 1)
            pe.wait_ge(s["lg_used"], 1)

            def chunk(t):
                for e in range(8):
                    gate_up(t * 8 + e, t, e, e % 2)
                    if e:
                        down(t * 8 + (e - 1), e - 1, (e - 1) % 2)
                    elif not is_static(t) or t:
                        down(t * 8 - 1, 7, 1)
            chunk(0)
            with pe.Fori(1, CH) as t:
                chunk(t)
            down(8 * CH - 1, 7, 1)


HB, DH, G = 16, 64, 4
HPG = HB // G
NB = -(-HB * SK // P)
LASTB = HB * SK - (NB - 1) * P


def pipeline4(eng, step, first, lo, hi, last):
    for t in range(first, lo):
        step(t, t % 4)
    with eng.Fori(0, (hi - lo) // 4) as j:
        for u in range(4):
            step(j * 4 + (lo + u), (lo + u) % 4)
    for t in range(hi, last):
        step(t, t % 4)


def attn_gqa(c, d):
    nc = c.nc
    Wq, Wk = sb(c, "g_Wq", [P, KC, HB * DH]), sb(c, "g_Wk", [P, KC, G * DH])
    Wv = sb(c, "g_Wv", [P, KC, G, 2, DH])
    Wo = sb(c, "g_Wo", [P, HB // 2, D])
    C, Sn = sb(c, "g_cos", [P, S // P, DH]), sb(c, "g_sin", [P, S // P, DH])
    mraw = sb(c, "g_mraw", [1, 40], I32)
    mrow = sb(c, "g_mrow", [1, B * SK])
    mtile = sb(c, "g_mtile", [1, B, HPB, SK], BF16)
    ones = sb(c, "g_ones", [1, P], BF16)
    KR = sb(c, "g_KR", [SK, B, G, 2, DH])
    KB = sb(c, "g_KB", [P, B, G, 2, SK])
    VT = sb(c, "g_VT", [P, G, B * SK])
    VW = sb(c, "g_VW", [P, B, NB, D])
    bias = [sb(c, f"g_bias{j}", [P, HB * SK]) for j in range(2)]
    t1, t2, qr = (sb(c, "g_" + n, [P, HB * DH]) for n in ("t1", "t2", "qr"))
    qT = [sb(c, f"g_qT{b}", [P, HB * DH]) for b in range(2)]
    rden = [sb(c, f"g_rden{b}", [P, HB]) for b in range(2)]
    VWs = [c.lnk[0:SK, :].rearrange("k (h n) -> k h n", h=HB),
           c.lnT_all[0:SK, :, :].rearrange("k a (h n) -> k (a h) n", n=D)]
    vw_dram = nc.dram_tensor("vw_scratch", (B, HB * SK, D), F32, kind="Internal").ap()
    s = sems(c, "g_", *NORM, "w_in", "k_ps", "vT_ps", "kr_chain", "kr_ok", "krT_ps", "kb_ok", "vT_ok", "vw_ps",
             "vwa_ok", "vwd_ok", "vw_out", "vw_in", "m_ok", "q_ps", "roped", "rope_ok", "qT_ps", "qT_ok", "s_ps",
             "s_used", "shifted", "exp_ok", "rd_ok", "p_ok", "pT_ps", "pT_ok", "y_ps", "x_ok", "bias0_in", "bias1_in", "links")
    bias_in = [s["bias0_in"], s["bias1_in"]]
    sview = c.psall[:, 0:3 * 512].rearrange("p (b n) -> p b n", b=3)
    qview = c.psall[:, 3 * 512:5 * 512].rearrange("p (h e) -> p h e", e=DH)
    ring = [c.ps[5], c.ps[6]]
    bank_y = c.ps[7]
    n_w = 11
    heads = lambda t: t[:, 0:HB * SK].rearrange("p (h k) -> p h k", k=SK)
    jof = lambda i, b, n: (i // 2) * n if is_static(i) else i * (n // 2) - b * (n // 2)

    with nc.Block() as block:
        @block.sync
        def _(sp):
            sp.dma_start(Wk[:, :, :], d["L3_xattn_Wk"].rearrange("(k p) n -> p k n", p=P)).then_inc(s["w_in"], 16)
            wv = d["L3_xattn_Wv"].rearrange("(k p) (g e) -> p k g e", p=P, g=G)
            for k in range(KC):
                for r in range(2):
                    sp.dma_start(Wv[:, k, :, r, :], wv[:, k, :, :]).then_inc(s["w_in"], 16)
            sp.dma_start(Wo[:, :, :], d["L3_xattn_Wo"].rearrange("(m p) n -> p m n", p=P)).then_inc(s["w_in"], 16)
            for k in range(KC):
                sp.dma_start(Wq[:, k, :], d["L3_xattn_Wq"][k * P:(k + 1) * P, :]).then_inc(s["w_in"], 16)
            sp.dma_start(C[:, :, :], d["c_cos"].rearrange("(j p) e -> p j e", p=P)).then_inc(s["w_in"], 16)
            sp.dma_start(Sn[:, :, :], d["c_sin"].rearrange("(j p) e -> p j e", p=P)).then_inc(s["w_in"], 16)
            sp.dma_start(mraw[:, :], d["mask3"]).then_inc(s["w_in"], 16)
            for j in range(2):
                sp.dma_start(bias[j][:, :], d["rel_bias"][j * P:(j + 1) * P, :]).then_inc(bias_in[j % 2], 16)
            for b in range(B):
                sp.wait_ge(s["vwa_ok"], 4 * (b + 1))
                sp.wait_ge(s["vwd_ok"], 4 * (b + 1))
                sp.dma_start(vw_dram[b].rearrange("(h k) n -> k h n", k=SK), VWs[b]).then_inc(s["vw_out"], 16)
            for b in range(B):
                sp.wait_ge(s["vw_out"], 16 * B)
                sp.dma_start(VW[:, b, 0:NB - 1, :], vw_dram[b, 0:(NB - 1) * P, :].rearrange("(j p) n -> p j n", p=P)
                             ).then_inc(s["vw_in"], 16)
                sp.dma_start(VW[0:LASTB, b, NB - 1, :], vw_dram[b, (NB - 1) * P:HB * SK, :]).then_inc(s["vw_in"], 16)
            for j in range(2, S // P):
                sp.wait_ge(s["s_used"], 2 * j - 2)
                sp.dma_start(bias[j % 2][:, :], d["rel_bias"][j * P:(j + 1) * P, :]).then_inc(bias_in[j % 2], 16)

        @block.gpsimd
        def _(pool):
            ng = nc.gpsimd

            def step(t, q):
                b = q % 2
                if inside(t + 1):
                    i = t + 1
                    pool.wait_ge(s["roped"], i + 1)
                    wait(pool, s["qT_ps"], i * 2)
                    ng.tensor_tensor(qr[:, :], t1[:, :], t2[:, :], ALU.add).then_inc(s["rope_ok"], 1)
                if inside(t):
                    pool.wait_ge(s["rd_ok"], t + 1)
                    ng.tensor_tensor(heads(c.prob[b]), heads(c.prob[b]),
                                     rden[b][:, :].unsqueeze(2).to_broadcast([P, HB, SK]), ALU.mult).then_inc(s["p_ok"], 1)
            pipeline4(pool, step, -1, 2, NT - 2, NT)

        @block.vector
        def _(dve):
            nv = nc.vector
            chain = Chain(dve, s["chain"])
            kr = Chain(dve, s["kr_chain"])
            dve_rstd(c, dve, chain, s["ve_ok"], s["std_ok"])

            def layer_norm(i, b):
                wait(dve, s["lnT_ps"], i - 1)
                nv.tensor_scalar(c.ln[b][:, :], xt(c, i), mean_of(c, i), rstd_of(c, i),
                                 ALU.subtract, ALU.mult).then_inc(s["ln_ok"], 1)
            layer_norm(0, 0)
            dve.wait_ge(s["w_in"], 16 * n_w)
            kr(nv.tensor_scalar(mrow[:, :], mraw[:, :].bitcast(U8)[:, 0:B * SK], 0.0, NEG, ALU.is_equal, ALU.mult))
            nv.tensor_copy(mtile[:, :, :, :], mrow[:, :].rearrange("a (b k) -> a b k", b=B).unsqueeze(2)
                           .to_broadcast([1, B, HPB, SK]))
            nv.memset(ones[:, :], 1.0).then_inc(s["m_ok"], 1)
            dve.wait_ge(s["k_ps"], 1)
            half = DH // 2
            for b in range(B):
                k = c.ps[b][0:SK, 0:G * DH].rearrange("k (g e) -> k g e", g=G)
                a1 = t1[0:SK, b * 256:b * 256 + 256].rearrange("k (g e) -> k g e", g=G)
                a2 = t2[0:SK, b * 256:b * 256 + 256].rearrange("k (g e) -> k g e", g=G)
                bcg = lambda ap: ap.unsqueeze(1).to_broadcast([SK, G, ap.shape[-1]])
                nv.tensor_tensor(a1, k, bcg(C[0:SK, 0, :]), ALU.mult)
                nv.tensor_tensor(a2[:, :, 0:half], k[:, :, half:DH], bcg(Sn[0:SK, 0, 0:half]), ALU.mult)
                kr(nv.tensor_tensor(a2[:, :, half:DH], k[:, :, 0:half], bcg(Sn[0:SK, 0, half:DH]), ALU.mult))
                for r in range(2):
                    nv.tensor_tensor(KR[:, b, :, r, :], a1, a2, ALU.add).then_inc(s["kr_ok"], 1)
            for b in range(B):
                dve.wait_ge(s["krT_ps"], b + 1)
                for g in range(G):
                    for r in range(2):
                        last = nv.tensor_scalar(KB[:, b, g, r, :], c.ps[6 + b][:, g * SK:(g + 1) * SK],
                                                c.hmask2[:, r:r + 1], DH ** -0.5, ALU.mult, ALU.mult)
                last.then_inc(s["kb_ok"], 1)
            for n in range(8):
                dve.wait_ge(s["vw_ps"], n + 1)
                h = 4 * (n % 4) + 1
                nv.tensor_copy(VWs[n // 4][:, h:h + 3:2, :],
                               c.ps[2 * (n % 2) + 1][0:SK, :].rearrange("k (a n) -> k a n", a=2)).then_inc(s["vwd_ok"], 1)

            def rope(i, b):
                dve.wait_ge(s["q_ps"], i + 1)
                wait(dve, s["rope_ok"], i)
                cs = C[:, :, :].rearrange("p j e -> p (j e)")
                sn = Sn[:, :, :].rearrange("p j e -> p (j e)")
                o = jof(i, b, DH)
                a1, a2 = (t[:, :].rearrange("p (h e) -> p h e", e=DH) for t in (t1, t2))
                bch = lambda ap: ap.unsqueeze(1).to_broadcast([P, HB, ap.shape[-1]])
                nv.tensor_tensor(a1, qview, bch(cs[:, ds(o, DH)]), ALU.mult)
                nv.tensor_tensor(a2[:, :, 0:half], qview[:, :, half:DH], bch(sn[:, ds(o, half)]), ALU.mult)
                nv.tensor_tensor(a2[:, :, half:DH], qview[:, :, 0:half], bch(sn[:, ds(o + half, half)]),
                                 ALU.mult).then_inc(s["roped"], 1)

            links = Chain(dve, s["links"])

            def shift(t, q):
                b, jb = q % 2, (q // 2) % 2
                p = heads(c.prob[b])
                dve.wait_ge(s["s_ps"], t + 1)
                dve.wait_ge(bias_in[jb], 16 * (t // 4 + 1) if is_static(t) else t * 4 + (16 - 4 * q))
                wait(dve, s["pT_ps"], t * 3 - 3)
                n = HPB * SK
                nv.tensor_tensor(c.prob[b][:, 0:2 * n].rearrange("p (q n) -> p q n", q=2), sview[:, 0:2, 0:n],
                                 bias[jb][:, 0:2 * n].rearrange("p (q n) -> p q n", q=2), ALU.add)
                nv.tensor_tensor(c.prob[b][:, 2 * n:HB * SK], sview[:, 2, 0:4 * SK], bias[jb][:, 2 * n:HB * SK],
                                 ALU.add).then_inc(s["s_used"], 1)
                dve.wait_ge(s["s_used"], t + 1)
                links(nv.reduce_max(c.mx[:, :], p, AX))
                nv.tensor_tensor(p, p, c.mx[:, :].unsqueeze(2).to_broadcast([P, HB, SK]),
                                 ALU.subtract).then_inc(s["shifted"], 1)

            def residual(i, b):
                dve.wait_ge(s["y_ps"], i + 1)
                nv.tensor_tensor(xt(c, i), xt(c, i), bank_y[:, 0:D], ALU.add).then_inc(s["x_ok"], 1)

            def sums(t, b):
                dve.wait_ge(s["exp_ok"], t + 1)
                wait(dve, s["p_ok"], t - 1)
                links(nv.reduce_sum(c.den[:, :], heads(c.prob[b]), AX))
                nv.reciprocal(rden[b][:, :], c.den[:, :]).then_inc(s["rd_ok"], 1)

            layer_norm(1, 1)

            def step(t, q):
                b = q % 2
                links.at(2 * max(0, min(t, NT)) if is_static(t) else t * 2)
                if inside(t + 1):
                    rope(t + 1, 1 - b)
                if inside(t):
                    shift(t, q)
                if inside(t - 1):
                    residual(t - 1, 1 - b)
                    dve.wait_ge(s["x_ok"], t)
                if inside(t + 3):
                    layer_norm(t + 3, 1 - b)
                if inside(t - 1):
                    nv.tensor_copy(c.gap[:, b:b + 1], c.ones[:, 0:1])
                    nv.bn_stats(bst_of(c, t - 1), xt(c, t - 1))
                if inside(t):
                    sums(t, b)
            pipeline4(dve, step, -1, 1, NT - 3, NT + 1)

        @block.scalar
        def _(act):
            na = nc.scalar
            act_std(c, act, s["ve_ok"], s["std_ok"])
            act.wait_ge(s["vT_ps"], 1)
            for g in range(G):
                last = na.activation(VT[:, g, :], c.ps[2 + g][:, 0:B * SK], ACT.Copy)
            last.then_inc(s["vT_ok"], 1)
            for n in range(8):
                act.wait_ge(s["vw_ps"], n + 1)
                h = 4 * (n % 4)
                na.activation(VWs[n // 4][:, h:h + 3:2, :],
                              c.ps[2 * (n % 2)][0:SK, :].rearrange("k (a n) -> k a n", a=2),
                              ACT.Copy).then_inc(s["vwa_ok"], 1)

            def lnT_copy(i, b):
                act.wait_ge(s["lnT_ps"], i + 1)
                wait(act, s["q_ps"], i - 1)
                na.activation(c.lnT[b][:, :], ring[1][:, 0:D], ACT.Copy).then_inc(s["lnT_ok"], 1)

            def qT_copy(i, b):
                wait(act, s["s_ps"], i - 1)
                for u in range(2):
                    act.wait_ge(s["qT_ps"], i * 2 + (u + 1))
                    na.activation(qT[b][:, u * 512:(u + 1) * 512], ring[u][:, :], ACT.Copy).then_inc(s["qT_ok"], 1)

            def exps(t, b):
                act.wait_ge(s["shifted"], t + 1)
                na.activation(c.prob[b][:, :], c.prob[b][:, :], ACT.Exp).then_inc(s["exp_ok"], 1)

            def pT_copy(i, b):
                wait(act, s["y_ps"], i - 1)
                for u in range(3):
                    act.wait_ge(s["pT_ps"], i * 3 + (u + 1))
                    if u < 2:
                        ins = na.activation(c.pT[b][:, u * 512:(u + 1) * 512], ring[u][:, :], ACT.Copy)
                    else:
                        na.activation(c.pT[b][:, 8 * P:9 * P], ring[0][:, 0:P], ACT.Copy)
                        ins = na.activation(c.pT[b][0:LASTB, 9 * P:10 * P], ring[0][0:LASTB, P:2 * P], ACT.Copy)
                    ins.then_inc(s["pT_ok"], 1)

            def step(t, q):
                b = q % 2
                if inside(t - 1):
                    pT_copy(t - 1, 1 - b)
                if inside(t + 2):
                    lnT_copy(t + 2, b)
                if inside(t):
                    exps(t, b)
                if inside(t + 1):
                    qT_copy(t + 1, 1 - b)
            pipeline4(act, step, -2, 2, NT - 2, NT + 1)

        @block.tensor
        def _(pe):
            nt = nc.tensor
            pe.wait_ge(s["w_in"], 16 * n_w)
            for b in range(B):
                for k in range(KC):
                    last = nt.matmul(c.ps[b][0:SK, 0:G * DH], c.ctxT[:, k, b * SK:(b + 1) * SK], Wk[:, k, :],
                                     start=(k == 0), stop=(k == KC - 1))
            last.then_inc(s["k_ps"], 1)
            for g in range(G):
                for k in range(KC):
                    last = nt.matmul(c.ps[2 + g][:, 0:B * SK], Wv[:, k, g, :, :].rearrange("p r e -> p (r e)"),
                                     c.ctxT[:, k, :], start=(k == 0), stop=(k == KC - 1))
            last.then_inc(s["vT_ps"], 1)
            for b in range(B):
                pe.wait_ge(s["kr_ok"], 2 * (b + 1))
                for g in range(G):
                    last = nt.transpose(c.ps[6 + b][:, g * SK:(g + 1) * SK],
                                        KR[:, b, g, :, :].rearrange("k r e -> k (r e)"), c.ident[0:SK, 0:SK])
                last.then_inc(s["krT_ps"], 1)
            pe.wait_ge(s["vT_ok"], 1)
            for n in range(8):
                b, m = n // 4, n % 4
                wait(pe, s["vwa_ok"], n - 1)
                wait(pe, s["vwd_ok"], n - 1)
                for a in range(2):
                    for r in range(2):
                        h = 4 * m + 2 * a + r
                        rows = slice(r * DH, (r + 1) * DH)
                        last = nt.matmul(c.ps[2 * (n % 2) + r][0:SK, a * D:(a + 1) * D],
                                         VT[rows, h // HPG, b * SK:(b + 1) * SK], Wo[rows, h // 2, :],
                                         start=True, stop=True)
                last.then_inc(s["vw_ps"], 1)

            def lnT(i, b):
                pe.wait_ge(s["ln_ok"], i + 1)
                wait(pe, s["pT_ok"], i * 3 - 7)
                for k in range(KC):
                    last = nt.transpose(ring[1][:, k * P:(k + 1) * P], c.ln[b][:, k * P:(k + 1) * P], c.ident[:, :])
                last.then_inc(s["lnT_ps"], 1)

            def queries(i, b):
                pe.wait_ge(s["lnT_ok"], i + 1)
                wait(pe, s["roped"], i)
                for u in range(2):
                    for k in range(KC):
                        last = nt.matmul(c.ps[3 + u][:, :], c.lnT[b][:, k * P:(k + 1) * P],
                                         Wq[:, k, u * 512:(u + 1) * 512], start=(k == 0), stop=(k == KC - 1))
                last.then_inc(s["q_ps"], 1)

            def q_transpose(i, b):
                pe.wait_ge(s["rope_ok"], i + 1)
                for u in range(2):
                    if u == 0:
                        wait(pe, s["pT_ok"], i * 3 - 3)
                    else:
                        pe.wait_ge(s["lnT_ok"], min(i + 2, NT) if is_static(i) else i + 2)
                    for m in range(4):
                        last = nt.transpose(ring[u][:, m * P:(m + 1) * P], qr[:, (4 * u + m) * P:(4 * u + m + 1) * P],
                                            c.ident[:, :])
                    last.then_inc(s["qT_ps"], 1)

            def scores(t, b):
                pe.wait_ge(s["qT_ok"], t * 2 + 2)
                wait(pe, s["s_used"], t)
                for m in range(HB // 2):
                    o = (m % 3) * 2 * SK
                    nt.matmul(sview[:, m // 3, o:o + 2 * SK], qT[b][:, m * P:(m + 1) * P],
                              KB[:, b, m // 2, :, :].rearrange("p r k -> p (r k)"),
                              start=(m % 3 == 0), stop=False, skip_group_check=True)
                for q in range(3):
                    nh = HPB if q < 2 else 4
                    last = nt.matmul(sview[:, q, 0:nh * SK], ones[:, :],
                                     mtile[:, b, 0:nh, :].rearrange("a h k -> a (h k)"),
                                     start=False, stop=True, skip_group_check=True)
                last.then_inc(s["s_ps"], 1)

            def prob_transpose(i, b):
                pe.wait_ge(s["p_ok"], i + 1)
                for u in range(3):
                    if u < 2:
                        pe.wait_ge(s["qT_ok"], min(i * 2 + 3 + u, 2 * NT) if is_static(i) else i * 2 + (3 + u))
                    else:
                        pe.wait_ge(s["pT_ok"], i * 3 + 1)
                    for j in range(4 * u, min(4 * u + 4, NB)):
                        w = P if j < NB - 1 else LASTB
                        last = nt.transpose(ring[u % 2][0:w, (j % 4) * P:(j % 4 + 1) * P],
                                            c.prob[b][:, j * P:j * P + w], c.ident[:, :])
                    last.then_inc(s["pT_ps"], 1)

            def output(i, b):
                pe.wait_ge(s["pT_ok"], i * 3 + 3)
                wait(pe, s["x_ok"], i)
                for j in range(NB):
                    w = P if j < NB - 1 else LASTB
                    last = nt.matmul(bank_y[:, 0:D], c.pT[b][0:w, j * P:(j + 1) * P], VW[0:w, b, j, :],
                                     start=(j == 0), stop=(j == NB - 1))
                last.then_inc(s["y_ps"], 1)
            pe.wait_ge(s["kb_ok"], B)
            pe.wait_ge(s["m_ok"], 1)
            pe.wait_ge(s["vwa_ok"], 8)
            pe.wait_ge(s["vwd_ok"], 8)
            loaded = [False]

            def step(t, q):
                b = q % 2
                if inside(t):
                    scores(t, b)
                if inside(t - 1):
                    if not loaded[0]:
                        loaded[0] = True
                        pe.wait_ge(s["vw_in"], 64)
                    prob_transpose(t - 1, 1 - b)
                if inside(t + 2):
                    lnT(t + 2, b)
                if inside(t - 1):
                    output(t - 1, 1 - b)
                if inside(t + 1):
                    q_transpose(t + 1, 1 - b)
                if inside(t + 2):
                    queries(t + 2, b)
            pipeline4(pe, step, -2, 2, NT - 2, NT + 1)


E3, CAP, HF = 8, 320, 1024
OVB = -(-(T - CAP) // P)
XR = [(0, P), (P, P), (2 * P, CAP - 2 * P)]
MH = HF // P


def moe3(c, d):
    nc = c.nc
    rw, rb = sb(c, "x_rw", [P, KC, 8]), sb(c, "x_rb", [P, 8])
    ohb = sb(c, "x_ohb", [P, NT * 8], BF16)
    upper, onesb = sb(c, "x_upper", [P, P], BF16), sb(c, "x_onesb", [P, P], BF16)
    upf = sb(c, "x_upf", [P, P])
    base, rank8 = sb(c, "x_base", [P, NT * 8]), sb(c, "x_rank8", [P, NT * 8])
    rank, valid, over, slotf, obase = (sb(c, "x_" + n, [P, NT]) for n in ("rank", "valid", "over", "slotf", "obase"))
    overb = sb(c, "x_overb", [P, NT], BF16)
    slot = sb(c, "x_slot", [P, NT], U32)
    steps_, nbf = sb(c, "x_steps", [1, OVB]), sb(c, "x_nbf", [1, 2])
    nbi = sb(c, "x_nbi", [1, 1], I32)
    w1 = [sb(c, f"x_w1{b}", [P, KC, HF]) for b in range(2)]
    w2 = [sb(c, f"x_w2{b}", [P, MH, D]) for b in range(2)]
    ow1, ow2 = sb(c, "x_ow1", [P, KC, HF]), sb(c, "x_ow2", [P, MH, D])
    b1, ob1 = sb(c, "x_b1", [P, E3 * MH]), sb(c, "x_ob1", [P, MH])
    b2, ob2 = sb(c, "x_b2", [P, E3 * D]), sb(c, "x_ob2", [P, D])
    X = [sb(c, f"x_X{b}", [P, 3, D]) for b in range(2)]
    xT = [sb(c, f"x_xT{b}", [P, KC, CAP]) for b in range(2)]
    hT = [c.prob_pair[b][:, 0:MH * CAP].rearrange("p (m n) -> p m n", m=MH) for b in range(2)]
    yt = [sb(c, f"x_yt{b}", [P, 3, D]) for b in range(2)]
    Xo, xTo, yo = sb(c, "x_Xo", [P, D]), sb(c, "x_xTo", [P, D]), sb(c, "x_yo", [P, D])
    pgap = sb(c, "x_pgap", [P, 1])
    hTo = sb(c, "x_hTo", [P, MH, P])
    xd, yd = c.xd, c.yd
    s = sems(c, "x_", *NORM, "w_in", "ow_in", "w1a_in", "w1b_in", "w2a_in", "w2b_in", "xa_in", "xb_in",
             "logits_ps", "oh_ok", "pre_ps", "over_ok", "opre_ps", "slot_ok", "kept", "scat",
             "xT_ps", "xT_ok", "h_ps", "h_ok", "y_ps", "y_ok", "ya_out", "yb_out",
             "oX_in", "oT_ps", "oT_ok", "oh_ps", "ohid_ok", "oy_ps", "oy_ok", "o_out",
             "g0_in", "g1_in", "g2_in", "g3_in", "sum_ok", "out_done")
    w1_in, w2_in, x_in = [s["w1a_in"], s["w1b_in"]], [s["w2a_in"], s["w2b_in"]], [s["xa_in"], s["xb_in"]]
    y_out, g_in = [s["ya_out"], s["yb_out"]], [s["g0_in"], s["g1_in"], s["g2_in"], s["g3_in"]]
    OV0 = E3 * CAP
    order = [2 * q + b for b in range(B) for q in range(NT // B)]
    turns = lambda e: e // 2 if is_static(e) else e

    def count16(e, b, per):
        return 16 * per * (e // 2 + 1) if is_static(e) else e * (8 * per) + (16 * per - 8 * per * b)

    with nc.Block() as block:
        @block.sync
        def _(sp):
            sp.dma_start(rw[:, :, :], d["L3_ffn_router_w"].rearrange("(k p) e -> p k e", p=P)).then_inc(s["w_in"], 16)
            sp.dma_start(rb[:, :], d["L3_ffn_router_b"].partition_broadcast(P)).then_inc(s["w_in"], 16)
            sp.dma_start(upf[:, :], d["c_upper"]).then_inc(s["w_in"], 16)
            sp.dma_start(steps_[:, :], d["c_steps"]).then_inc(s["w_in"], 16)
            sp.dma_start(b1[:, :], d["L3_ffn_b1T"]).then_inc(s["w_in"], 16)
            sp.dma_start(ob1[:, :], d["L3_ffn_ob1T"]).then_inc(s["w_in"], 16)
            sp.dma_start(b2[:, :], d["L3_ffn_b2"].rearrange("e n -> (e n)").partition_broadcast(P)).then_inc(s["w_in"], 16)
            sp.dma_start(ob2[:, :], d["L3_ffn_ob2"].partition_broadcast(P)).then_inc(s["w_in"], 16)

            def load_w1(e, b):
                for k in range(KC):
                    sp.dma_start(w1[b][:, k, :], d["L3_ffn_w1"][ds(e * D + k * P, P), :]).then_inc(w1_in[b], 16)

            def load_w2(e, b):
                sp.dma_start(w2[b][:, :, :], d["L3_ffn_w2"][ds(e * HF, HF), :].rearrange("(m p) n -> p m n", p=P)
                             ).then_inc(w2_in[b], 16)

            def load_x(e, b):
                sp.dma_start(X[b][:, 0:2, :], xd[ds(e * CAP, 2 * P), :].rearrange("(r p) n -> p r n", p=P)
                             ).then_inc(x_in[b], 16)
                sp.dma_start(X[b][0:CAP - 2 * P, 2, :], xd[ds(e * CAP + 2 * P, CAP - 2 * P), :]).then_inc(x_in[b], 16)
            for e in range(2):
                load_w1(e, e)
                load_w2(e, e)
            for k in range(KC):
                sp.dma_start(ow1[:, k, :], d["L3_ffn_ow1"][k * P:(k + 1) * P, :]).then_inc(s["ow_in"], 16)
            sp.dma_start(ow2[:, :, :], d["L3_ffn_ow2"].rearrange("(m p) n -> p m n", p=P)).then_inc(s["ow_in"], 16)
            sp.wait_ge(s["scat"], 16 * NT)
            for e in range(2):
                load_x(e, e)

            def store_y(e, b):
                for r, (r0, n) in enumerate(XR):
                    sp.wait_ge(s["y_ok"], e * 3 + (r + 1))
                    sp.dma_start(yd[ds(e * CAP + r0, n), :], yt[b][0:n, r, :]).then_inc(y_out[b], 16)

            def step(e, b):
                if not is_static(e) or e + 2 < E3:
                    sp.wait_ge(s["xT_ps"], e + 1)
                    load_x(e + 2, b)
                    sp.wait_ge(s["h_ps"], e * 8 + 8)
                    load_w1(e + 2, b)
                store_y(e, b)
                if not is_static(e) or e + 2 < E3:
                    sp.wait_ge(s["y_ps"], e * 3 + 3)
                    load_w2(e + 2, b)
            pipeline(sp, step, 0, 0, E3 - 2, E3)

            def load_over(n):
                sp.dma_start(Xo[:, :], xd[ds(n * P + OV0, P), :]).then_inc(s["oX_in"], 16)

            def store_over(n):
                sp.wait_ge(s["oy_ok"], n + 1)
                sp.dma_start(yd[ds(n * P + OV0, P), :], yo[:, :]).then_inc(s["o_out"], 16)
            load_over(0)
            sp.wait_ge(s["slot_ok"], 1)
            nb = sp.value_load(nbi[0:1, 0:1], min_val=2, max_val=OVB)
            with sp.Fori(1, nb) as n:
                sp.wait_ge(s["oT_ps"], n)
                load_over(n)
                store_over(n - 1)
            sp.wait_ge(s["oy_ok"], nb)
            sp.dma_start(yd[ds(nb * P + (OV0 - P), P), :], yo[:, :]).then_inc(s["o_out"], 16)
            xo = c.x[:, :].rearrange("p (q b n) -> p q b n", b=B, n=D)
            for g in range(4):
                sp.wait_ge(s["sum_ok"], g + 1)
                for b in range(B):
                    sp.dma_start(d["out"][b, 2 * g * P:(2 * g + 2) * P, :].rearrange("(q p) n -> p q n", p=P),
                                 xo[:, 2 * g:2 * g + 2, b, :]).then_inc(s["out_done"], 16)
            sp.wait_ge(s["out_done"], 16 * 8)

        @block.gpsimd
        def _(pool):
            ng = nc.gpsimd

            def keep(i, b):
                pool.wait_ge(s["ln_ok"], i + 1)
                ng.tensor_copy(c.lnk[:, ds(i * D, D)], c.ln[b][:, :]).then_inc(s["kept"], 1)
            pipeline(pool, keep, 0, 0, NT, NT)
            pool.wait_ge(s["slot_ok"], 1)
            pool.wait_ge(s["kept"], NT)
            for i in range(NT):
                ng.indirect_dma_start(out=xd, out_offset=bass.IndirectOffsetOnAxis(ap=slot[:, i:i + 1], axis=0),
                                      in_=c.lnk[:, i * D:(i + 1) * D], in_offset=None).then_inc(s["scat"], 16)
            nb = pool.value_load(nbi[0:1, 0:1], min_val=2, max_val=OVB)
            for b in range(2):
                pool.wait_ge(y_out[b], 16 * 3 * E3 // 2)
            pool.wait_ge(s["o_out"], nb * 16)
            ng.tensor_tensor(pgap[:, :], rb[:, 0:1], rb[:, 0:1], ALU.add)
            for i in range(NT):
                ng.indirect_dma_start(out=c.lnk[:, i * D:(i + 1) * D], out_offset=None, in_=yd,
                                      in_offset=bass.IndirectOffsetOnAxis(ap=slot[:, i:i + 1], axis=0)
                                      ).then_inc(g_in[i // 4], 16)

        @block.vector
        def _(dve):
            nv = nc.vector
            chain = Chain(dve, s["chain"])
            dve_rstd(c, dve, chain, s["ve_ok"], s["std_ok"])

            def norm(i, b):
                wait(dve, s["lnT_ps"], i - 1)
                wait(dve, s["kept"], i - 1)
                nv.tensor_scalar(c.ln[b][:, :], xt(c, i), mean_of(c, i), rstd_of(c, i),
                                 ALU.subtract, ALU.mult).then_inc(s["ln_ok"], 1)
            pipeline(dve, norm, 0, 2, NT, NT)
            dve.wait_ge(s["w_in"], 16 * 8)
            nv.tensor_copy(upper[:, :], upf[:, :])
            nv.tensor_copy(onesb[:, :], c.ones[:, :])
            l, oh = g8(c.lg), g8(c.gates)
            dve.wait_ge(s["logits_ps"], 1)
            chain(nv.tensor_tensor(l, g8(c.ps[5][:, 0:NT * 8]), rb[:, :].unsqueeze(1).to_broadcast([P, NT, 8]), ALU.add))
            top1(c, chain, l, 8, oh, g8(c.lgt), c.m1[:, :])
            nv.tensor_copy(ohb[:, :], c.gates[:, :]).then_inc(s["oh_ok"], 1)
            dve.wait_ge(s["pre_ps"], 1)
            tot = g8(c.lg2)
            nv.tensor_copy(c.lg2[:, :], c.ps[1][:, 0:NT * 8])
            chain(nv.memset(base[:, 0:8], 0.0))
            for prev, i in zip(order, order[1:]):
                chain(nv.tensor_tensor(base[:, i * 8:(i + 1) * 8], base[:, prev * 8:(prev + 1) * 8], tot[:, prev, :],
                                       ALU.add))
            chain(nv.tensor_tensor(rank8[:, :], c.ps[0][:, 0:NT * 8], base[:, :], ALU.add))
            chain(nv.tensor_tensor(rank8[:, :], rank8[:, :], c.gates[:, :], ALU.mult))
            chain(nv.reduce_sum(rank[:, :], g8(rank8), AX))
            nv.tensor_scalar(valid[:, :], rank[:, :], float(CAP), None, ALU.is_lt)
            chain(nv.tensor_scalar(over[:, :], rank[:, :], float(CAP), None, ALU.is_ge))
            nv.tensor_copy(overb[:, :], over[:, :]).then_inc(s["over_ok"], 1)
            chain(nv.tensor_scalar(slotf[:, :], c.first[:, :], -float(CAP), float(E3 * CAP), ALU.mult, ALU.add))
            chain(nv.tensor_tensor(slotf[:, :], slotf[:, :], rank[:, :], ALU.add))
            chain(nv.tensor_tensor(slotf[:, :], slotf[:, :], valid[:, :], ALU.mult))
            dve.wait_ge(s["opre_ps"], 1)
            nv.tensor_copy(c.m2[:, :], c.ps[3][:, 0:NT])
            chain(nv.memset(obase[:, 0:1], float(OV0)))
            for prev, i in zip(order, order[1:]):
                chain(nv.tensor_tensor(obase[:, i:i + 1], obase[:, prev:prev + 1], c.m2[:, prev:prev + 1], ALU.add))
            chain(nv.tensor_tensor(nbf[:, 0:1], obase[0:1, NT - 1:NT], c.m2[0:1, NT - 1:NT], ALU.add))
            chain(nv.tensor_scalar(steps_[:, :], steps_[:, :], nbf[:, 0:1], None, ALU.is_lt))
            chain(nv.reduce_sum(nbf[:, 1:2], steps_[:, :], AX))
            nv.tensor_scalar(nbi[:, :], nbf[:, 1:2], 2.0, None, ALU.max)
            chain(nv.tensor_tensor(obase[:, :], c.ps[2][:, 0:NT], obase[:, :], ALU.add))
            chain(nv.tensor_tensor(obase[:, :], obase[:, :], over[:, :], ALU.mult))
            nv.tensor_tensor(slot[:, :], slotf[:, :], obase[:, :], ALU.add).then_inc(s["slot_ok"], 1)

            def x_copy(e, b):
                dve.wait_ge(s["xT_ps"], e + 1)
                for k in range(KC):
                    last = nv.tensor_copy(xT[b][:, k, :], c.ps[k][:, 0:CAP])
                last.then_inc(s["xT_ok"], 1)

            def y_bias(e, b):
                wait(dve, y_out[b], count16(e, b, 3) - 48)
                for r, (r0, n) in enumerate(XR):
                    dve.wait_ge(s["y_ps"], e * 3 + (r + 1))
                    nv.tensor_tensor(yt[b][0:n, r, :], c.ps[6 + (3 * b + r) % 2][0:n, 0:D], b2[0:n, ds(e * D, D)],
                                     ALU.add).then_inc(s["y_ok"], 1)
            x_copy(0, 0)

            def step(e, b):
                if not is_static(e) or e + 1 < E3:
                    x_copy(e + 1, 1 - b)
                y_bias(e, b)
            pipeline(dve, step, 0, 2, E3 - 2, E3)

            def over_block(n):
                dve.wait_ge(s["oT_ps"], n + 1)
                nv.tensor_copy(xTo[:, :], c.ps[0][:, 0:D]).then_inc(s["oT_ok"], 1)
                dve.wait_ge(s["oy_ps"], n + 1)
                wait(dve, s["o_out"], n * 16)
                nv.tensor_tensor(yo[:, :], c.ps[6][:, 0:D], ob2[:, :], ALU.add).then_inc(s["oy_ok"], 1)
            over_block(0)
            nb = dve.value_load(nbi[0:1, 0:1], min_val=2, max_val=OVB)
            with dve.Fori(1, nb) as n:
                over_block(n)
            for g in range(4):
                dve.wait_ge(g_in[g], 64)
                sl = slice(4 * g * D, (4 * g + 4) * D)
                nv.tensor_tensor(c.x[:, sl], c.x[:, sl], c.lnk[:, sl], ALU.add).then_inc(s["sum_ok"], 1)

        @block.scalar
        def _(act):
            na = nc.scalar
            act_ln_all(c, act, s)

            def step(e, b):
                wait(act, s["y_ps"], e * 3 - 3)
                for m in range(MH):
                    act.wait_ge(s["h_ps"], e * 8 + (m + 1))
                    na.activation(hT[b][:, m, :], c.ps[2 + m % 4][:, 0:CAP], ACT.Relu,
                                  bias=b1[:, ds(e * MH + m, 1)]).then_inc(s["h_ok"], 1)
            pipeline(act, step, 0, 2, E3, E3)

            def over_block(n):
                for u in range(2):
                    act.wait_ge(s["oh_ps"], n * 2 + (u + 1))
                    for m in range(4):
                        last = na.activation(hTo[:, 4 * u + m, :], c.ps[2 + u][:, m * P:(m + 1) * P], ACT.Relu,
                                             bias=ob1[:, 4 * u + m:4 * u + m + 1])
                    last.then_inc(s["ohid_ok"], 1)
            over_block(0)
            act.wait_ge(s["slot_ok"], 1)
            nb = act.value_load(nbi[0:1, 0:1], min_val=2, max_val=OVB)
            with act.Fori(1, nb) as n:
                over_block(n)

        @block.tensor
        def _(pe):
            nt = nc.tensor
            pe_ln_all(c, pe, s)
            pe.wait_ge(s["lnT_ok"], NT)
            pe.wait_ge(s["w_in"], 16 * 8)
            pe_router(c, s, rw)
            pe.wait_ge(s["oh_ok"], 1)
            nt.matmul(c.ps[0][:, 0:NT * 8], upper[:, :], ohb[:, :], start=True, stop=True)
            nt.matmul(c.ps[1][:, 0:NT * 8], onesb[:, :], ohb[:, :], start=True, stop=True).then_inc(s["pre_ps"], 1)
            pe.wait_ge(s["over_ok"], 1)
            nt.matmul(c.ps[2][:, 0:NT], upper[:, :], overb[:, :], start=True, stop=True)
            nt.matmul(c.ps[3][:, 0:NT], onesb[:, :], overb[:, :], start=True, stop=True).then_inc(s["opre_ps"], 1)
            pe.wait_ge(s["slot_ok"], 1)

            def x_transpose(e, b):
                pe.wait_ge(x_in[b], count16(e, b, 2))
                wait(pe, s["xT_ok"], e)
                for k in range(KC):
                    for r, (r0, n) in enumerate(XR):
                        last = nt.transpose(c.ps[k][:, r0:r0 + n], X[b][0:n, r, k * P:(k + 1) * P],
                                            c.ident[0:n, 0:n])
                last.then_inc(s["xT_ps"], 1)

            def hidden(e, b):
                pe.wait_ge(w1_in[b], count16(e, b, 2))
                pe.wait_ge(s["xT_ok"], e + 1)
                for m in range(MH):
                    wait(pe, s["h_ok"], e * 8 + (m - 3))
                    for k in range(KC):
                        last = nt.matmul(c.ps[2 + m % 4][:, 0:CAP], w1[b][:, k, m * P:(m + 1) * P], xT[b][:, k, :],
                                         start=(k == 0), stop=(k == KC - 1))
                    last.then_inc(s["h_ps"], 1)

            def outputs(e, b):
                pe.wait_ge(w2_in[b], count16(e, b, 1))
                pe.wait_ge(s["h_ok"], e * 8 + 8)
                for r, (r0, n) in enumerate(XR):
                    wait(pe, s["y_ok"], e * 3 + (r - 1))
                    for m in range(MH):
                        last = nt.matmul(c.ps[6 + (3 * b + r) % 2][0:n, 0:D], hT[b][:, m, r0:r0 + n], w2[b][:, m, :],
                                         start=(m == 0), stop=(m == MH - 1))
                    last.then_inc(s["y_ps"], 1)
            x_transpose(0, 0)

            def step(e, b):
                hidden(e, b)
                if not is_static(e) or e + 1 < E3:
                    x_transpose(e + 1, 1 - b)
                outputs(e, b)
            pipeline(pe, step, 0, 2, E3 - 2, E3)
            pe.wait_ge(s["ow_in"], 48)

            def over_block(n):
                pe.wait_ge(s["oX_in"], n * 16 + 16)
                for k in range(KC):
                    last = nt.transpose(c.ps[0][:, k * P:(k + 1) * P], Xo[:, k * P:(k + 1) * P], c.ident[:, :])
                last.then_inc(s["oT_ps"], 1)
                pe.wait_ge(s["oT_ok"], n + 1)
                for u in range(2):
                    for m in range(4):
                        for k in range(KC):
                            last = nt.matmul(c.ps[2 + u][:, m * P:(m + 1) * P],
                                             ow1[:, k, (4 * u + m) * P:(4 * u + m + 1) * P], xTo[:, k * P:(k + 1) * P],
                                             start=(k == 0), stop=(k == KC - 1))
                    last.then_inc(s["oh_ps"], 1)
                pe.wait_ge(s["ohid_ok"], n * 2 + 2)
                wait(pe, s["oy_ok"], n)
                for m in range(MH):
                    last = nt.matmul(c.ps[6][:, 0:D], hTo[:, m, :], ow2[:, m, :], start=(m == 0), stop=(m == MH - 1))
                last.then_inc(s["oy_ps"], 1)
            pe.wait_ge(s["y_ok"], 3 * E3)
            over_block(0)
            nb = pe.value_load(nbi[0:1, 0:1], min_val=2, max_val=OVB)
            with pe.Fori(1, nb) as n:
                over_block(n)


def store_stage(c, d):
    nc = c.nc
    out_done = sem(c, "out_done")
    xv = c.x[:, :].rearrange("p (q b n) -> p q b n", b=B, n=D)
    with nc.Block() as block:
        @block.sync
        def _(sp):
            for b in range(B):
                sp.dma_start(d["out"][b].rearrange("(q p) n -> p q n", p=P), xv[:, :, b, :]).then_inc(out_done, 16)
            sp.wait_ge(out_done, 16 * B)


def build(nc, d):
    c = Core()
    with ExitStack() as ctx:
        c.nc, c.ctx, c.stage_ctx = nc, ctx, ctx
        c.stages = STAGES
        c.x = sb(c, "x_tiles", [P, NT * D])
        c.mean = sb(c, "mean", [P, NT])
        c.ve = sb(c, "var_eps", [P, NT])
        c.std = sb(c, "std", [P, NT])
        c.rstd = sb(c, "rstd", [P, NT])
        c.bst = sb(c, "bst", [P, NT * 6])
        c.ident = sb(c, "ident", [P, P])
        c.identb = sb(c, "identb", [P, P], BF16)
        c.tiledI = sb(c, "tiledI", [SK, HPB * SK], BF16)
        c.ones = sb(c, "ones", [P, P])
        c.hmask = sb(c, "hmask", [P, 8])
        c.hmask2 = sb(c, "hmask2", [P, 2])
        c.ctxT = sb(c, "ctxT", [P, KC, B * SK])
        c.ctxn = sb(c, "ctxn", [SK, B, D])
        c.W = [sb(c, f"W{k}", [P, KC, D]) for k in range(4)]
        c.bo, c.bv = sb(c, "bo", [P, D]), sb(c, "bv", [P, D])
        c.bq, c.bk = sb(c, "bq", [P, KC]), sb(c, "bk", [P, KC])
        pair = lambda name, shape: [sb(c, f"{name}{b}", shape) for b in range(2)]
        c.ln, c.lnT, c.qT = pair("ln", [P, D]), pair("lnT", [P, D]), pair("qT", [P, D])
        c.o, c.oT, c.pT = pair("o", [P, D]), pair("oT", [P, D]), pair("pT", [P, H * P])
        c.prob_pair = [sb(c, f"prob{b}", [P, MH * CAP]) for b in range(2)]
        c.prob = [t[:, 0:H * SK] for t in c.prob_pair]
        rows = (E3 * CAP + OVB * P, D)
        c.xd = nc.dram_tensor("expert_rows", rows, F32, kind="Internal").ap()
        c.yd = nc.dram_tensor("expert_outputs", rows, F32, kind="Internal").ap()
        c.mx = sb(c, "mx", [P, H])
        c.den = sb(c, "den", [P, H])
        c.rden = sb(c, "rden", [P, H])
        c.lnT_all = sb(c, "lnT_all", [P, KC, NT * P])
        c.lnk = sb(c, "lnk", [P, NT * D])
        c.gates, c.lg, c.lg2, c.lgt, c.choice, c.down = (
            sb(c, n, [P, NT * 8]) for n in ("gates", "lg", "lg2", "lgt", "choice", "down"))
        c.down4 = sb(c, "down4", [P, NT * 4])
        c.m1, c.m2, c.first = (sb(c, n, [P, NT]) for n in ("m1", "m2", "first"))
        c.acc = [sb(c, f"acc{o}", [P, D]) for o in range(2)]
        c.gap = sb(c, "gap", [P, 2])
        c.psall_t = ctx.enter_context(nc.psum_tensor("psum", [P, 8 * 512], F32))
        c.psall = c.psall_t[:, :]
        c.ps = [c.psall[:, k * 512:(k + 1) * 512] for k in range(8)]
        stages = [
            lambda: attn16(c, d, 0, False, True, HD ** -0.5,
                           {k: "L0_xattn_" + k for k in ("Wq", "Wk", "Wv", "Wo", "bq", "bk", "bv", "bo")}
                           | {"mask": "maskT0"}),
            lambda: moe0(c, d),
            lambda: attn16(c, d, 1, True, False, HD ** -0.5,
                           {k: "L1_xattn_" + k.lower() for k in ("Wq", "Wk", "Wv", "Wo", "bo")}
                           | {"mask": "maskT1"}),
            lambda: int8_linear(c, d),
            lambda: attn1(c, d),
            lambda: moe2(c, d),
            lambda: attn_gqa(c, d),
            lambda: moe3(c, d),
        ]
        run_stage(c, lambda: load_stage(c, d))
        for n, stage in enumerate(stages[:c.stages]):
            run_stage(c, stage, n == 7)
        if c.stages < 8:
            run_stage(c, lambda: store_stage(c, d), True)


def host_arrays(inputs):
    a = {k: np.ascontiguousarray(v) for k, v in inputs.items()}
    out = {"x": a["x"], "ctx_1024": a["ctx_1024"]}
    out["ctxT"] = np.ascontiguousarray(a["ctx_1024"].transpose(2, 0, 1).reshape(D, B * SK))
    out["maskT0"] = np.ascontiguousarray(a["mask_Bx1xSxS2_bk1"][:, 0].transpose(2, 0, 1)).view(np.int32)
    out["maskT1"] = np.ascontiguousarray(a["mask_Bx1xSxS2_ik1"][:, 0].transpose(2, 0, 1))
    for k in ("Wq", "Wk", "Wv", "Wo", "bq", "bk", "bv", "bo"):
        out["L0_xattn_" + k] = a["L0_xattn_" + k]
    for k in ("bq", "bk"):
        out["L0_xattn_" + k] = np.ascontiguousarray(a["L0_xattn_" + k].reshape(KC, P).T)
    out["L0_xattn_bv"] = np.concatenate([a["L0_xattn_bv"][h * HD:(h + VHEADS) * HD] for h in VHEAD0])
    rows_head = (np.arange(NBLK)[:, None] * P + np.arange(P)[None]) // SK
    out["c_vsel"] = np.ascontiguousarray(
        (rows_head[:, :, None] == np.array(VHEAD0)[:, None, None] + np.arange(VHEADS)).astype(np.float32)
        .transpose(1, 0, 2).reshape(P, NBLK * VHEADS))
    out["c_ident"] = np.eye(P, dtype=np.float32)
    out["c_tiled"] = np.tile(np.eye(SK, dtype=np.float32), (1, HPB))
    out["c_hmask"] = np.repeat(np.eye(8, dtype=np.float32), HD, axis=0)
    out["L0_ffn_gate_wT"] = np.ascontiguousarray(a["L0_ffn_gate_w"].T)
    for k in ("gate_b", "expert_w", "expert_b"):
        out["L0_ffn_" + k] = a["L0_ffn_" + k]
    out["c_down"] = np.tile(np.arange(8, 0, -1, dtype=np.float32), NT)
    out["c_down4"] = np.tile(np.arange(4, 0, -1, dtype=np.float32), NT)
    for k in ("wq", "wk", "wv", "wo", "bo"):
        out["L1_xattn_" + k] = a["L1_xattn_" + k]
    out["L1_ffn_rhsT"] = np.ascontiguousarray(a["L1_ffn_rhs"].T)
    out["maskT2"] = np.ascontiguousarray(a["mask_BxSxS2_ik1"].transpose(2, 0, 1).reshape(SK, B * S))
    out["L2_xattn_gamma"], out["L2_xattn_beta"] = a["L2_xattn_gamma"], a["L2_xattn_beta"]
    out["L2_ffn_gate_weightT"] = np.ascontiguousarray(a["L2_ffn_gate_weight"].T)
    out["L2_ffn_e_score_correction_bias"] = a["L2_ffn_e_score_correction_bias"]
    for k in ("gate_proj", "up_proj"):
        out["L2_ffn_" + k + "T"] = np.ascontiguousarray(a["L2_ffn_" + k].transpose(2, 0, 1).reshape(D, -1))
    out["L2_ffn_down_projT"] = np.ascontiguousarray(a["L2_ffn_down_proj"].transpose(2, 0, 1).reshape(P, -1))
    for k in ("Wq", "Wk", "Wv", "Wo"):
        out["L3_xattn_" + k] = a["L3_xattn_" + k]
    rows = np.concatenate([a["mask_BxS2_bf1"].reshape(-1), np.zeros(160 - B * SK, a["mask_BxS2_bf1"].dtype)])
    out["mask3"] = rows.reshape(1, 160).view(np.int32)
    rb = a["L3_xattn_rel_pos_bias"]
    away = np.minimum(np.abs(np.arange(S)[:, None] - np.arange(SK)[None]), rb.shape[1] - 1)
    out["rel_bias"] = np.ascontiguousarray(rb[:, away].transpose(1, 0, 2).reshape(S, HB * SK))
    inv = np.float32(1) / np.float32(10000) ** (np.arange(0, DH, 2, dtype=np.float32) / np.float32(DH))
    angle = np.repeat(np.outer(np.arange(S, dtype=np.float32), inv.astype(np.float32)), 2, axis=-1).astype(np.float64)
    out["c_cos"] = np.cos(angle).astype(np.float32)
    sin = np.sin(angle).astype(np.float32)
    out["c_sin"] = np.concatenate([-sin[:, :DH // 2], sin[:, DH // 2:]], axis=1)
    for k in ("router_w", "router_b", "b2", "ob2", "ow1", "ow2"):
        out["L3_ffn_" + k] = a["L3_ffn_" + k]
    out["L3_ffn_w1"] = a["L3_ffn_w1"].reshape(E3 * D, HF)
    out["L3_ffn_w2"] = a["L3_ffn_w2"].reshape(E3 * HF, D)
    out["L3_ffn_b1T"] = np.ascontiguousarray(a["L3_ffn_b1"].reshape(E3 * MH, P).T)
    out["L3_ffn_ob1T"] = np.ascontiguousarray(a["L3_ffn_ob1"].reshape(MH, P).T)
    out["c_upper"] = np.triu(np.ones((P, P), np.float32), 1)
    out["c_steps"] = (E3 * CAP + P * np.arange(OVB, dtype=np.float32)).astype(np.float32)[None]
    out["c_hmask2"] = np.repeat(np.eye(2, dtype=np.float32), P // 2, axis=0)
    return out


def kernel(**inputs):
    import concourse.bacc as bacc
    from concourse.bass_utils import run_bass_kernel_spmd as run

    nc = bacc.Bacc("TRN2", target_bir_lowering=False, num_devices=1)
    arrays = host_arrays(inputs)
    d = {n: nc.dram_tensor("in_" + n, a.shape, mybir.dt.from_np(a.dtype), kind="ExternalInput").ap()
         for n, a in arrays.items()}
    d["out"] = nc.dram_tensor("out_x", (B, S, D), F32, kind="ExternalOutput").ap()
    build(nc, d)
    r = run(nc, [{"in_" + n: a for n, a in arrays.items()}], core_ids=[0])
    return r.results[0]["out_x"]
```

```python
from contextlib import ExitStack

import numpy as np
import concourse.bass as bass
from concourse import mybir

P = 128
ALU = mybir.AluOpType
ACT = mybir.ActivationFunctionType
F32 = mybir.dt.float32
BF16 = mybir.dt.bfloat16
I32 = mybir.dt.int32
U32 = mybir.dt.uint32
STAGES = 8
U8 = mybir.dt.uint8
AX = mybir.AxisListType.X
ds = bass.ds

B, S, D = 2, 1024, 256
T = B * S
NT = T // P
KC = D // P
SK = 77
H = 16
HD = D // H
HPB = 6
HEAD_RUNS = [(0, 0, 6), (0, 6, 8), (1, 8, 12), (1, 12, 16)]
NEG = -float(2 ** 100)
EPS = 1e-5
NBLK = -(-H * SK // P)
VHEADS = 3
VHEAD0 = [min(j * P // SK, H - VHEADS) for j in range(NBLK)]
VHALF = NBLK // 2
PGROUPS = [(0, 4), (4, 8), (8, NBLK)]
PG = len(PGROUPS)
CH0 = 6
VC = HD + 1


def is_static(i):
    return isinstance(i, int)


def inside(i):
    return not is_static(i) or 0 <= i < NT


def wait(eng, sem, value):
    if not is_static(value) or value > 0:
        eng.wait_ge(sem, value)


def pipeline(eng, step, first, lo, hi, last, turn=2):
    for t in range(first, lo):
        step(t, t % 2)
    with eng.Fori(0, (hi - lo) // turn) as j:
        for u in range(turn):
            step(j * turn + (lo + u), (lo + u) % 2)
    for t in range(hi, last):
        step(t, t % 2)


class Chain:

    def __init__(self, eng, sem, per_turn=0):
        self.eng, self.sem, self.base, self.n = eng, sem, 0, 0

    def at(self, base):
        self.base, self.n = base, 0

    def __call__(self, ins):
        self.n += 1
        ins.then_inc(self.sem, 1)
        self.eng.wait_ge(self.sem, self.base + self.n)


class Core:
    pass


def sb(c, name, shape, dt=F32):
    return c.stage_ctx.enter_context(c.nc.sbuf_tensor(name, shape, dt))


def sem(c, name):
    c.stage_sems.append(c.nc.alloc_semaphore(name=name))
    return c.stage_sems[-1]


def run_stage(c, stage, last=False):
    with ExitStack() as c.stage_ctx:
        c.stage_sems = []
        stage()
    if not last:
        c.nc.clear_and_free_semaphores(c.stage_sems)
        c.nc.all_engine_barrier()


def xt(c, i):
    return c.x[:, ds(i * D, D)]


def mean_of(c, i):
    return c.mean[:, ds(i, 1)]


def rstd_of(c, i):
    return c.rstd[:, ds(i, 1)]


def bst_of(c, i):
    return c.bst[:, ds(i * 6, 6)]


def dve_rstd(c, dve, chain, ve_ready, std_ready, bst=None):
    nv = c.nc.vector
    st = (c.bst if bst is None else bst)[:, :].rearrange("p (i s) -> p i s", s=6)
    chain(nv.tensor_tensor(c.mean[:, :], st[:, :, 1], st[:, :, 4], ALU.add))
    chain(nv.tensor_tensor(c.ve[:, :], st[:, :, 1], st[:, :, 4], ALU.subtract))
    nv.tensor_scalar(c.mean[:, :], c.mean[:, :], 0.5, None, ALU.mult)
    chain(nv.tensor_tensor(c.rstd[:, :], st[:, :, 2], st[:, :, 5], ALU.add))
    chain(nv.scalar_tensor_tensor(out=c.ve[:, :], in0=c.ve[:, :], scalar=0.25, in1=c.ve[:, :],
                                  op0=ALU.mult, op1=ALU.mult))
    chain(nv.scalar_tensor_tensor(out=c.ve[:, :], in0=c.rstd[:, :], scalar=1.0 / D, in1=c.ve[:, :],
                                  op0=ALU.mult, op1=ALU.add))
    nv.tensor_scalar(c.ve[:, :], c.ve[:, :], EPS, None, ALU.add).then_inc(ve_ready, 1)
    dve.wait_ge(std_ready, 1 if bst is None else 2)
    chain(nv.reciprocal(c.rstd[:, :], c.std[:, :]))


def act_std(c, act, ve_ready, std_ready, nth=1):
    act.wait_ge(ve_ready, nth)
    c.nc.scalar.activation(c.std[:, :], c.ve[:, :], ACT.Sqrt).then_inc(std_ready, 1)


def load_stage(c, d):
    nc = c.nc
    x_in = [sem(c, f"x_in{b}") for b in range(B)]
    const_in = sem(c, "const_in")
    st = sem(c, "stats_chain")
    const_done = sem(c, "const_done")
    xv = c.x[:, :].rearrange("p (q b n) -> p q b n", b=B, n=D)
    with nc.Block() as block:
        @block.sync
        def _(sp):
            for b in range(B):
                sp.dma_start(xv[:, :, b, :], d["x"][b].rearrange("(q p) n -> p q n", p=P)).then_inc(x_in[b], 16)
            sp.dma_start(c.ctxT[:, :, :], d["ctxT"].rearrange("(k p) n -> p k n", p=P)).then_inc(const_in, 16)
            sp.dma_start(c.ctxn[:, :, :], d["ctx_1024"].rearrange("b s n -> s b n")).then_inc(const_in, 16)
            sp_attn16_inputs(c, sp, d, ATTN0, B * S // 4)
            sp.wait_ge(const_in, 128)

        @block.scalar
        def _(act):
            act.dma_start(c.ident[:, :], d["c_ident"]).then_inc(const_in, 16)
            act.dma_start(c.tiled_f, d["c_tiled"]).then_inc(const_in, 16)
            act.dma_start(c.hmask[:, :], d["c_hmask"]).then_inc(const_in, 16)
            act.dma_start(c.hmask2[:, :], d["c_hmask2"]).then_inc(const_in, 16)
            act.dma_start(c.down[:, :], d["c_down"].partition_broadcast(P)).then_inc(const_in, 16)
            act.dma_start(c.down4[:, :], d["c_down4"].partition_broadcast(P)).then_inc(const_in, 16)

        @block.vector
        def _(dve):
            for i in range(NT):
                if i < 2:
                    dve.wait_ge(x_in[i], 16)
                nc.vector.bn_stats(bst_of(c, i), xt(c, i)).then_inc(st, 1)
            dve.wait_ge(const_in, 128)
            nc.vector.tensor_copy(c.tiledI[:, :], c.tiled_f)
            nc.vector.tensor_copy(c.identb[:, :], c.ident[:, :]).then_inc(const_done, 1)
            nc.vector.memset(c.ones[:, :], 1.0)


def sp_attn16_inputs(c, sp, d, w, mask_words):
    for k, name in enumerate(("Wk", "Wv", "Wq", "Wo")):
        sp.dma_start(c.W[k][:, :, :], d[w[name]].rearrange("(k p) n -> p k n", p=P)).then_inc(c.w_in, 16)
    sp.dma_start(c.bo[:, :], d[w["bo"]].partition_broadcast(P)).then_inc(c.w_in, 16)
    if "bq" in w:
        sp.dma_start(c.bq[:, :], d[w["bq"]]).then_inc(c.w_in, 16)
        sp.dma_start(c.bk[:, :], d[w["bk"]]).then_inc(c.w_in, 16)
        sp.dma_start(c.bv[:, :], d[w["bv"]].partition_broadcast(P)).then_inc(c.w_in, 16)
        sp.dma_start(c.vsel[:, :], d["c_vsel"]).then_inc(c.w_in, 16)
    sp.dma_start(c.mraw[:, 0:mask_words], d[w["mask"]].rearrange("k b s -> k (b s)")).then_inc(c.mask_in, 16)


def pool_mask(pool, c, raw, masked_op, done):
    c.nc.gpsimd.tensor_scalar(c.maskT[:, :], raw, 0.0, NEG, masked_op, ALU.mult).then_inc(done, 1)


ATTN0 = {k: "L0_xattn_" + k for k in ("Wq", "Wk", "Wv", "Wo", "bq", "bk", "bv", "bo")} | {"mask": "maskT0"}
ATTN1 = {k: "L1_xattn_" + k.lower() for k in ("Wq", "Wk", "Wv", "Wo", "bo")} | {"mask": "maskT1"}
N_ATTN0, N_ATTN1 = 9, 5


def attn16(c, n, has_bias, scale, n_in):
    nc = c.nc
    L = f"a{n}_"
    KT = sb(c, L + "KT", [P, KC, B * SK])
    KB = sb(c, L + "KB", [P, KC, B, 8, SK])
    VB = sb(c, L + "VB", [P, B, NBLK * VHEADS, VC])
    V = sb(c, L + "V", [SK, B, D])
    vsel, maskT = c.vsel, c.maskT
    names = ("k_ps", "k_sb", "kb_ok", "v_ps", "v_sb", "vb_ps", "v_raw", "mask_ok", "ve_ok", "std_ok", "chain",
             "ln_ok", "lnT_ps", "lnT_ok", "q_ps", "qT_ok", "s_ps", "shifted", "exp_ok", "pT_ps", "pT_ok",
             "pv_ps", "o_ok", "oT_ps", "oT_ok", "y_ps", "y_used", "biased", "mx_chain", "stats_ok")
    (k_ps, k_sb, kb_ok, v_ps, v_sb, vb_ps, v_raw, mask_ok, ve_ok, std_ok, chain_s,
     ln_ok, lnT_ps, lnT_ok, q_ps, qT_ok, s_ps, shifted, exp_ok, pT_ps, pT_ok,
     pv_ps, o_ok, oT_ps, oT_ok, y_ps, y_used, biased, mx_chain, stats_ok) = [sem(c, L + s) for s in names]
    w_in = c.w_in
    bank_s = c.psall[:, 0:3 * 512]
    bank_pT = [c.ps[3], c.ps[4]]
    bank_t = c.ps[5]
    bank_q = c.ps[6]
    bank_pv = bank_y = c.ps[7]
    bank_v = [c.ps[4], c.ps[7]]
    sview = bank_s.rearrange("p (b n) -> p b n", b=3)

    with nc.Block() as block:
        @block.gpsimd
        def _(pool):
            if n == 0:
                pool.wait_ge(c.mask_in, 16)
                pool_mask(pool, c, c.mraw[:, :].bitcast(U8)[:, 0:B * S], ALU.is_gt, mask_ok)
            pool.wait_ge(w_in, 16 * n_in)

            def step(i, b):
                pool.wait_ge(ln_ok, i + 1)
                nc.gpsimd.tensor_tensor(xt(c, i), xt(c, i), c.bo[:, :], ALU.add).then_inc(biased, 1)
            pipeline(pool, step, 0, 0, NT, NT)

        @block.vector
        def _(dve):
            chain = Chain(dve, chain_s)
            dve_rstd(c, dve, chain, ve_ok, std_ok)
            nv = nc.vector

            def layer_norm(i, b):
                wait(dve, lnT_ps, i - 1)
                nv.tensor_scalar(c.ln[b][:, :], xt(c, i), mean_of(c, i), rstd_of(c, i),
                                 ALU.subtract, ALU.mult).then_inc(ln_ok, 1)
            layer_norm(0, 0)
            layer_norm(1, 1)
            dve.wait_ge(w_in, 16 * n_in)
            dve.wait_ge(v_ps, 1)
            src = bank_v[0][0:SK, :].rearrange("k (b n) -> k b n", b=B)
            if has_bias:
                nv.tensor_tensor(V[:, :, :], src, c.bv[0:SK, :].unsqueeze(1).to_broadcast([SK, B, D]),
                                 ALU.add).then_inc(v_raw, 1)
            else:
                nv.tensor_copy(V[:, :, :], src).then_inc(v_raw, 1)
            dve.wait_ge(k_sb, 2)
            for k in range(KC):
                for b in range(B):
                    last = nv.tensor_tensor(KB[:, k, b, :, :],
                                            KT[:, k, b * SK:(b + 1) * SK].unsqueeze(1).to_broadcast([P, 8, SK]),
                                            c.hmask[:, :].unsqueeze(2).to_broadcast([P, 8, SK]), ALU.mult)
            last.then_inc(kb_ok, 1)
            def value_blocks():
                blocks = lambda t: t.rearrange("p (j g) -> p j g", g=VHEADS)
                for b in range(B):
                    for q in range(2):
                        dve.wait_ge(vb_ps, q + 1)
                        src = bank_v[q][:, 0:VHALF * B * VHEADS * HD].rearrange("p (j b g e) -> p b j g e", b=B, g=VHEADS,
                                                                              e=HD)[:, b]
                        r = slice(q * VHALF * VHEADS, (q + 1) * VHALF * VHEADS)
                        out = VB[:, b, r, 0:HD].rearrange("p (j g) e -> p j g e", g=VHEADS)
                        nv.tensor_tensor(out, src, blocks(vsel[:, r]).unsqueeze(3)
                                         .to_broadcast([P, VHALF, VHEADS, HD]), ALU.mult)
                    nv.tensor_copy(VB[:, b, :, HD], vsel[:, :]).then_inc(v_sb, 1)

            def maxima(i, b):
                dve.wait_ge(s_ps, i + 1)
                nv.reduce_max(c.mx[:, 0:12], sview[:, 0:2, 0:HPB * SK].rearrange("p b (h k) -> p b h k", k=SK), AX)
                nv.reduce_max(c.mx[:, 12:16], sview[:, 2, 0:4 * SK].rearrange("p (h k) -> p h k", k=SK),
                              AX).then_inc(mx_chain, 1)

            def shift(i, b):
                wait(dve, pT_ps, PG * (i - 1))
                dve.wait_ge(mx_chain, i + 1)
                for q in range(3):
                    nh = HPB if q < 2 else 4
                    out = c.prob[b][:, q * HPB * SK:(q * HPB + nh) * SK].rearrange("p (h k) -> p h k", k=SK)
                    last = nv.tensor_tensor(out, sview[:, q, 0:nh * SK].rearrange("p (h k) -> p h k", k=SK),
                                            c.mx[:, q * HPB:q * HPB + nh].unsqueeze(2).to_broadcast([P, nh, SK]),
                                            ALU.subtract)
                last.then_inc(shifted, 1)

            def normalise(i, b):
                dve.wait_ge(pv_ps, i + 1)
                pv = bank_pv[:, 0:H * VC].rearrange("p (h e) -> p h e", e=VC)
                chain(nv.reciprocal(c.rden[:, :], pv[:, :, HD]))
                nv.tensor_tensor(c.o[b][:, :].rearrange("p (h e) -> p h e", e=HD), pv[:, :, 0:HD],
                                 c.rden[:, :].unsqueeze(2).to_broadcast([P, H, HD]), ALU.mult).then_inc(o_ok, 1)

            def residual(i, b):
                dve.wait_ge(y_ps, i + 1)
                dve.wait_ge(biased, i + 1)
                nv.tensor_tensor(xt(c, i), xt(c, i), bank_y[:, 0:D], ALU.add).then_inc(y_used, 1)

            def step(t, b):
                chain.at((CH0 + max(0, min(t - 1, NT))) if is_static(t) else t + (CH0 - 1))
                if inside(t + 2):
                    layer_norm(t + 2, b)
                if inside(t):
                    maxima(t, b)
                if inside(t - 2):
                    residual(t - 2, b)
                if inside(t):
                    shift(t, b)
                if inside(t - 2):
                    dve.wait_ge(y_used, t - 1)
                    nv.bn_stats(bst_of(c, t - 2), xt(c, t - 2)).then_inc(stats_ok, 1)
                if inside(t - 1):
                    normalise(t - 1, 1 - b)
            step(0, 0)
            value_blocks()
            pipeline(dve, step, 1, 2, NT - 2, NT + 2)

        @block.scalar
        def _(act):
            na = nc.scalar
            act_std(c, act, ve_ok, std_ok)
            act.wait_ge(k_ps, 1)
            for k in range(KC):
                if has_bias:
                    ins = na.activation(KT[:, k, :], c.ps[k + 2][:, 0:B * SK], ACT.Identity, bias=c.bk[:, k:k + 1])
                else:
                    ins = na.activation(KT[:, k, :], c.ps[k + 2][:, 0:B * SK], ACT.Copy)
                ins.then_inc(k_sb, 1)

            def lnT_copy(i, b):
                act.wait_ge(lnT_ps, i + 1)
                na.activation(c.lnT[b][:, :], bank_t[:, 0:D], ACT.Copy).then_inc(lnT_ok, 1)

            def q_copy(i, b):
                act.wait_ge(q_ps, i + 1)
                if has_bias:
                    for k in range(KC):
                        ins = na.activation(c.qT[b][:, k * P:(k + 1) * P], bank_q[:, k * P:(k + 1) * P],
                                            ACT.Identity, bias=c.bq[:, k:k + 1])
                else:
                    ins = na.activation(c.qT[b][:, :], bank_q[:, 0:D], ACT.Copy)
                ins.then_inc(qT_ok, 1)

            def exps(i, b):
                act.wait_ge(shifted, i + 1)
                na.activation(c.prob[b][:, :], c.prob[b][:, :], ACT.Exp, scale=scale).then_inc(exp_ok, 1)

            def pT_copy(i, b):
                wait(act, pv_ps, i - 1)
                for g, (j0, j1) in enumerate(PGROUPS):
                    act.wait_ge(pT_ps, i * PG + (g + 1))
                    na.activation(c.pT[b][:, j0 * P:j1 * P], bank_pT[g % 2][:, 0:(j1 - j0) * P],
                                  ACT.Copy).then_inc(pT_ok, 1)

            def oT_copy(i, b):
                act.wait_ge(oT_ps, i + 1)
                na.activation(c.oT[b][:, :], bank_t[:, 0:D], ACT.Copy).then_inc(oT_ok, 1)

            lnT_copy(0, 0)
            lnT_copy(1, 1)
            q_copy(0, 0)

            def step(t, b):
                if inside(t - 2):
                    oT_copy(t - 2, b)
                if inside(t - 1):
                    pT_copy(t - 1, 1 - b)
                if inside(t + 1):
                    q_copy(t + 1, 1 - b)
                if inside(t + 2):
                    lnT_copy(t + 2, b)
                if inside(t):
                    exps(t, b)
            pipeline(act, step, 0, 2, NT - 2, NT + 2)

        @block.tensor
        def _(pe):
            nt = nc.tensor
            pe.wait_ge(w_in, 16 * n_in)
            for m in range(KC):
                for k in range(KC):
                    last = nt.matmul(c.ps[m + 2][:, 0:B * SK], c.W[0][:, k, m * P:(m + 1) * P], c.ctxT[:, k, :],
                                     start=(k == 0), stop=(k == KC - 1))
            last.then_inc(k_ps, 1)

            for b in range(B):
                for k in range(KC):
                    last = nt.matmul(bank_v[0][0:SK, b * D:(b + 1) * D], c.ctxT[:, k, b * SK:(b + 1) * SK],
                                     c.W[1][:, k, :], start=(k == 0), stop=(k == KC - 1))
            last.then_inc(v_ps, 1)

            def value_blocks():
                pe.wait_ge(v_raw, 1)
                for j, h0 in enumerate(VHEAD0):
                    key0, o = j * P % SK, j % VHALF * B * VHEADS * HD
                    last = nt.matmul(bank_v[j // VHALF][:, o:o + B * VHEADS * HD], c.tiled_f[:, key0:key0 + P],
                                     V[:, :, h0 * HD:(h0 + VHEADS) * HD], start=True, stop=True)
                    if j % VHALF == VHALF - 1:
                        last.then_inc(vb_ps, 1)

            def lnT(i, b):
                pe.wait_ge(ln_ok, i + 1)
                wait(pe, lnT_ok, i)
                wait(pe, oT_ok, i - 3)
                for k in range(KC):
                    last = nt.transpose(bank_t[:, k * P:(k + 1) * P], c.ln[b][:, k * P:(k + 1) * P], c.ident[:, :])
                last.then_inc(lnT_ps, 1)

            def queries(i, b):
                pe.wait_ge(lnT_ok, i + 1)
                wait(pe, qT_ok, i)
                for m in range(KC):
                    for k in range(KC):
                        last = nt.matmul(bank_q[:, m * P:(m + 1) * P], c.W[2][:, k, m * P:(m + 1) * P],
                                         c.lnT[b][:, k * P:(k + 1) * P], start=(k == 0), stop=(k == KC - 1))
                last.then_inc(q_ps, 1)

            def scores(i, b, q0):
                pe.wait_ge(qT_ok, i + 1)
                wait(pe, shifted, i)
                for half, h0, h1 in HEAD_RUNS:
                    q, o = h0 // HPB, (h0 % HPB) * SK
                    nt.matmul(sview[:, q, o:o + (h1 - h0) * SK], c.qT[b][:, half * P:(half + 1) * P],
                              KB[:, half, b, h0 - 8 * half:h1 - 8 * half, :].rearrange("p h k -> p (h k)"),
                              start=(h0 % HPB == 0), stop=False, skip_group_check=True)
                for q in range(3):
                    nh = HPB if q < 2 else 4
                    last = nt.matmul(sview[:, q, 0:nh * SK], maskT[:, ds(q0, P)],
                                     c.tiledI[:, 0:nh * SK], start=False, stop=True, skip_group_check=True)
                last.then_inc(s_ps, 1)

            def prob_transpose(i, b, g):
                if g == 0:
                    pe.wait_ge(exp_ok, i + 1)
                wait(pe, pT_ok, i * PG + max(g - 1, 0))
                j0, j1 = PGROUPS[g]
                for j in range(j0, j1):
                    rows = min(P, H * SK - j * P)
                    last = nt.transpose(bank_pT[g % 2][0:rows, (j - j0) * P:(j - j0 + 1) * P],
                                        c.prob[b][:, j * P:j * P + rows], c.ident[:, :])
                last.then_inc(pT_ps, 1)

            def weighted_values(i, b):
                pe.wait_ge(pT_ok, i * PG + PG)
                wait(pe, y_used, i)
                for j, h0 in enumerate(VHEAD0):
                    rows = min(P, H * SK - j * P)
                    last = nt.matmul(bank_pv[:, h0 * VC:(h0 + VHEADS) * VC], c.pT[b][0:rows, j * P:(j + 1) * P],
                                     VB[0:rows, b, j * VHEADS:(j + 1) * VHEADS, :].rearrange("p g e -> p (g e)"),
                                     start=(j == 0), stop=(j == NBLK - 1), skip_group_check=True)
                last.then_inc(pv_ps, 1)

            def o_transpose(i, b):
                pe.wait_ge(o_ok, i + 1)
                wait(pe, lnT_ok, min(i + 4, NT) if is_static(i) else i + 4)
                for k in range(KC):
                    last = nt.transpose(bank_t[:, k * P:(k + 1) * P], c.o[b][:, k * P:(k + 1) * P], c.ident[:, :])
                last.then_inc(oT_ps, 1)

            def project(i, b):
                pe.wait_ge(oT_ok, i + 1)
                for k in range(KC):
                    last = nt.matmul(bank_y[:, 0:D], c.oT[b][:, k * P:(k + 1) * P], c.W[3][:, k, :],
                                     start=(k == 0), stop=(k == KC - 1))
                last.then_inc(y_ps, 1)

            lnT(0, 0)
            lnT(1, 1)
            queries(0, 0)
            pe.wait_ge(kb_ok, 1)
            if n == 0:
                pe.wait_ge(mask_ok, 1)

            def step(t, b):
                if inside(t):
                    q0 = b * S + (t // 2) * P if is_static(t) else t * (P // 2) + (b * S - b * (P // 2))
                    scores(t, b, q0)
                if inside(t - 2):
                    o_transpose(t - 2, b)
                if inside(t - 1):
                    prob_transpose(t - 1, 1 - b, 0)
                    prob_transpose(t - 1, 1 - b, 1)
                if inside(t - 2):
                    project(t - 2, b)
                if inside(t - 1):
                    prob_transpose(t - 1, 1 - b, 2)
                if inside(t + 1):
                    queries(t + 1, 1 - b)
                if inside(t + 2):
                    lnT(t + 2, b)
                if inside(t - 1):
                    weighted_values(t - 1, 1 - b)
            step(0, 0)
            value_blocks()
            pe.wait_ge(v_sb, B)
            pipeline(pe, step, 1, 2, NT - 2, NT + 2)


def sems(c, prefix, *names):
    return {n: sem(c, prefix + n) for n in names}


NORM = ("router_in", "lgT_ps", "lgT_ok", "ve_ok", "std_ok", "chain", "ln_ok", "lnT_ps", "lnT_ok")



def dve_ln_all(c, dve, s, chain, rows=None):
    dve_rstd(c, dve, chain, s["ve_ok"], s["std_ok"])
    nv = c.nc.vector

    def step(i, b):
        if rows is None:
            wait(dve, s["lnT_ps"], i - 1)
        out = c.ln[b][:, :] if rows is None else rows[:, ds(i * D, D)]
        nv.tensor_scalar(out, xt(c, i), mean_of(c, i), rstd_of(c, i), ALU.subtract, ALU.mult).then_inc(s["ln_ok"], 1)
    for i in range(NT):
        step(i, i % 2)


T_BANKS = (4, 6, 7)


def pe_ln_all(c, pe, s, w, router_in, rows=None):
    nt = c.nc.tensor

    def logits(g):
        if g == 0:
            pe.wait_ge(s["router_in"], router_in)
        pe.wait_ge(s["lnT_ok"], 4 * g + 4)
        for k in range(KC):
            last = nt.matmul(c.ps[g][0:8, :], w[:, k, :], c.lnT_all[:, k, g * 512:(g + 1) * 512],
                             start=(k == 0), stop=(k == KC - 1))
        last.then_inc(s["lgT_ps"], 1)

    for t in range(NT):
        b = t % 2
        pe.wait_ge(s["ln_ok"], t + 1)
        wait(pe, s["lnT_ok"], t - 2)
        for k in range(KC):
            src = c.ln[b][:, k * P:(k + 1) * P] if rows is None else rows[:, t * D + k * P:t * D + (k + 1) * P]
            last = nt.transpose(c.ps[T_BANKS[t % 3]][:, k * P:(k + 1) * P], src, c.ident[:, :])
        last.then_inc(s["lnT_ps"], 1)
        if t % 4 == 1 and t > 4:
            logits(t // 4 - 1)
    logits(NT // 4 - 1)
    for g in range(NT // 4):
        pe.wait_ge(s["lgT_ok"], g + 1)
        for i in range(4 * g, 4 * g + 4):
            last = nt.transpose(c.ps[5][:, i * 8:(i + 1) * 8], c.prob_pair[0][0:8, i * P:(i + 1) * P],
                                c.ident[0:8, 0:8])
    last.then_inc(s["logits_ps"], 1)


def dve_logits(c, dve, s):
    for g in range(NT // 4):
        dve.wait_ge(s["lgT_ps"], g + 1)
        c.nc.vector.tensor_copy(c.prob_pair[0][0:8, g * 512:(g + 1) * 512], c.ps[g][0:8, :]).then_inc(s["lgT_ok"], 1)


def act_ln_all(c, act, s):
    act_std(c, act, s["ve_ok"], s["std_ok"])
    na = c.nc.scalar

    for i in range(NT):
        act.wait_ge(s["lnT_ps"], i + 1)
        na.activation(lnT_tile(c, i), c.ps[T_BANKS[i % 3]][:, 0:D].rearrange("p (k n) -> p k n", k=KC),
                      ACT.Copy).then_inc(s["lnT_ok"], 1)


def lnT_tile(c, i):
    return c.lnT_all[:, :, ds(i * P, P)]


def bc(ap, g):
    return ap.unsqueeze(2).to_broadcast([P, NT, g])


def top1(c, chain, l, g, hot, tmp, m):
    nv = c.nc.vector
    chain(nv.reduce_max(m, l, AX))
    chain(nv.tensor_tensor(tmp, l, bc(m, g), ALU.is_equal))
    chain(nv.tensor_tensor(tmp, tmp, c.down[:, 0:NT * g].rearrange("p (i g) -> p i g", g=g)
                           if g == 8 else c.down4[:, 0:NT * g].rearrange("p (i g) -> p i g", g=g), ALU.mult))
    chain(nv.reduce_max(c.first[:, :], tmp, AX))
    chain(nv.tensor_tensor(hot, tmp, bc(c.first[:, :], g), ALU.is_equal))


def top2(c, chain, l, g, keep, l2, tmp, m):
    nv = c.nc.vector
    m2 = c.m2[:, :]
    top1(c, chain, l, g, keep, tmp, m)
    chain(nv.scalar_tensor_tensor(out=l2, in0=keep, scalar=NEG, in1=l, op0=ALU.mult, op1=ALU.add))
    top1(c, chain, l2, g, l2, tmp, m2)
    chain(nv.tensor_tensor(keep, keep, l2, ALU.add))


def g8(t):
    return t[:, :].rearrange("p (i g) -> p i g", g=8)


def moe0(c, d):
    nc = c.nc
    W = sb(c, "m0_W", [P, KC, 8 * D])
    gw = sb(c, "m0_gw", [P, KC, 8])
    gb = sb(c, "m0_gb", [P, 8])
    eb = sb(c, "m0_eb", [8, D])
    gT = sb(c, "m0_gT", [8, NT * P])
    gTs = [sb(c, f"m0_gTs{b}", [8, P]) for b in range(2)]
    s = sems(c, "m0_", *NORM, "mask_ok", "w_in", "logits_ps", "max_ok", "exp_ok", "gates_ok", "gT_ps", "gT_ok", "tile_in",
             "gtile_in", "e_ps", "acc", "bias_ps", "y_used", "x_ok")
    gates = g8(c.gates)
    with nc.Block() as block:
        @block.sync
        def _(sp):
            sp.dma_start(gw[:, :, :], d["L0_ffn_gate_wT"].rearrange("(k p) e -> p k e", p=P)).then_inc(s["router_in"], 16)
            sp.dma_start(gb[:, :], d["L0_ffn_gate_b"].partition_broadcast(P)).then_inc(s["router_in"], 16)
            sp.dma_start(eb[:, :], d["L0_ffn_expert_b"]).then_inc(s["w_in"], 16)
            for k in range(KC):
                sp.dma_start(W[:, k, :].rearrange("p (e n) -> p e n", e=8),
                             d["L0_ffn_expert_w"][:, k * P:(k + 1) * P, :].rearrange("e p n -> p e n")
                             ).then_inc(s["w_in"], 16)
            sp_attn16_inputs(c, sp, d, ATTN1, B * S)

        @block.vector
        def _(dve):
            nv = nc.vector
            chain = Chain(dve, s["chain"])
            dve_ln_all(c, dve, s, chain)
            dve_logits(c, dve, s)
            dve.wait_ge(s["logits_ps"], 1)
            l = g8(c.lg)
            chain(nv.tensor_tensor(l, g8(c.ps[5][:, 0:NT * 8]), gb[:, :].unsqueeze(1).to_broadcast([P, NT, 8]), ALU.add))
            top2(c, chain, l, 8, gates, g8(c.lg2), g8(c.lgt), c.m1[:, :])
            nv.tensor_tensor(l, l, bc(c.m1[:, :], 8), ALU.subtract).then_inc(s["max_ok"], 1)
            dve.wait_ge(s["exp_ok"], 1)
            chain(nv.tensor_tensor(gates, gates, l, ALU.mult))
            chain(nv.reduce_sum(c.m1[:, :], gates, AX))
            chain(nv.reciprocal(c.m1[:, :], c.m1[:, :]))
            nv.tensor_tensor(gates, gates, bc(c.m1[:, :], 8), ALU.mult).then_inc(s["gates_ok"], 1)
            for q in range(4):
                dve.wait_ge(s["gT_ps"], q + 1)
                nv.tensor_copy(gT[:, q * 512:(q + 1) * 512], c.ps[4 + q][0:8, :]).then_inc(s["gT_ok"], 1)

            def step(i, b):
                for p in range(4):
                    dve.wait_ge(s["e_ps"], i * 4 + (p + 1))
                    for o in range(2):
                        src = c.ps[p][:, o * D:(o + 1) * D]
                        gate = c.gates[:, ds(i * 8 + (2 * p + o), 1)]
                        if p == 0:
                            ins = nv.tensor_scalar(c.acc[o][:, :], src, gate, None, ALU.mult)
                        else:
                            dve.wait_ge(s["acc"], i * 8 + (2 * p + o - 1))
                            ins = nv.scalar_tensor_tensor(out=c.acc[o][:, :], in0=src, scalar=gate,
                                                          in1=c.acc[o][:, :], op0=ALU.mult, op1=ALU.add)
                        ins.then_inc(s["acc"], 1)
                dve.wait_ge(s["acc"], i * 8 + 8)
                dve.wait_ge(s["bias_ps"], i + 1)
                nv.tensor_tensor(xt(c, i), xt(c, i), c.acc[1][:, :], ALU.add)
                nv.tensor_tensor(c.acc[0][:, :], c.ps[4][:, 0:D], c.acc[0][:, :], ALU.add).then_inc(s["y_used"], 1)
                dve.wait_ge(s["y_used"], i + 1)
                nv.tensor_tensor(xt(c, i), xt(c, i), c.acc[0][:, :], ALU.add).then_inc(s["x_ok"], 1)
                dve.wait_ge(s["x_ok"], i + 1)
                nv.tensor_copy(c.gap[:, b:b + 1], c.ones[:, 0:1])
                nv.bn_stats(bst_of(c, i), xt(c, i))
            pipeline(dve, step, 0, 0, NT, NT)

        @block.scalar
        def _(act):
            na = nc.scalar
            act_ln_all(c, act, s)

            def step(i, b):
                wait(act, s["bias_ps"], i - 1)
                na.activation(c.lnT[b][:, :].rearrange("p (k n) -> p k n", k=KC), lnT_tile(c, i),
                              ACT.Copy).then_inc(s["tile_in"], 1)
            step(0, 0)
            step(1, 1)
            act.wait_ge(s["max_ok"], 1)
            na.activation(c.lg[:, :], c.lg[:, :], ACT.Exp).then_inc(s["exp_ok"], 1)
            pipeline(act, step, 2, 2, NT, NT)

        @block.gpsimd
        def _(pool):
            def step(i, b):
                wait(pool, s["bias_ps"], i - 1)
                nc.gpsimd.tensor_copy(gTs[b][:, :], gT[:, ds(i * P, P)]).then_inc(s["gtile_in"], 1)
            pool.wait_ge(c.mask_in, 32)
            pool_mask(pool, c, c.mraw[:, :], ALU.is_equal, s["mask_ok"])
            pool.wait_ge(s["gT_ok"], 4)
            pipeline(pool, step, 0, 2, NT, NT)

        @block.tensor
        def _(pe):
            nt = nc.tensor
            pe_ln_all(c, pe, s, gw, 16 * 2)
            pe.wait_ge(s["w_in"], 16 * 3)

            def products(i, b):
                pe.wait_ge(s["tile_in"], i + 1)
                for p in range(4):
                    wait(pe, s["acc"], i * 8 - 6 + 2 * p)
                    for k in range(KC):
                        last = nt.matmul(c.ps[p][:, :], c.lnT[b][:, k * P:(k + 1) * P],
                                         W[:, k, p * 512:(p + 1) * 512], start=(k == 0), stop=(k == KC - 1))
                    last.then_inc(s["e_ps"], 1)

            def bias(i, b):
                pe.wait_ge(s["gtile_in"], i + 1)
                wait(pe, s["y_used"], i)
                nt.matmul(c.ps[4][:, 0:D], gTs[b][:, :], eb[:, :], start=True, stop=True).then_inc(s["bias_ps"], 1)

            def step(i, b):
                products(i, b)
                bias(i, b)
            products(0, 0)
            pe.wait_ge(s["gates_ok"], 1)
            for i in range(NT):
                last = nt.transpose(c.ps[4 + i // 4][0:8, (i % 4) * P:(i % 4 + 1) * P], c.gates[:, i * 8:(i + 1) * 8],
                                    c.ident[:, :])
                if i % 4 == 3:
                    last.then_inc(s["gT_ps"], 1)
            pe.wait_ge(s["gT_ok"], 4)
            bias(0, 0)
            pipeline(pe, step, 1, 2, NT, NT)


ROUND = 1.5 * 2 ** 23
QMAX = 127.0


def int8_linear(c, d):
    nc = c.nc
    R = sb(c, "i8_R", [P, KC, D])
    Rq = sb(c, "i8_Rq", [P, KC, D], BF16)
    RQ = sb(c, "i8_RQ", [P, KC, D], BF16)
    rs, rinv = sb(c, "i8_rs", [P, KC]), sb(c, "i8_rinv", [P, KC])
    rsw = sb(c, "i8_rsw", [P, KC, P])
    rsB = sb(c, "i8_rsB", [P, D])
    ls, linv = sb(c, "i8_ls", [P, NT]), sb(c, "i8_linv", [P, NT])
    r = [sb(c, f"i8_r{b}", [P, D]) for b in range(2)]
    q = [sb(c, f"i8_q{b}", [P, D], BF16) for b in range(2)]
    qT = [sb(c, f"i8_qT{b}", [P, D], BF16) for b in range(2)]
    zeros = sb(c, "i8_zeros", [P, 17 * D])
    unr = sb(c, "i8_unround", [P, 1])
    mraw2 = c.lnT_all[0:SK, :, :].rearrange("k a n -> k (a n)")[:, 0:B * S].bitcast(I32)
    s = sems(c, "i8_", "mask_ok", "zero_ok", "zero_out", "ve_ok", "std_ok", "chain", "w_in", "rq_ok", "rT_ps", "RQ_ok", "rsB_ps", "t_ok", "r_ok", "q_ok",
             "qT_ps", "qT_ok", "y_ps", "y_ok", "x_ok", "ln_done")
    with nc.Block() as block:
        @block.sync
        def _(sp):
            sp.dma_start(R[:, :, :], d["L1_ffn_rhsT"].rearrange("(m p) k -> p m k", p=P)).then_inc(s["w_in"], 16)
            sp.dma_start(mraw2, d["maskT2"]).then_inc(c.mask_in, 16)
            sp.wait_ge(s["zero_ok"], 1)
            for j in range(2):
                sp.dma_start(c.xd[j * 17 * P:(j + 1) * 17 * P, :].rearrange("(p r) n -> p (r n)", p=P),
                             zeros[:, :]).then_inc(s["zero_out"], 16)
            sp.dma_start(c.yd[E3 * CAP:, :].rearrange("(p r) n -> p (r n)", p=P), zeros[:, 0:OVB * D]
                         ).then_inc(s["zero_out"], 16)
            sp.wait_ge(s["zero_out"], 48)

        @block.gpsimd
        def _(pool):
            nc.gpsimd.memset(zeros[:, :], 0.0).then_inc(s["zero_ok"], 1)
            pool.wait_ge(c.mask_in, 48)
            pool_mask(pool, c, mraw2, ALU.is_equal, s["mask_ok"])

            def residual(i, b):
                pool.wait_ge(s["y_ok"], i + 1)
                nc.gpsimd.tensor_tensor(xt(c, i), xt(c, i), c.acc[b][:, :], ALU.add).then_inc(s["x_ok"], 1)
            pipeline(pool, residual, 0, 4, NT, NT, 4)

        @block.vector
        def _(dve):
            nv = nc.vector
            chain = Chain(dve, s["chain"])
            dve_rstd(c, dve, chain, s["ve_ok"], s["std_ok"])

            def norm(i, b):
                nv.tensor_scalar(c.lnk[:, ds(i * D, D)], xt(c, i), mean_of(c, i), rstd_of(c, i),
                                 ALU.subtract, ALU.mult).then_inc(s["ln_done"], 1)
            for i in range(NT):
                norm(i, i % 2)
            dve.wait_ge(s["ln_done"], NT)
            dve.wait_ge(s["w_in"], 16)
            chain(nv.tensor_reduce(out=rs[:, :], in_=R[:, :, :], axis=AX, op=ALU.max, apply_absolute_value=True))
            chain(nv.tensor_scalar(rs[:, :], rs[:, :], 1e-12, 1.0 / QMAX, ALU.max, ALU.mult))
            chain(nv.reciprocal(rinv[:, :], rs[:, :]))
            for m in range(KC):
                chain(nv.tensor_scalar(R[:, m, :], R[:, m, :], rinv[:, m:m + 1], ROUND, ALU.mult, ALU.add))
                chain(nv.tensor_scalar(R[:, m, :], R[:, m, :], ROUND, QMAX, ALU.subtract, ALU.min))
                nv.tensor_scalar(Rq[:, m, :], R[:, m, :], -QMAX, None, ALU.max)
                nv.tensor_scalar(rsw[:, m, :], c.ones[:, :], rs[:, m:m + 1], None, ALU.mult).then_inc(s["rq_ok"], 1)
            chain(nv.tensor_reduce(out=ls[:, :], in_=c.lnk[:, :].rearrange("p (i n) -> p i n", n=D), axis=AX,
                                   op=ALU.max, apply_absolute_value=True))
            chain(nv.tensor_scalar(ls[:, :], ls[:, :], 1e-12, 1.0 / QMAX, ALU.max, ALU.mult))
            chain(nv.reciprocal(linv[:, :], ls[:, :]))
            nv.memset(unr[:, :], -ROUND)
            dve.wait_ge(s["rsB_ps"], 1)
            chain(nv.tensor_copy(rsB[:, :], c.ps[1][:, 0:D]))

            def scaled(i, b):
                nv.tensor_scalar(r[b][:, :], c.lnk[:, ds(i * D, D)], linv[:, ds(i, 1)], QMAX,
                                 ALU.mult, ALU.min).then_inc(s["t_ok"], 1)
            scaled(0, 0)

            def step(t, b):
                if inside(t):
                    dve.wait_ge(s["t_ok"], t + 1)
                    nv.tensor_scalar(r[b][:, :], r[b][:, :], -QMAX, ROUND, ALU.max, ALU.add).then_inc(s["r_ok"], 1)
                if inside(t + 1):
                    wait(dve, s["q_ok"], t)
                    scaled(t + 1, 1 - b)
                if inside(t - 2):
                    dve.wait_ge(s["y_ps"], t - 1)
                    wait(dve, s["x_ok"], t - 3)
                    nv.scalar_tensor_tensor(out=c.acc[b][:, :], in0=c.ps[4 + b][:, 0:D], scalar=ls[:, ds(t - 2, 1)],
                                            in1=rsB[:, :], op0=ALU.mult, op1=ALU.mult).then_inc(s["y_ok"], 1)
                if inside(t - 4):
                    dve.wait_ge(s["x_ok"], t - 3)
                    nv.tensor_copy(c.m1[:, ds(t - 4, 1)], c.ones[:, 0:1])
                    nv.bn_stats(bst_of(c, t - 4), xt(c, t - 4))
            pipeline(dve, step, 0, 4, NT - 4, NT + 4, 4)

        @block.scalar
        def _(act):
            na = nc.scalar
            act_std(c, act, s["ve_ok"], s["std_ok"])
            act.wait_ge(s["rT_ps"], 1)
            na.activation(RQ[:, :, :].rearrange("p k n -> p (k n)"), c.ps[0].bitcast(BF16)[:, 0:KC * D],
                          ACT.Copy).then_inc(s["RQ_ok"], 1)

            def unround(i, b):
                act.wait_ge(s["r_ok"], i + 1)
                wait(act, s["qT_ps"], i - 1)
                na.activation(q[b][:, :], r[b][:, :], ACT.Identity, bias=unr[:, :]).then_inc(s["q_ok"], 1)

            def qT_copy(i, b):
                act.wait_ge(s["qT_ps"], i + 1)
                wait(act, s["y_ps"], i - 1)
                na.activation(qT[b][:, :], c.ps[6 + b].bitcast(BF16)[:, 0:D], ACT.Copy).then_inc(s["qT_ok"], 1)

            def step(t, b):
                if inside(t - 1):
                    qT_copy(t - 1, 1 - b)
                if inside(t):
                    unround(t, b)
            pipeline(act, step, 0, 4, NT, NT + 1, 4)

        @block.tensor
        def _(pe):
            nt = nc.tensor
            pe.wait_ge(s["rq_ok"], KC)
            rT = c.ps[0].bitcast(BF16)
            for k in range(KC):
                for m in range(KC):
                    last = nt.transpose(rT[:, k * D + m * P:k * D + (m + 1) * P], Rq[:, m, k * P:(k + 1) * P],
                                        c.identb[:, :])
            last.then_inc(s["rT_ps"], 1)
            for m in range(KC):
                last = nt.matmul(c.ps[1][:, m * P:(m + 1) * P], rsw[:, m, :], c.ident[:, :], start=True, stop=True)
            last.then_inc(s["rsB_ps"], 1)
            pe.wait_ge(s["RQ_ok"], 1)

            def transpose(i, b):
                pe.wait_ge(s["q_ok"], i + 1)
                wait(pe, s["qT_ok"], i - 1)
                for k in range(KC):
                    last = nt.transpose(c.ps[6 + b].bitcast(BF16)[:, k * P:(k + 1) * P],
                                        q[b][:, k * P:(k + 1) * P], c.identb[:, :])
                last.then_inc(s["qT_ps"], 1)

            def product(i, b):
                pe.wait_ge(s["qT_ok"], i + 1)
                wait(pe, s["y_ok"], i - 1)
                for k in range(KC):
                    last = nt.matmul(c.ps[4 + b][:, 0:D], qT[b][:, k * P:(k + 1) * P], RQ[:, k, :],
                                     start=(k == 0), stop=(k == KC - 1))
                last.then_inc(s["y_ps"], 1)

            def step(t, b):
                if inside(t):
                    transpose(t, b)
                if inside(t - 1):
                    product(t - 1, 1 - b)
            pipeline(pe, step, 0, 4, NT, NT + 1, 4)


def attn1(c, d):
    nc = c.nc
    maskT = c.maskT
    ctxs = sb(c, "b_ctxs", [P, KC, B * SK])
    gam, bet = sb(c, "b_gam", [P, D]), sb(c, "b_bet", [P, D])
    bsty, nmean = sb(c, "b_bsty", [P, NT * 6]), sb(c, "b_nmean", [P, NT])
    nmx, rsum, rd = ([sb(c, f"b_{n}{b}", [P, 1]) for b in range(2)] for n in ("nmx", "rsum", "rd"))
    s = sems(c, "b_", *NORM, "w_in", "rd_ok", "nmean_ok", "centred", "ctxs_ok", "s_ps", "nmax_ok", "exp_ok", "pT_ps", "pT_ok",
             "pv_ps", "y_ok", "yst", "z_ok", "x_ok", "biased")
    with nc.Block() as block:
        @block.sync
        def _(sp):
            sp.dma_start(gam[:, :], d["L2_xattn_gamma"].partition_broadcast(P)).then_inc(s["w_in"], 16)
            sp.dma_start(bet[:, :], d["L2_xattn_beta"].partition_broadcast(P)).then_inc(s["w_in"], 16)

        @block.gpsimd
        def _(pool):
            pool.wait_ge(s["w_in"], 32)

            def step(i, b):
                pool.wait_ge(s["ln_ok"], i + 1)
                nc.gpsimd.tensor_tensor(xt(c, i), xt(c, i), bet[:, :], ALU.add).then_inc(s["biased"], 1)
            pipeline(pool, step, 0, 0, NT, NT, 4)
            pool.wait_ge(s["biased"], NT)

            def add(i, b):
                pool.wait_ge(s["z_ok"], i + 1)
                nc.gpsimd.tensor_tensor(xt(c, i), xt(c, i), c.acc[b][:, :], ALU.add).then_inc(s["x_ok"], 1)
            pipeline(pool, add, 0, 0, NT, NT, 4)

        @block.vector
        def _(dve):
            nv = nc.vector
            chain = Chain(dve, s["chain"])
            nv.tensor_scalar(ctxs[:, :, :], c.ctxT[:, :, :], float(D) ** -0.5, None, ALU.mult).then_inc(s["ctxs_ok"], 1)
            dve_rstd(c, dve, chain, s["ve_ok"], s["std_ok"])

            def layer_norm(i, b):
                wait(dve, s["lnT_ps"], i - 1)
                nv.tensor_scalar(c.ln[b][:, :], xt(c, i), mean_of(c, i), rstd_of(c, i),
                                 ALU.subtract, ALU.mult).then_inc(s["ln_ok"], 1)

            def negative_max(i, b):
                dve.wait_ge(s["s_ps"], i + 1)
                wait(dve, s["exp_ok"], i - 1)
                nv.tensor_reduce(out=nmx[b][:, :], in_=c.ps[b][:, 0:SK], axis=AX, op=ALU.max,
                                 negate=True).then_inc(s["nmax_ok"], 1)

            def recip(i, b):
                dve.wait_ge(s["exp_ok"], i + 1)
                nv.reciprocal(rd[b][:, :], rsum[b][:, :]).then_inc(s["rd_ok"], 1)

            def weighted(i, b):
                dve.wait_ge(s["pv_ps"], i + 1)
                dve.wait_ge(s["rd_ok"], i + 1)
                nv.tensor_scalar(c.lnk[:, ds(i * D, D)], c.ps[4 + b][:, 0:D], rd[b][:, :], None,
                                 ALU.mult).then_inc(s["y_ok"], 1)
            layer_norm(0, 0)
            layer_norm(1, 1)

            layer_norm(2, 0)

            def step(t, b):
                if inside(t):
                    negative_max(t, b)
                if inside(t - 1):
                    recip(t - 1, 1 - b)
                if inside(t + 3):
                    layer_norm(t + 3, 1 - b)
                if inside(t - 2):
                    weighted(t - 2, b)
                    dve.wait_ge(s["y_ok"], t - 1)
                    nv.tensor_copy(c.gap[:, b:b + 1], c.ones[:, 0:1])
                    nv.bn_stats(bsty[:, ds(t * 6 - 12, 6)], c.lnk[:, ds(t * D - 2 * D, D)]).then_inc(s["yst"], 1)
            pipeline(dve, step, 0, 4, NT - 4, NT + 2, 4)
            chain.at(CH0)
            dve.wait_ge(s["yst"], NT)
            dve_rstd(c, dve, chain, s["ve_ok"], s["std_ok"], bsty)
            nv.tensor_scalar(nmean[:, :], c.mean[:, :], -1.0, None, ALU.mult).then_inc(s["nmean_ok"], 1)
            dve.wait_ge(s["w_in"], 32)

            def finish(t, b):
                if inside(t):
                    dve.wait_ge(s["centred"], t + 1)
                    wait(dve, s["x_ok"], t - 1)
                    nv.scalar_tensor_tensor(out=c.acc[b][:, :], in0=c.ln[b][:, :], scalar=rstd_of(c, t),
                                            in1=gam[:, :], op0=ALU.mult, op1=ALU.mult).then_inc(s["z_ok"], 1)
                if inside(t - 2):
                    dve.wait_ge(s["x_ok"], t - 1)
                    nv.tensor_copy(c.m1[:, ds(t - 2, 1)], c.ones[:, 0:1])
                    nv.bn_stats(bst_of(c, t - 2), xt(c, t - 2))
            pipeline(dve, finish, 0, 4, NT, NT + 2, 4)

        @block.scalar
        def _(act):
            na = nc.scalar
            act_std(c, act, s["ve_ok"], s["std_ok"])

            def lnT_copy(i, b):
                act.wait_ge(s["lnT_ps"], i + 1)
                wait(act, s["s_ps"], i - 1)
                na.activation(c.lnT[b][:, :], c.ps[6 + b][:, 0:D], ACT.Copy).then_inc(s["lnT_ok"], 1)

            def exps(i, b):
                act.wait_ge(s["nmax_ok"], i + 1)
                wait(act, s["pT_ps"], i - 1)
                wait(act, s["rd_ok"], i - 1)
                na.activation(c.prob[b][:, 0:SK], c.ps[b][:, 0:SK], ACT.Exp, bias=nmx[b][:, :],
                              accum_out=rsum[b][:, :]).then_inc(s["exp_ok"], 1)

            def pT_copy(i, b):
                act.wait_ge(s["pT_ps"], i + 1)
                wait(act, s["pv_ps"], i - 1)
                na.activation(c.pT[b][0:SK, 0:P], c.ps[2 + b][0:SK, 0:P], ACT.Copy).then_inc(s["pT_ok"], 1)
            lnT_copy(0, 0)
            lnT_copy(1, 1)

            def step(t, b):
                if inside(t - 1):
                    pT_copy(t - 1, 1 - b)
                if inside(t + 2):
                    lnT_copy(t + 2, b)
                if inside(t):
                    exps(t, b)
            pipeline(act, step, 0, 4, NT - 4, NT + 1, 4)
            act_std(c, act, s["ve_ok"], s["std_ok"], 2)
            act.wait_ge(s["nmean_ok"], 1)

            def centre(i, b):
                wait(act, s["z_ok"], i - 1)
                na.activation(c.ln[b][:, :], c.lnk[:, ds(i * D, D)], ACT.Identity, bias=nmean[:, ds(i, 1)]
                              ).then_inc(s["centred"], 1)
            pipeline(act, centre, 0, 4, NT, NT, 4)

        @block.tensor
        def _(pe):
            nt = nc.tensor
            pe.wait_ge(s["ctxs_ok"], 1)

            def lnT(i, b):
                pe.wait_ge(s["ln_ok"], i + 1)
                wait(pe, s["lnT_ok"], i - 1)
                for k in range(KC):
                    last = nt.transpose(c.ps[6 + b][:, k * P:(k + 1) * P], c.ln[b][:, k * P:(k + 1) * P], c.ident[:, :])
                last.then_inc(s["lnT_ps"], 1)

            def scores(i, b, q0):
                pe.wait_ge(s["lnT_ok"], i + 1)
                wait(pe, s["exp_ok"], i - 1)
                for k in range(KC):
                    nt.matmul(c.ps[b][:, 0:SK], c.lnT[b][:, k * P:(k + 1) * P], ctxs[:, k, b * SK:(b + 1) * SK],
                              start=(k == 0), stop=False)
                nt.matmul(c.ps[b][:, 0:SK], maskT[:, ds(q0, P)], c.tiledI[:, 0:SK],
                          start=False, stop=True).then_inc(s["s_ps"], 1)

            def prob_transpose(i, b):
                pe.wait_ge(s["exp_ok"], i + 1)
                wait(pe, s["pT_ok"], i - 1)
                nt.transpose(c.ps[2 + b][0:SK, 0:P], c.prob[b][:, 0:SK], c.ident[:, :]).then_inc(s["pT_ps"], 1)

            def weighted_values(i, b):
                pe.wait_ge(s["pT_ok"], i + 1)
                wait(pe, s["y_ok"], i - 1)
                nt.matmul(c.ps[4 + b][:, 0:D], c.pT[b][0:SK, 0:P], c.ctxn[:, b, :], start=True,
                          stop=True).then_inc(s["pv_ps"], 1)
            lnT(0, 0)
            lnT(1, 1)

            def step(t, b):
                if inside(t):
                    q0 = b * S + (t // 2) * P if is_static(t) else t * (P // 2) + (b * S - b * (P // 2))
                    scores(t, b, q0)
                if inside(t - 1):
                    prob_transpose(t - 1, 1 - b)
                if inside(t + 2):
                    lnT(t + 2, b)
                if inside(t - 2):
                    weighted_values(t - 2, b)
            pipeline(pe, step, 0, 4, NT - 4, NT + 2, 4)


def moe2(c, d):
    nc = c.nc
    WG, WU = sb(c, "m2_WG", [P, KC, 8 * P]), sb(c, "m2_WU", [P, KC, 8 * P])
    WD = sb(c, "m2_WD", [P, 8 * D])
    gw, gb = sb(c, "m2_gw", [P, KC, 8]), sb(c, "m2_gb", [P, 8])
    gs, gkeep, gl2, gt = (sb(c, "m2_" + n, [P, NT * 4]) for n in ("gs", "gkeep", "gl2", "gt"))
    sig, sg, hid = ([sb(c, f"m2_{n}{b}", [P, 512]) for b in range(2)] for n in ("sig", "sg", "hid"))
    s = sems(c, "m2_", *NORM, "w_in", "logits_ps", "scores_ok", "lg_used", "gates_ok", "gu_ps", "sig_ok", "sg_ok",
             "hid_ok", "down_ps", "acc")
    CH = NT // 4
    with nc.Block() as block:
        @block.sync
        def _(sp):
            sp.dma_start(gw[:, :, :], d["L2_ffn_gate_weightT"].rearrange("(k p) e -> p k e", p=P)).then_inc(s["router_in"], 16)
            sp.dma_start(gb[:, :], d["L2_ffn_e_score_correction_bias"].partition_broadcast(P)).then_inc(s["router_in"], 16)
            for k in range(KC):
                for W, name in ((WG, "gate_projT"), (WU, "up_projT")):
                    sp.dma_start(W[:, k, :], d["L2_ffn_" + name][k * P:(k + 1) * P, :]).then_inc(s["w_in"], 16)
            sp.dma_start(WD[:, :], d["L2_ffn_down_projT"]).then_inc(s["w_in"], 16)
            Wk3, Wv3 = gqa_kv_weights(c)
            sp.dma_start(Wk3, d["L3_xattn_Wk"].rearrange("(k p) n -> p k n", p=P)).then_inc(c.w_in, 16)
            wv = d["L3_xattn_Wv"].rearrange("(k p) (g e) -> p k g e", p=P, g=G)
            for k in range(KC):
                for r in range(2):
                    sp.dma_start(Wv3[:, k, :, r, :], wv[:, k, :, :]).then_inc(c.w_in, 16)

        @block.vector
        def _(dve):
            nv = nc.vector
            chain = Chain(dve, s["chain"])
            dve_ln_all(c, dve, s, chain, c.lnk)
            dve_logits(c, dve, s)
            dve.wait_ge(s["logits_ps"], 1)
            nv.tensor_copy(c.lg[:, :], c.ps[5][:, 0:NT * 8]).then_inc(s["lg_used"], 1)
            dve.wait_ge(s["scores_ok"], 1)
            score, choice, gates = g8(c.lg), g8(c.choice), g8(c.gates)
            chain(nv.tensor_tensor(choice, score, gb[:, :].unsqueeze(1).to_broadcast([P, NT, 8]), ALU.add))
            pairs = c.choice[:, :].rearrange("p (g two) -> p g two", two=2)
            chain(nv.tensor_tensor(gs[:, :], pairs[:, :, 0], pairs[:, :, 1], ALU.add))
            g4 = lambda t: t[:, :].rearrange("p (i g) -> p i g", g=4)
            top2(c, chain, g4(gs), 4, g4(gkeep), g4(gl2), g4(gt), c.m1[:, :])
            chain(nv.tensor_tensor(pairs, pairs, gkeep[:, :].unsqueeze(2).to_broadcast([P, NT * 4, 2]), ALU.mult))
            top2(c, chain, choice, 8, gates, g8(c.lg2), g8(c.lgt), c.m1[:, :])
            chain(nv.tensor_tensor(gates, gates, score, ALU.mult))
            chain(nv.reduce_sum(c.m1[:, :], gates, AX))
            chain(nv.tensor_scalar(c.m1[:, :], c.m1[:, :], 1e-20, None, ALU.add))
            chain(nv.reciprocal(c.m1[:, :], c.m1[:, :]))
            chain(nv.tensor_tensor(gates, gates, bc(c.m1[:, :], 8), ALU.mult))

            def activate(n, b):
                dve.wait_ge(s["sig_ok"], n + 1)
                nv.tensor_tensor(sg[b][:, :], c.ps[b][:, :], sig[b][:, :], ALU.mult).then_inc(s["sg_ok"], 1)
                wait(dve, s["down_ps"], n - 1)
                dve.wait_ge(s["sg_ok"], n + 1)
                nv.tensor_tensor(hid[b][:, :], c.ps[2 + b][:, :], sg[b][:, :], ALU.mult).then_inc(s["hid_ok"], 1)

            def accumulate(n, tile0, e, b):
                dve.wait_ge(s["down_ps"], n + 1)
                wait(dve, s["acc"], n * 4)
                for j in range(4):
                    xj = c.x[:, ds(tile0 * D + j * D, D)]
                    nv.scalar_tensor_tensor(out=xj, in0=c.ps[4 + 2 * b + j // 2][:, (j % 2) * D:(j % 2 + 1) * D],
                                            scalar=c.gates[:, ds(tile0 * 8 + (j * 8 + e), 1)], in1=xj,
                                            op0=ALU.mult, op1=ALU.add).then_inc(s["acc"], 1)
                if e == 7:
                    dve.wait_ge(s["acc"], n * 4 + 4)
                    nv.tensor_copy(c.gap[:, 0:1], c.ones[:, 0:1])
                    for j in range(4):
                        nv.bn_stats(bst_of(c, tile0 + j), c.x[:, ds(tile0 * D + j * D, D)])

            def chunk(t):
                for e in range(8):
                    activate(t * 8 + e, e % 2)
                    if e:
                        accumulate(t * 8 + (e - 1), t * 4, e - 1, (e - 1) % 2)
                    elif not is_static(t) or t:
                        accumulate(t * 8 - 1, t * 4 - 4, 7, 1)
            chunk(0)
            with dve.Fori(1, CH) as t:
                chunk(t)
            accumulate(8 * CH - 1, 4 * CH - 4, 7, 1)

        @block.scalar
        def _(act):
            na = nc.scalar
            act_ln_all(c, act, s)
            act.wait_ge(s["lg_used"], 1)
            na.activation(c.lg[:, :], c.lg[:, :], ACT.Sigmoid).then_inc(s["scores_ok"], 1)

            def chunk(t):
                for e in range(8):
                    b = e % 2
                    n = t * 8 + e
                    act.wait_ge(s["gu_ps"], n + 1)
                    wait(act, s["sg_ok"], n - 1)
                    na.activation(sig[b][:, :], c.ps[b][:, :], ACT.Sigmoid).then_inc(s["sig_ok"], 1)
            chunk(0)
            with act.Fori(1, CH) as t:
                chunk(t)

        @block.tensor
        def _(pe):
            nt = nc.tensor
            pe_ln_all(c, pe, s, gw, 16 * 2, c.lnk)
            pe.wait_ge(s["w_in"], 16 * 5)

            def gate_up(n, t, e, b):
                wait(pe, s["hid_ok"], n - 1)
                for W, bank in ((WG, b), (WU, 2 + b)):
                    for k in range(KC):
                        last = nt.matmul(c.ps[bank][:, :], W[:, k, e * P:(e + 1) * P],
                                         c.lnT_all[:, k, ds(t * 512, 512)], start=(k == 0), stop=(k == KC - 1))
                last.then_inc(s["gu_ps"], 1)

            def down(n, e, b):
                pe.wait_ge(s["hid_ok"], n + 1)
                wait(pe, s["acc"], n * 4 - 4)
                for j in range(4):
                    last = nt.matmul(c.ps[4 + 2 * b + j // 2][:, (j % 2) * D:(j % 2 + 1) * D],
                                     hid[b][:, j * P:(j + 1) * P], WD[:, e * D:(e + 1) * D], start=True, stop=True)
                last.then_inc(s["down_ps"], 1)
            pe.wait_ge(s["lg_used"], 1)

            def chunk(t):
                for e in range(8):
                    gate_up(t * 8 + e, t, e, e % 2)
                    if e:
                        down(t * 8 + (e - 1), e - 1, (e - 1) % 2)
                    elif not is_static(t) or t:
                        down(t * 8 - 1, 7, 1)
            chunk(0)
            with pe.Fori(1, CH) as t:
                chunk(t)
            down(8 * CH - 1, 7, 1)


HB, DH, G = 16, 64, 4
HPG = HB // G
NB = -(-HB * SK // P)
LASTB = HB * SK - (NB - 1) * P


def gqa_kv_weights(c):
    return c.W[0], c.Wall[:, KC * D:3 * KC * D].rearrange("p (k g r e) -> p k g r e", k=KC, g=G, r=2)


def pipeline4(eng, step, first, lo, hi, last):
    for t in range(first, lo):
        step(t, t % 4)
    with eng.Fori(0, (hi - lo) // 4) as j:
        for u in range(4):
            step(j * 4 + (lo + u), (lo + u) % 4)
    for t in range(hi, last):
        step(t, t % 4)


def attn_gqa(c, d):
    nc = c.nc
    Wq = sb(c, "g_Wq", [P, KC, HB * DH])
    Wk, Wv = gqa_kv_weights(c)
    Wo = sb(c, "g_Wo", [P, HB // 2, D])
    C, Sn = sb(c, "g_cos", [P, S // P, DH]), sb(c, "g_sin", [P, S // P, DH])
    mraw = sb(c, "g_mraw", [1, 40], I32)
    mrow = sb(c, "g_mrow", [1, B * SK])
    mtile = sb(c, "g_mtile", [1, B, HPB, SK], BF16)
    ones = sb(c, "g_ones", [1, P], BF16)
    KR = sb(c, "g_KR", [SK, B, G, 2, DH])
    KB = sb(c, "g_KB", [P, B, G, 2, SK])
    VT = sb(c, "g_VT", [P, G, B * SK])
    VW = sb(c, "g_VW", [P, B, NB, D])
    bias = [sb(c, f"g_bias{j}", [P, HB * SK]) for j in range(2)]
    t1, t2, qr = (sb(c, "g_" + n, [P, HB * DH]) for n in ("t1", "t2", "qr"))
    qT = [sb(c, f"g_qT{b}", [P, HB * DH]) for b in range(2)]
    rden = [sb(c, f"g_rden{b}", [P, HB]) for b in range(2)]
    VWs = [c.lnk[0:SK, :].rearrange("k (h n) -> k h n", h=HB),
           c.lnT_all[0:SK, :, :].rearrange("k a (h n) -> k (a h) n", n=D)]
    vw_dram = nc.dram_tensor("vw_scratch", (B, HB * SK, D), F32, kind="Internal").ap()
    s = sems(c, "g_", *NORM, "kv_in", "w_in", "k_ps", "vT_ps", "kr_chain", "kr_ok", "krT_ps", "kb_ok", "vT_ok", "vw_ps",
             "vwa_ok", "vwd_ok", "vw_out", "vw_in", "m_ok", "q_ps", "roped", "rope_ok", "qT_ps", "qT_ok", "s_ps",
             "s_used", "shifted", "exp_ok", "rd_ok", "p_ok", "pT_ps", "pT_ok", "y_ps", "x_ok", "bias0_in", "bias1_in", "links")
    bias_in = [s["bias0_in"], s["bias1_in"]]
    sview = c.psall[:, 0:3 * 512].rearrange("p (b n) -> p b n", b=3)
    qview = c.psall[:, 3 * 512:5 * 512].rearrange("p (h e) -> p h e", e=DH)
    ring = [c.ps[5], c.ps[6]]
    bank_y = c.ps[7]
    heads = lambda t: t[:, 0:HB * SK].rearrange("p (h k) -> p h k", k=SK)
    jof = lambda i, b, n: (i // 2) * n if is_static(i) else i * (n // 2) - b * (n // 2)

    with nc.Block() as block:
        @block.sync
        def _(sp):
            sp.dma_start(C[:, :, :], d["c_cos"].rearrange("(j p) e -> p j e", p=P)).then_inc(s["kv_in"], 16)
            sp.dma_start(Sn[:, :, :], d["c_sin"].rearrange("(j p) e -> p j e", p=P)).then_inc(s["kv_in"], 16)
            sp.dma_start(mraw[:, :], d["mask3"]).then_inc(s["kv_in"], 16)
            sp.dma_start(Wo[:, :, :], d["L3_xattn_Wo"].rearrange("(m p) n -> p m n", p=P)).then_inc(s["w_in"], 16)
            for k in range(KC):
                sp.dma_start(Wq[:, k, :], d["L3_xattn_Wq"][k * P:(k + 1) * P, :]).then_inc(s["w_in"], 16)
            for j in range(2):
                sp.dma_start(bias[j][:, :], d["rel_bias"][j * P:(j + 1) * P, :]).then_inc(bias_in[j % 2], 16)
            for b in range(B):
                sp.wait_ge(s["vwa_ok"], 4 * (b + 1))
                sp.wait_ge(s["vwd_ok"], 4 * (b + 1))
                sp.dma_start(vw_dram[b].rearrange("(h k) n -> k h n", k=SK), VWs[b]).then_inc(s["vw_out"], 16)
            for b in range(B):
                sp.wait_ge(s["vw_out"], 16 * B)
                sp.dma_start(VW[:, b, 0:NB - 1, :], vw_dram[b, 0:(NB - 1) * P, :].rearrange("(j p) n -> p j n", p=P)
                             ).then_inc(s["vw_in"], 16)
                sp.dma_start(VW[0:LASTB, b, NB - 1, :], vw_dram[b, (NB - 1) * P:HB * SK, :]).then_inc(s["vw_in"], 16)
            for j in range(2, S // P):
                sp.wait_ge(s["s_used"], 2 * j - 2)
                sp.dma_start(bias[j % 2][:, :], d["rel_bias"][j * P:(j + 1) * P, :]).then_inc(bias_in[j % 2], 16)

        @block.gpsimd
        def _(pool):
            ng = nc.gpsimd

            def step(t, q):
                b = q % 2
                if inside(t + 1):
                    i = t + 1
                    pool.wait_ge(s["roped"], i + 1)
                    wait(pool, s["qT_ps"], i * 2)
                    ng.tensor_tensor(qr[:, :], t1[:, :], t2[:, :], ALU.add).then_inc(s["rope_ok"], 1)
                if inside(t):
                    pool.wait_ge(s["rd_ok"], t + 1)
                    ng.tensor_tensor(heads(c.prob[b]), heads(c.prob[b]),
                                     rden[b][:, :].unsqueeze(2).to_broadcast([P, HB, SK]), ALU.mult).then_inc(s["p_ok"], 1)
            pipeline4(pool, step, -1, 2, NT - 2, NT)

        @block.vector
        def _(dve):
            nv = nc.vector
            chain = Chain(dve, s["chain"])
            kr = Chain(dve, s["kr_chain"])
            dve_rstd(c, dve, chain, s["ve_ok"], s["std_ok"])

            def layer_norm(i, b):
                wait(dve, s["lnT_ps"], i - 1)
                nv.tensor_scalar(c.ln[b][:, :], xt(c, i), mean_of(c, i), rstd_of(c, i),
                                 ALU.subtract, ALU.mult).then_inc(s["ln_ok"], 1)
            layer_norm(0, 0)
            dve.wait_ge(s["kv_in"], 16 * 3)
            kr(nv.tensor_scalar(mrow[:, :], mraw[:, :].bitcast(U8)[:, 0:B * SK], 0.0, NEG, ALU.is_equal, ALU.mult))
            nv.tensor_copy(mtile[:, :, :, :], mrow[:, :].rearrange("a (b k) -> a b k", b=B).unsqueeze(2)
                           .to_broadcast([1, B, HPB, SK]))
            nv.memset(ones[:, :], 1.0).then_inc(s["m_ok"], 1)
            dve.wait_ge(s["k_ps"], 1)
            half = DH // 2
            for b in range(B):
                k = c.ps[b][0:SK, 0:G * DH].rearrange("k (g e) -> k g e", g=G)
                a1 = t1[0:SK, b * 256:b * 256 + 256].rearrange("k (g e) -> k g e", g=G)
                a2 = t2[0:SK, b * 256:b * 256 + 256].rearrange("k (g e) -> k g e", g=G)
                bcg = lambda ap: ap.unsqueeze(1).to_broadcast([SK, G, ap.shape[-1]])
                nv.tensor_tensor(a1, k, bcg(C[0:SK, 0, :]), ALU.mult)
                nv.tensor_tensor(a2[:, :, 0:half], k[:, :, half:DH], bcg(Sn[0:SK, 0, 0:half]), ALU.mult)
                kr(nv.tensor_tensor(a2[:, :, half:DH], k[:, :, 0:half], bcg(Sn[0:SK, 0, half:DH]), ALU.mult))
                for r in range(2):
                    nv.tensor_tensor(KR[:, b, :, r, :], a1, a2, ALU.add).then_inc(s["kr_ok"], 1)
            for b in range(B):
                dve.wait_ge(s["krT_ps"], b + 1)
                for g in range(G):
                    for r in range(2):
                        last = nv.tensor_scalar(KB[:, b, g, r, :], c.ps[6 + b][:, g * SK:(g + 1) * SK],
                                                c.hmask2[:, r:r + 1], DH ** -0.5, ALU.mult, ALU.mult)
                last.then_inc(s["kb_ok"], 1)
            for n in range(8):
                dve.wait_ge(s["vw_ps"], n + 1)
                h = 4 * (n % 4) + 1
                nv.tensor_copy(VWs[n // 4][:, h:h + 3:2, :],
                               c.ps[2 * (n % 2) + 1][0:SK, :].rearrange("k (a n) -> k a n", a=2)).then_inc(s["vwd_ok"], 1)

            def rope(i, b):
                dve.wait_ge(s["q_ps"], i + 1)
                wait(dve, s["rope_ok"], i)
                cs = C[:, :, :].rearrange("p j e -> p (j e)")
                sn = Sn[:, :, :].rearrange("p j e -> p (j e)")
                o = jof(i, b, DH)
                a1, a2 = (t[:, :].rearrange("p (h e) -> p h e", e=DH) for t in (t1, t2))
                bch = lambda ap: ap.unsqueeze(1).to_broadcast([P, HB, ap.shape[-1]])
                nv.tensor_tensor(a1, qview, bch(cs[:, ds(o, DH)]), ALU.mult)
                nv.tensor_tensor(a2[:, :, 0:half], qview[:, :, half:DH], bch(sn[:, ds(o, half)]), ALU.mult)
                nv.tensor_tensor(a2[:, :, half:DH], qview[:, :, 0:half], bch(sn[:, ds(o + half, half)]),
                                 ALU.mult).then_inc(s["roped"], 1)

            links = Chain(dve, s["links"])

            def shift(t, q):
                b, jb = q % 2, (q // 2) % 2
                p = heads(c.prob[b])
                dve.wait_ge(s["s_ps"], t + 1)
                dve.wait_ge(bias_in[jb], 16 * (t // 4 + 1) if is_static(t) else t * 4 + (16 - 4 * q))
                wait(dve, s["pT_ps"], t * 3 - 3)
                n = HPB * SK
                nv.tensor_tensor(c.prob[b][:, 0:2 * n].rearrange("p (q n) -> p q n", q=2), sview[:, 0:2, 0:n],
                                 bias[jb][:, 0:2 * n].rearrange("p (q n) -> p q n", q=2), ALU.add)
                nv.tensor_tensor(c.prob[b][:, 2 * n:HB * SK], sview[:, 2, 0:4 * SK], bias[jb][:, 2 * n:HB * SK],
                                 ALU.add).then_inc(s["s_used"], 1)
                dve.wait_ge(s["s_used"], t + 1)
                links(nv.reduce_max(c.mx[:, :], p, AX))
                nv.tensor_tensor(p, p, c.mx[:, :].unsqueeze(2).to_broadcast([P, HB, SK]),
                                 ALU.subtract).then_inc(s["shifted"], 1)

            def residual(i, b):
                dve.wait_ge(s["y_ps"], i + 1)
                nv.tensor_tensor(xt(c, i), xt(c, i), bank_y[:, 0:D], ALU.add).then_inc(s["x_ok"], 1)

            def sums(t, b):
                dve.wait_ge(s["exp_ok"], t + 1)
                wait(dve, s["p_ok"], t - 1)
                links(nv.reduce_sum(c.den[:, :], heads(c.prob[b]), AX))
                nv.reciprocal(rden[b][:, :], c.den[:, :]).then_inc(s["rd_ok"], 1)

            layer_norm(1, 1)

            def step(t, q):
                b = q % 2
                links.at(2 * max(0, min(t, NT)) if is_static(t) else t * 2)
                if inside(t + 1):
                    rope(t + 1, 1 - b)
                if inside(t):
                    shift(t, q)
                if inside(t - 1):
                    residual(t - 1, 1 - b)
                    dve.wait_ge(s["x_ok"], t)
                if inside(t + 3):
                    layer_norm(t + 3, 1 - b)
                if inside(t - 1):
                    nv.tensor_copy(c.gap[:, b:b + 1], c.ones[:, 0:1])
                    nv.bn_stats(bst_of(c, t - 1), xt(c, t - 1))
                if inside(t):
                    sums(t, b)
            pipeline4(dve, step, -1, 1, NT - 3, NT + 1)

        @block.scalar
        def _(act):
            na = nc.scalar
            act_std(c, act, s["ve_ok"], s["std_ok"])
            act.wait_ge(s["vT_ps"], 1)
            for g in range(G):
                last = na.activation(VT[:, g, :], c.ps[2 + g][:, 0:B * SK], ACT.Copy)
            last.then_inc(s["vT_ok"], 1)
            for n in range(8):
                act.wait_ge(s["vw_ps"], n + 1)
                h = 4 * (n % 4)
                na.activation(VWs[n // 4][:, h:h + 3:2, :],
                              c.ps[2 * (n % 2)][0:SK, :].rearrange("k (a n) -> k a n", a=2),
                              ACT.Copy).then_inc(s["vwa_ok"], 1)

            def lnT_copy(i, b):
                act.wait_ge(s["lnT_ps"], i + 1)
                wait(act, s["q_ps"], i - 1)
                na.activation(c.lnT[b][:, :], ring[1][:, 0:D], ACT.Copy).then_inc(s["lnT_ok"], 1)

            def qT_copy(i, b):
                wait(act, s["s_ps"], i - 1)
                for u in range(2):
                    act.wait_ge(s["qT_ps"], i * 2 + (u + 1))
                    na.activation(qT[b][:, u * 512:(u + 1) * 512], ring[u][:, :], ACT.Copy).then_inc(s["qT_ok"], 1)

            def exps(t, b):
                act.wait_ge(s["shifted"], t + 1)
                na.activation(c.prob[b][:, :], c.prob[b][:, :], ACT.Exp).then_inc(s["exp_ok"], 1)

            def pT_copy(i, b):
                wait(act, s["y_ps"], i - 1)
                for u in range(3):
                    act.wait_ge(s["pT_ps"], i * 3 + (u + 1))
                    if u < 2:
                        ins = na.activation(c.pT[b][:, u * 512:(u + 1) * 512], ring[u][:, :], ACT.Copy)
                    else:
                        na.activation(c.pT[b][:, 8 * P:9 * P], ring[0][:, 0:P], ACT.Copy)
                        ins = na.activation(c.pT[b][0:LASTB, 9 * P:10 * P], ring[0][0:LASTB, P:2 * P], ACT.Copy)
                    ins.then_inc(s["pT_ok"], 1)

            def step(t, q):
                b = q % 2
                if inside(t - 1):
                    pT_copy(t - 1, 1 - b)
                if inside(t + 2):
                    lnT_copy(t + 2, b)
                if inside(t):
                    exps(t, b)
                if inside(t + 1):
                    qT_copy(t + 1, 1 - b)
            pipeline4(act, step, -2, 2, NT - 2, NT + 1)

        @block.tensor
        def _(pe):
            nt = nc.tensor
            pe.wait_ge(c.w_in, 16 * (N_ATTN0 + N_ATTN1 + 1 + 2 * KC))
            for b in range(B):
                for k in range(KC):
                    last = nt.matmul(c.ps[b][0:SK, 0:G * DH], c.ctxT[:, k, b * SK:(b + 1) * SK], Wk[:, k, :],
                                     start=(k == 0), stop=(k == KC - 1))
            last.then_inc(s["k_ps"], 1)
            for g in range(G):
                for k in range(KC):
                    last = nt.matmul(c.ps[2 + g][:, 0:B * SK], Wv[:, k, g, :, :].rearrange("p r e -> p (r e)"),
                                     c.ctxT[:, k, :], start=(k == 0), stop=(k == KC - 1))
            last.then_inc(s["vT_ps"], 1)
            for b in range(B):
                pe.wait_ge(s["kr_ok"], 2 * (b + 1))
                for g in range(G):
                    last = nt.transpose(c.ps[6 + b][:, g * SK:(g + 1) * SK],
                                        KR[:, b, g, :, :].rearrange("k r e -> k (r e)"), c.ident[0:SK, 0:SK])
                last.then_inc(s["krT_ps"], 1)
            pe.wait_ge(s["vT_ok"], 1)
            pe.wait_ge(s["w_in"], 16 * (1 + KC))
            for n in range(8):
                b, m = n // 4, n % 4
                wait(pe, s["vwa_ok"], n - 1)
                wait(pe, s["vwd_ok"], n - 1)
                for r in range(2):
                    rows = slice(r * DH, (r + 1) * DH)
                    last = nt.matmul(c.ps[2 * (n % 2) + r][0:SK, :], VT[rows, m, b * SK:(b + 1) * SK],
                                     Wo[rows, 2 * m:2 * m + 2, :].rearrange("p a n -> p (a n)"),
                                     start=True, stop=True)
                last.then_inc(s["vw_ps"], 1)

            def lnT(i, b):
                pe.wait_ge(s["ln_ok"], i + 1)
                wait(pe, s["pT_ok"], i * 3 - 7)
                for k in range(KC):
                    last = nt.transpose(ring[1][:, k * P:(k + 1) * P], c.ln[b][:, k * P:(k + 1) * P], c.ident[:, :])
                last.then_inc(s["lnT_ps"], 1)

            def queries(i, b):
                pe.wait_ge(s["lnT_ok"], i + 1)
                wait(pe, s["roped"], i)
                for u in range(2):
                    for k in range(KC):
                        last = nt.matmul(c.ps[3 + u][:, :], c.lnT[b][:, k * P:(k + 1) * P],
                                         Wq[:, k, u * 512:(u + 1) * 512], start=(k == 0), stop=(k == KC - 1))
                last.then_inc(s["q_ps"], 1)

            def q_transpose(i, b):
                pe.wait_ge(s["rope_ok"], i + 1)
                for u in range(2):
                    if u == 0:
                        wait(pe, s["pT_ok"], i * 3 - 3)
                    else:
                        pe.wait_ge(s["lnT_ok"], min(i + 2, NT) if is_static(i) else i + 2)
                    for m in range(4):
                        last = nt.transpose(ring[u][:, m * P:(m + 1) * P], qr[:, (4 * u + m) * P:(4 * u + m + 1) * P],
                                            c.ident[:, :])
                    last.then_inc(s["qT_ps"], 1)

            def scores(t, b):
                pe.wait_ge(s["qT_ok"], t * 2 + 2)
                wait(pe, s["s_used"], t)
                for m in range(HB // 2):
                    o = (m % 3) * 2 * SK
                    nt.matmul(sview[:, m // 3, o:o + 2 * SK], qT[b][:, m * P:(m + 1) * P],
                              KB[:, b, m // 2, :, :].rearrange("p r k -> p (r k)"),
                              start=(m % 3 == 0), stop=False, skip_group_check=True)
                for q in range(3):
                    nh = HPB if q < 2 else 4
                    last = nt.matmul(sview[:, q, 0:nh * SK], ones[:, :],
                                     mtile[:, b, 0:nh, :].rearrange("a h k -> a (h k)"),
                                     start=False, stop=True, skip_group_check=True)
                last.then_inc(s["s_ps"], 1)

            def prob_transpose(i, b):
                pe.wait_ge(s["p_ok"], i + 1)
                for u in range(3):
                    if u < 2:
                        pe.wait_ge(s["qT_ok"], min(i * 2 + 3 + u, 2 * NT) if is_static(i) else i * 2 + (3 + u))
                    else:
                        pe.wait_ge(s["pT_ok"], i * 3 + 1)
                    for j in range(4 * u, min(4 * u + 4, NB)):
                        w = P if j < NB - 1 else LASTB
                        last = nt.transpose(ring[u % 2][0:w, (j % 4) * P:(j % 4 + 1) * P],
                                            c.prob[b][:, j * P:j * P + w], c.ident[:, :])
                    last.then_inc(s["pT_ps"], 1)

            def output(i, b):
                pe.wait_ge(s["pT_ok"], i * 3 + 3)
                wait(pe, s["x_ok"], i)
                for j in range(NB):
                    w = P if j < NB - 1 else LASTB
                    last = nt.matmul(bank_y[:, 0:D], c.pT[b][0:w, j * P:(j + 1) * P], VW[0:w, b, j, :],
                                     start=(j == 0), stop=(j == NB - 1))
                last.then_inc(s["y_ps"], 1)
            pe.wait_ge(s["kb_ok"], B)
            pe.wait_ge(s["m_ok"], 1)
            pe.wait_ge(s["vwa_ok"], 8)
            pe.wait_ge(s["vwd_ok"], 8)
            loaded = [False]

            def step(t, q):
                b = q % 2
                if inside(t):
                    scores(t, b)
                if inside(t - 1):
                    if not loaded[0]:
                        loaded[0] = True
                        pe.wait_ge(s["vw_in"], 64)
                    prob_transpose(t - 1, 1 - b)
                if inside(t + 2):
                    lnT(t + 2, b)
                if inside(t - 1):
                    output(t - 1, 1 - b)
                if inside(t + 1):
                    q_transpose(t + 1, 1 - b)
                if inside(t + 2):
                    queries(t + 2, b)
            pipeline4(pe, step, -2, 2, NT - 2, NT + 1)


E3, CAP, HF = 8, 320, 1024
OVB = -(-(T - CAP) // P)
XR = [(0, P), (P, P), (2 * P, CAP - 2 * P)]
MH = HF // P


def moe3(c, d):
    nc = c.nc
    rw, rb = sb(c, "x_rw", [P, KC, 8]), sb(c, "x_rb", [P, 8])
    ohb = sb(c, "x_ohb", [P, NT * 8], BF16)
    upper, onesb = sb(c, "x_upper", [P, P], BF16), sb(c, "x_onesb", [P, P], BF16)
    upf = sb(c, "x_upf", [P, P])
    base, rank8 = sb(c, "x_base", [P, NT * 8]), sb(c, "x_rank8", [P, NT * 8])
    rank, valid, over, slotf, obase = (sb(c, "x_" + n, [P, NT]) for n in ("rank", "valid", "over", "slotf", "obase"))
    overb = sb(c, "x_overb", [P, NT], BF16)
    slot = sb(c, "x_slot", [P, NT], U32)
    steps_, nbf = sb(c, "x_steps", [1, OVB]), sb(c, "x_nbf", [1, 2])
    nbi = sb(c, "x_nbi", [1, 1], I32)
    w1 = [sb(c, f"x_w1{b}", [P, KC, HF]) for b in range(2)]
    w2 = [sb(c, f"x_w2{b}", [P, MH, D]) for b in range(2)]
    ow1, ow2 = sb(c, "x_ow1", [P, KC, HF]), sb(c, "x_ow2", [P, MH, D])
    b1, ob1 = sb(c, "x_b1", [P, E3 * MH]), sb(c, "x_ob1", [P, MH])
    b2, ob2 = sb(c, "x_b2", [P, E3 * D]), sb(c, "x_ob2", [P, D])
    X = [sb(c, f"x_X{b}", [P, 3, D]) for b in range(2)]
    xT = [sb(c, f"x_xT{b}", [P, KC, CAP]) for b in range(2)]
    hT = [c.prob_pair[b][:, 0:MH * CAP].rearrange("p (m n) -> p m n", m=MH) for b in range(2)]
    yt = [sb(c, f"x_yt{b}", [P, 3, D]) for b in range(2)]
    Xo, xTo, yo = sb(c, "x_Xo", [P, D]), sb(c, "x_xTo", [P, D]), sb(c, "x_yo", [P, D])
    pgap = sb(c, "x_pgap", [P, 1])
    hTo = sb(c, "x_hTo", [P, MH, P])
    xd, yd = c.xd, c.yd
    s = sems(c, "x_", *NORM, "w_in", "ow_in", "w1a_in", "w1b_in", "w2a_in", "w2b_in", "xa_in", "xb_in",
             "logits_ps", "oh_ok", "pre_ps", "over_ok", "opre_ps", "slot_ok", "scat",
             "xT_ps", "xT_ok", "h_ps", "h_ok", "y_ps", "y_ok", "ya_out", "yb_out",
             "oX_in", "oT_ps", "oT_ok", "oh_ps", "ohid_ok", "oy_ps", "oy_ok", "o_out",
             "g0_in", "g1_in", "g2_in", "g3_in", "sum_ok", "out_done")
    w1_in, w2_in, x_in = [s["w1a_in"], s["w1b_in"]], [s["w2a_in"], s["w2b_in"]], [s["xa_in"], s["xb_in"]]
    y_out, g_in = [s["ya_out"], s["yb_out"]], [s["g0_in"], s["g1_in"], s["g2_in"], s["g3_in"]]
    OV0 = E3 * CAP
    order = [2 * q + b for b in range(B) for q in range(NT // B)]
    turns = lambda e: e // 2 if is_static(e) else e

    def count16(e, b, per):
        return 16 * per * (e // 2 + 1) if is_static(e) else e * (8 * per) + (16 * per - 8 * per * b)

    with nc.Block() as block:
        @block.sync
        def _(sp):
            sp.dma_start(rw[:, :, :], d["L3_ffn_router_w"].rearrange("(k p) e -> p k e", p=P)).then_inc(s["router_in"], 16)
            sp.dma_start(rb[:, :], d["L3_ffn_router_b"].partition_broadcast(P)).then_inc(s["router_in"], 16)
            sp.dma_start(upf[:, :], d["c_upper"]).then_inc(s["w_in"], 16)
            sp.dma_start(steps_[:, :], d["c_steps"]).then_inc(s["w_in"], 16)
            sp.dma_start(b1[:, :], d["L3_ffn_b1T"]).then_inc(s["w_in"], 16)
            sp.dma_start(ob1[:, :], d["L3_ffn_ob1T"]).then_inc(s["w_in"], 16)
            sp.dma_start(b2[:, :], d["L3_ffn_b2"].rearrange("e n -> (e n)").partition_broadcast(P)).then_inc(s["w_in"], 16)
            sp.dma_start(ob2[:, :], d["L3_ffn_ob2"].partition_broadcast(P)).then_inc(s["w_in"], 16)

            def load_w1(e, b):
                for k in range(KC):
                    sp.dma_start(w1[b][:, k, :], d["L3_ffn_w1"][ds(e * D + k * P, P), :]).then_inc(w1_in[b], 16)

            def load_w2(e, b):
                sp.dma_start(w2[b][:, :, :], d["L3_ffn_w2"][ds(e * HF, HF), :].rearrange("(m p) n -> p m n", p=P)
                             ).then_inc(w2_in[b], 16)

            def load_x(e, b):
                sp.dma_start(X[b][:, 0:2, :], xd[ds(e * CAP, 2 * P), :].rearrange("(r p) n -> p r n", p=P)
                             ).then_inc(x_in[b], 16)
                sp.dma_start(X[b][0:CAP - 2 * P, 2, :], xd[ds(e * CAP + 2 * P, CAP - 2 * P), :]).then_inc(x_in[b], 16)
            for e in range(2):
                load_w1(e, e)
                load_w2(e, e)
            for k in range(KC):
                sp.dma_start(ow1[:, k, :], d["L3_ffn_ow1"][k * P:(k + 1) * P, :]).then_inc(s["ow_in"], 16)
            sp.dma_start(ow2[:, :, :], d["L3_ffn_ow2"].rearrange("(m p) n -> p m n", p=P)).then_inc(s["ow_in"], 16)
            sp.wait_ge(s["scat"], 16 * NT)
            for e in range(2):
                load_x(e, e)

            def store_y(e, b):
                for r, (r0, n) in enumerate(XR):
                    sp.wait_ge(s["y_ok"], e * 3 + (r + 1))
                    sp.dma_start(yd[ds(e * CAP + r0, n), :], yt[b][0:n, r, :]).then_inc(y_out[b], 16)

            def step(e, b):
                if not is_static(e) or e + 2 < E3:
                    sp.wait_ge(s["xT_ps"], e + 1)
                    load_x(e + 2, b)
                    sp.wait_ge(s["h_ps"], e * 8 + 8)
                    load_w1(e + 2, b)
                store_y(e, b)
                if not is_static(e) or e + 2 < E3:
                    sp.wait_ge(s["y_ps"], e * 3 + 3)
                    load_w2(e + 2, b)
            pipeline(sp, step, 0, 0, E3 - 2, E3)

            def load_over(n):
                sp.dma_start(Xo[:, :], xd[ds(n * P + OV0, P), :]).then_inc(s["oX_in"], 16)

            def store_over(n):
                sp.wait_ge(s["oy_ok"], n + 1)
                sp.dma_start(yd[ds(n * P + OV0, P), :], yo[:, :]).then_inc(s["o_out"], 16)
            load_over(0)
            sp.wait_ge(s["slot_ok"], 1)
            nb = sp.value_load(nbi[0:1, 0:1], min_val=2, max_val=OVB)
            with sp.Fori(1, nb) as n:
                sp.wait_ge(s["oT_ps"], n)
                load_over(n)
                store_over(n - 1)
            sp.wait_ge(s["oy_ok"], nb)
            sp.dma_start(yd[ds(nb * P + (OV0 - P), P), :], yo[:, :]).then_inc(s["o_out"], 16)
            xo = c.x[:, :].rearrange("p (q b n) -> p q b n", b=B, n=D)
            for g in range(4):
                sp.wait_ge(s["sum_ok"], g + 1)
                for b in range(B):
                    sp.dma_start(d["out"][b, 2 * g * P:(2 * g + 2) * P, :].rearrange("(q p) n -> p q n", p=P),
                                 xo[:, 2 * g:2 * g + 2, b, :]).then_inc(s["out_done"], 16)
            sp.wait_ge(s["out_done"], 16 * 8)

        @block.gpsimd
        def _(pool):
            ng = nc.gpsimd

            pool.wait_ge(s["slot_ok"], 1)
            for i in range(NT):
                ng.indirect_dma_start(out=xd, out_offset=bass.IndirectOffsetOnAxis(ap=slot[:, i:i + 1], axis=0),
                                      in_=c.lnk[:, i * D:(i + 1) * D], in_offset=None).then_inc(s["scat"], 16)
            nb = pool.value_load(nbi[0:1, 0:1], min_val=2, max_val=OVB)
            for b in range(2):
                pool.wait_ge(y_out[b], 16 * 3 * E3 // 2)
            pool.wait_ge(s["o_out"], nb * 16)
            ng.tensor_tensor(pgap[:, :], rb[:, 0:1], rb[:, 0:1], ALU.add)
            for i in range(NT):
                ng.indirect_dma_start(out=c.lnk[:, i * D:(i + 1) * D], out_offset=None, in_=yd,
                                      in_offset=bass.IndirectOffsetOnAxis(ap=slot[:, i:i + 1], axis=0)
                                      ).then_inc(g_in[i // 4], 16)

        @block.vector
        def _(dve):
            nv = nc.vector
            chain = Chain(dve, s["chain"])
            dve_ln_all(c, dve, s, chain, c.lnk)
            dve.wait_ge(s["w_in"], 16 * 6)
            nv.tensor_copy(upper[:, :], upf[:, :])
            nv.tensor_copy(onesb[:, :], c.ones[:, :])
            l, oh = g8(c.lg), g8(c.gates)
            dve_logits(c, dve, s)
            dve.wait_ge(s["logits_ps"], 1)
            chain(nv.tensor_tensor(l, g8(c.ps[5][:, 0:NT * 8]), rb[:, :].unsqueeze(1).to_broadcast([P, NT, 8]), ALU.add))
            top1(c, chain, l, 8, oh, g8(c.lgt), c.m1[:, :])
            nv.tensor_copy(ohb[:, :], c.gates[:, :]).then_inc(s["oh_ok"], 1)
            dve.wait_ge(s["pre_ps"], 1)
            tot = g8(c.lg2)
            nv.tensor_copy(c.lg2[:, :], c.ps[1][:, 0:NT * 8])
            chain(nv.memset(base[:, 0:8], 0.0))
            for prev, i in zip(order, order[1:]):
                chain(nv.tensor_tensor(base[:, i * 8:(i + 1) * 8], base[:, prev * 8:(prev + 1) * 8], tot[:, prev, :],
                                       ALU.add))
            chain(nv.tensor_tensor(rank8[:, :], c.ps[0][:, 0:NT * 8], base[:, :], ALU.add))
            chain(nv.tensor_tensor(rank8[:, :], rank8[:, :], c.gates[:, :], ALU.mult))
            chain(nv.reduce_sum(rank[:, :], g8(rank8), AX))
            nv.tensor_scalar(valid[:, :], rank[:, :], float(CAP), None, ALU.is_lt)
            chain(nv.tensor_scalar(over[:, :], rank[:, :], float(CAP), None, ALU.is_ge))
            nv.tensor_copy(overb[:, :], over[:, :]).then_inc(s["over_ok"], 1)
            chain(nv.tensor_scalar(slotf[:, :], c.first[:, :], -float(CAP), float(E3 * CAP), ALU.mult, ALU.add))
            chain(nv.tensor_tensor(slotf[:, :], slotf[:, :], rank[:, :], ALU.add))
            chain(nv.tensor_tensor(slotf[:, :], slotf[:, :], valid[:, :], ALU.mult))
            dve.wait_ge(s["opre_ps"], 1)
            nv.tensor_copy(c.m2[:, :], c.ps[3][:, 0:NT])
            chain(nv.memset(obase[:, 0:1], float(OV0)))
            for prev, i in zip(order, order[1:]):
                chain(nv.tensor_tensor(obase[:, i:i + 1], obase[:, prev:prev + 1], c.m2[:, prev:prev + 1], ALU.add))
            chain(nv.tensor_tensor(nbf[:, 0:1], obase[0:1, NT - 1:NT], c.m2[0:1, NT - 1:NT], ALU.add))
            chain(nv.tensor_scalar(steps_[:, :], steps_[:, :], nbf[:, 0:1], None, ALU.is_lt))
            chain(nv.reduce_sum(nbf[:, 1:2], steps_[:, :], AX))
            nv.tensor_scalar(nbi[:, :], nbf[:, 1:2], 2.0, None, ALU.max)
            chain(nv.tensor_tensor(obase[:, :], c.ps[2][:, 0:NT], obase[:, :], ALU.add))
            chain(nv.tensor_tensor(obase[:, :], obase[:, :], over[:, :], ALU.mult))
            nv.tensor_tensor(slot[:, :], slotf[:, :], obase[:, :], ALU.add).then_inc(s["slot_ok"], 1)

            def x_copy(e, b):
                dve.wait_ge(s["xT_ps"], e + 1)
                for k in range(KC):
                    last = nv.tensor_copy(xT[b][:, k, :], c.ps[k][:, 0:CAP])
                last.then_inc(s["xT_ok"], 1)

            def y_bias(e, b):
                wait(dve, y_out[b], count16(e, b, 3) - 48)
                for r, (r0, n) in enumerate(XR):
                    dve.wait_ge(s["y_ps"], e * 3 + (r + 1))
                    nv.tensor_tensor(yt[b][0:n, r, :], c.ps[6 + (3 * b + r) % 2][0:n, 0:D], b2[0:n, ds(e * D, D)],
                                     ALU.add).then_inc(s["y_ok"], 1)
            x_copy(0, 0)

            def step(e, b):
                if not is_static(e) or e + 1 < E3:
                    x_copy(e + 1, 1 - b)
                y_bias(e, b)
            pipeline(dve, step, 0, 2, E3 - 2, E3)

            def over_block(n):
                dve.wait_ge(s["oT_ps"], n + 1)
                nv.tensor_copy(xTo[:, :], c.ps[0][:, 0:D]).then_inc(s["oT_ok"], 1)
                dve.wait_ge(s["oy_ps"], n + 1)
                wait(dve, s["o_out"], n * 16)
                nv.tensor_tensor(yo[:, :], c.ps[6][:, 0:D], ob2[:, :], ALU.add).then_inc(s["oy_ok"], 1)
            over_block(0)
            nb = dve.value_load(nbi[0:1, 0:1], min_val=2, max_val=OVB)
            with dve.Fori(1, nb) as n:
                over_block(n)
            for g in range(4):
                dve.wait_ge(g_in[g], 64)
                sl = slice(4 * g * D, (4 * g + 4) * D)
                nv.tensor_tensor(c.x[:, sl], c.x[:, sl], c.lnk[:, sl], ALU.add).then_inc(s["sum_ok"], 1)

        @block.scalar
        def _(act):
            na = nc.scalar
            act_ln_all(c, act, s)

            def step(e, b):
                wait(act, s["y_ps"], e * 3 - 3)
                for m in range(MH):
                    act.wait_ge(s["h_ps"], e * 8 + (m + 1))
                    na.activation(hT[b][:, m, :], c.ps[2 + m % 4][:, 0:CAP], ACT.Relu,
                                  bias=b1[:, ds(e * MH + m, 1)]).then_inc(s["h_ok"], 1)
            pipeline(act, step, 0, 2, E3, E3)

            def over_block(n):
                for u in range(2):
                    act.wait_ge(s["oh_ps"], n * 2 + (u + 1))
                    for m in range(4):
                        last = na.activation(hTo[:, 4 * u + m, :], c.ps[2 + u][:, m * P:(m + 1) * P], ACT.Relu,
                                             bias=ob1[:, 4 * u + m:4 * u + m + 1])
                    last.then_inc(s["ohid_ok"], 1)
            over_block(0)
            act.wait_ge(s["slot_ok"], 1)
            nb = act.value_load(nbi[0:1, 0:1], min_val=2, max_val=OVB)
            with act.Fori(1, nb) as n:
                over_block(n)

        @block.tensor
        def _(pe):
            nt = nc.tensor
            pe_ln_all(c, pe, s, rw, 16 * 2, c.lnk)
            pe.wait_ge(s["w_in"], 16 * 6)
            pe.wait_ge(s["oh_ok"], 1)
            nt.matmul(c.ps[0][:, 0:NT * 8], upper[:, :], ohb[:, :], start=True, stop=True)
            nt.matmul(c.ps[1][:, 0:NT * 8], onesb[:, :], ohb[:, :], start=True, stop=True).then_inc(s["pre_ps"], 1)
            pe.wait_ge(s["over_ok"], 1)
            nt.matmul(c.ps[2][:, 0:NT], upper[:, :], overb[:, :], start=True, stop=True)
            nt.matmul(c.ps[3][:, 0:NT], onesb[:, :], overb[:, :], start=True, stop=True).then_inc(s["opre_ps"], 1)
            pe.wait_ge(s["slot_ok"], 1)

            def x_transpose(e, b):
                pe.wait_ge(x_in[b], count16(e, b, 2))
                wait(pe, s["xT_ok"], e)
                for k in range(KC):
                    for r, (r0, n) in enumerate(XR):
                        last = nt.transpose(c.ps[k][:, r0:r0 + n], X[b][0:n, r, k * P:(k + 1) * P],
                                            c.ident[0:n, 0:n])
                last.then_inc(s["xT_ps"], 1)

            def hidden(e, b):
                pe.wait_ge(w1_in[b], count16(e, b, 2))
                pe.wait_ge(s["xT_ok"], e + 1)
                for m in range(MH):
                    wait(pe, s["h_ok"], e * 8 + (m - 3))
                    for k in range(KC):
                        last = nt.matmul(c.ps[2 + m % 4][:, 0:CAP], w1[b][:, k, m * P:(m + 1) * P], xT[b][:, k, :],
                                         start=(k == 0), stop=(k == KC - 1))
                    last.then_inc(s["h_ps"], 1)

            def outputs(e, b):
                pe.wait_ge(w2_in[b], count16(e, b, 1))
                pe.wait_ge(s["h_ok"], e * 8 + 8)
                for r, (r0, n) in enumerate(XR):
                    wait(pe, s["y_ok"], e * 3 + (r - 1))
                    for m in range(MH):
                        last = nt.matmul(c.ps[6 + (3 * b + r) % 2][0:n, 0:D], hT[b][:, m, r0:r0 + n], w2[b][:, m, :],
                                         start=(m == 0), stop=(m == MH - 1))
                    last.then_inc(s["y_ps"], 1)
            x_transpose(0, 0)

            def step(e, b):
                hidden(e, b)
                if not is_static(e) or e + 1 < E3:
                    x_transpose(e + 1, 1 - b)
                outputs(e, b)
            pipeline(pe, step, 0, 2, E3 - 2, E3)
            pe.wait_ge(s["ow_in"], 48)

            def over_block(n):
                pe.wait_ge(s["oX_in"], n * 16 + 16)
                for k in range(KC):
                    last = nt.transpose(c.ps[0][:, k * P:(k + 1) * P], Xo[:, k * P:(k + 1) * P], c.ident[:, :])
                last.then_inc(s["oT_ps"], 1)
                pe.wait_ge(s["oT_ok"], n + 1)
                for u in range(2):
                    for m in range(4):
                        for k in range(KC):
                            last = nt.matmul(c.ps[2 + u][:, m * P:(m + 1) * P],
                                             ow1[:, k, (4 * u + m) * P:(4 * u + m + 1) * P], xTo[:, k * P:(k + 1) * P],
                                             start=(k == 0), stop=(k == KC - 1))
                    last.then_inc(s["oh_ps"], 1)
                pe.wait_ge(s["ohid_ok"], n * 2 + 2)
                wait(pe, s["oy_ok"], n)
                for m in range(MH):
                    last = nt.matmul(c.ps[6][:, 0:D], hTo[:, m, :], ow2[:, m, :], start=(m == 0), stop=(m == MH - 1))
                last.then_inc(s["oy_ps"], 1)
            pe.wait_ge(s["y_ok"], 3 * E3)
            over_block(0)
            nb = pe.value_load(nbi[0:1, 0:1], min_val=2, max_val=OVB)
            with pe.Fori(1, nb) as n:
                over_block(n)


def store_stage(c, d):
    nc = c.nc
    out_done = sem(c, "out_done")
    xv = c.x[:, :].rearrange("p (q b n) -> p q b n", b=B, n=D)
    with nc.Block() as block:
        @block.sync
        def _(sp):
            for b in range(B):
                sp.dma_start(d["out"][b].rearrange("(q p) n -> p q n", p=P), xv[:, :, b, :]).then_inc(out_done, 16)
            sp.wait_ge(out_done, 16 * B)


def build(nc, d):
    c = Core()
    with ExitStack() as ctx:
        c.nc, c.ctx, c.stage_ctx = nc, ctx, ctx
        c.stages = STAGES
        c.x = sb(c, "x_tiles", [P, NT * D])
        c.mean = sb(c, "mean", [P, NT])
        c.ve = sb(c, "var_eps", [P, NT])
        c.std = sb(c, "std", [P, NT])
        c.rstd = sb(c, "rstd", [P, NT])
        c.bst = sb(c, "bst", [P, NT * 6])
        c.ident = sb(c, "ident", [P, P])
        c.identb = sb(c, "identb", [P, P], BF16)
        c.tiledI = sb(c, "tiledI", [SK, HPB * SK], BF16)
        c.ones = sb(c, "ones", [P, P])
        c.hmask = sb(c, "hmask", [P, 8])
        c.hmask2 = sb(c, "hmask2", [P, 2])
        c.ctxT = sb(c, "ctxT", [P, KC, B * SK])
        c.ctxn = sb(c, "ctxn", [SK, B, D])
        c.Wall = sb(c, "Wall", [P, 4 * KC * D])
        c.W = [c.Wall[:, k * KC * D:(k + 1) * KC * D].rearrange("p (k n) -> p k n", k=KC) for k in range(4)]
        c.w_in, c.mask_in = nc.alloc_semaphore(name="w_in"), nc.alloc_semaphore(name="mask_in")
        c.bo, c.bv = sb(c, "bo", [P, D]), sb(c, "bv", [P, D])
        c.vsel = sb(c, "vsel", [P, NBLK * VHEADS])
        c.maskT = sb(c, "maskT", [SK, B * S], BF16)
        c.bq, c.bk = sb(c, "bq", [P, KC]), sb(c, "bk", [P, KC])
        pair = lambda name, shape: [sb(c, f"{name}{b}", shape) for b in range(2)]
        c.ln, c.lnT, c.qT = pair("ln", [P, D]), pair("lnT", [P, D]), pair("qT", [P, D])
        c.o, c.oT, c.pT = pair("o", [P, D]), pair("oT", [P, D]), pair("pT", [P, H * P])
        c.prob_pair = [sb(c, f"prob{b}", [P, MH * CAP]) for b in range(2)]
        c.prob = [t[:, 0:H * SK] for t in c.prob_pair]
        rows = (E3 * CAP + OVB * P, D)
        c.xd = nc.dram_tensor("expert_rows", rows, F32, kind="Internal").ap()
        c.yd = nc.dram_tensor("expert_outputs", rows, F32, kind="Internal").ap()
        c.mx = sb(c, "mx", [P, H])
        c.den = sb(c, "den", [P, H])
        c.rden = sb(c, "rden", [P, H])
        c.lnT_all = sb(c, "lnT_all", [P, KC, NT * P])
        c.lnk = sb(c, "lnk", [P, NT * D])
        c.tiled_f = c.lnk[0:SK, 0:HPB * SK]
        c.mraw = c.lnk[0:SK, HPB * SK:HPB * SK + B * S].bitcast(I32)
        c.gates, c.lg, c.lg2, c.lgt, c.choice, c.down = (
            sb(c, n, [P, NT * 8]) for n in ("gates", "lg", "lg2", "lgt", "choice", "down"))
        c.down4 = sb(c, "down4", [P, NT * 4])
        c.m1, c.m2, c.first = (sb(c, n, [P, NT]) for n in ("m1", "m2", "first"))
        c.acc = [sb(c, f"acc{o}", [P, D]) for o in range(2)]
        c.gap = sb(c, "gap", [P, 2])
        c.psall_t = ctx.enter_context(nc.psum_tensor("psum", [P, 8 * 512], F32))
        c.psall = c.psall_t[:, :]
        c.ps = [c.psall[:, k * 512:(k + 1) * 512] for k in range(8)]
        stages = [
            lambda: attn16(c, 0, True, HD ** -0.5, N_ATTN0),
            lambda: moe0(c, d),
            lambda: attn16(c, 1, False, HD ** -0.5, N_ATTN0 + N_ATTN1),
            lambda: int8_linear(c, d),
            lambda: attn1(c, d),
            lambda: moe2(c, d),
            lambda: attn_gqa(c, d),
            lambda: moe3(c, d),
        ]
        run_stage(c, lambda: load_stage(c, d))
        for n, stage in enumerate(stages[:c.stages]):
            run_stage(c, stage, n == 7)
        if c.stages < 8:
            run_stage(c, lambda: store_stage(c, d), True)


def host_arrays(inputs):
    a = {k: np.ascontiguousarray(v) for k, v in inputs.items()}
    out = {"x": a["x"], "ctx_1024": a["ctx_1024"]}
    out["ctxT"] = np.ascontiguousarray(a["ctx_1024"].transpose(2, 0, 1).reshape(D, B * SK))
    out["maskT0"] = np.ascontiguousarray(a["mask_Bx1xSxS2_bk1"][:, 0].transpose(2, 0, 1)).view(np.int32)
    out["maskT1"] = np.ascontiguousarray(a["mask_Bx1xSxS2_ik1"][:, 0].transpose(2, 0, 1))
    for k in ("Wq", "Wk", "Wv", "Wo", "bq", "bk", "bv", "bo"):
        out["L0_xattn_" + k] = a["L0_xattn_" + k]
    for k in ("bq", "bk"):
        out["L0_xattn_" + k] = np.ascontiguousarray(a["L0_xattn_" + k].reshape(KC, P).T)
    rows_head = (np.arange(NBLK)[:, None] * P + np.arange(P)[None]) // SK
    out["c_vsel"] = np.ascontiguousarray(
        (rows_head[:, :, None] == np.array(VHEAD0)[:, None, None] + np.arange(VHEADS)).astype(np.float32)
        .transpose(1, 0, 2).reshape(P, NBLK * VHEADS))
    out["c_ident"] = np.eye(P, dtype=np.float32)
    out["c_tiled"] = np.tile(np.eye(SK, dtype=np.float32), (1, HPB))
    out["c_hmask"] = np.repeat(np.eye(8, dtype=np.float32), HD, axis=0)
    out["L0_ffn_gate_wT"] = np.ascontiguousarray(a["L0_ffn_gate_w"].T)
    for k in ("gate_b", "expert_w", "expert_b"):
        out["L0_ffn_" + k] = a["L0_ffn_" + k]
    out["c_down"] = np.tile(np.arange(8, 0, -1, dtype=np.float32), NT)
    out["c_down4"] = np.tile(np.arange(4, 0, -1, dtype=np.float32), NT)
    for k in ("wq", "wk", "wv", "wo", "bo"):
        out["L1_xattn_" + k] = a["L1_xattn_" + k]
    out["L1_ffn_rhsT"] = np.ascontiguousarray(a["L1_ffn_rhs"].T)
    out["maskT2"] = np.ascontiguousarray(a["mask_BxSxS2_ik1"].transpose(2, 0, 1).reshape(SK, B * S))
    out["L2_xattn_gamma"], out["L2_xattn_beta"] = a["L2_xattn_gamma"], a["L2_xattn_beta"]
    out["L2_ffn_gate_weightT"] = np.ascontiguousarray(a["L2_ffn_gate_weight"].T)
    out["L2_ffn_e_score_correction_bias"] = a["L2_ffn_e_score_correction_bias"]
    for k in ("gate_proj", "up_proj"):
        out["L2_ffn_" + k + "T"] = np.ascontiguousarray(a["L2_ffn_" + k].transpose(2, 0, 1).reshape(D, -1))
    out["L2_ffn_down_projT"] = np.ascontiguousarray(a["L2_ffn_down_proj"].transpose(2, 0, 1).reshape(P, -1))
    for k in ("Wq", "Wk", "Wv", "Wo"):
        out["L3_xattn_" + k] = a["L3_xattn_" + k]
    rows = np.concatenate([a["mask_BxS2_bf1"].reshape(-1), np.zeros(160 - B * SK, a["mask_BxS2_bf1"].dtype)])
    out["mask3"] = rows.reshape(1, 160).view(np.int32)
    rb = a["L3_xattn_rel_pos_bias"]
    away = np.minimum(np.abs(np.arange(S)[:, None] - np.arange(SK)[None]), rb.shape[1] - 1)
    out["rel_bias"] = np.ascontiguousarray(rb[:, away].transpose(1, 0, 2).reshape(S, HB * SK))
    inv = np.float32(1) / np.float32(10000) ** (np.arange(0, DH, 2, dtype=np.float32) / np.float32(DH))
    angle = np.repeat(np.outer(np.arange(S, dtype=np.float32), inv.astype(np.float32)), 2, axis=-1).astype(np.float64)
    out["c_cos"] = np.cos(angle).astype(np.float32)
    sin = np.sin(angle).astype(np.float32)
    out["c_sin"] = np.concatenate([-sin[:, :DH // 2], sin[:, DH // 2:]], axis=1)
    for k in ("router_w", "router_b", "b2", "ob2", "ow1", "ow2"):
        out["L3_ffn_" + k] = a["L3_ffn_" + k]
    out["L3_ffn_w1"] = a["L3_ffn_w1"].reshape(E3 * D, HF)
    out["L3_ffn_w2"] = a["L3_ffn_w2"].reshape(E3 * HF, D)
    out["L3_ffn_b1T"] = np.ascontiguousarray(a["L3_ffn_b1"].reshape(E3 * MH, P).T)
    out["L3_ffn_ob1T"] = np.ascontiguousarray(a["L3_ffn_ob1"].reshape(MH, P).T)
    out["c_upper"] = np.triu(np.ones((P, P), np.float32), 1)
    out["c_steps"] = (E3 * CAP + P * np.arange(OVB, dtype=np.float32)).astype(np.float32)[None]
    out["c_hmask2"] = np.repeat(np.eye(2, dtype=np.float32), P // 2, axis=0)
    return out


def kernel(**inputs):
    import concourse.bacc as bacc
    from concourse.bass_utils import run_bass_kernel_spmd as run

    nc = bacc.Bacc("TRN2", target_bir_lowering=False, num_devices=1)
    arrays = host_arrays(inputs)
    d = {n: nc.dram_tensor("in_" + n, a.shape, mybir.dt.from_np(a.dtype), kind="ExternalInput").ap()
         for n, a in arrays.items()}
    d["out"] = nc.dram_tensor("out_x", (B, S, D), F32, kind="ExternalOutput").ap()
    build(nc, d)
    r = run(nc, [{"in_" + n: a for n, a in arrays.items()}], core_ids=[0])
    return r.results[0]["out_x"]
```
